# Optimizing a Trainium2 kernel written in Bass

```python
import numpy as np
import jax
import jax.numpy as jnp

def _softmax(x, axis=-1):
    return jax.nn.softmax(x, axis=axis)

def _gelu(x):
    return jax.nn.gelu(x, approximate=True)

def _silu(x):
    return jax.nn.silu(x)

def _sigmoid(x):
    return jax.nn.sigmoid(x)

def _layernorm(x, axis=-1, eps=1e-05):
    m = jnp.mean(x, axis=axis, keepdims=True)
    v = jnp.var(x, axis=axis, keepdims=True)
    return (x - m) / jnp.sqrt(v + eps)

def _scatter_add(tgt, idx, src, axis=0):
    return tgt.at[idx].add(src)

def _segment_sum(src, seg, n):
    return jax.ops.segment_sum(src, seg, n)
kernel_name = 'mk_flamingo_gated_d2_seqx_r4_5016f5'

def setup_inputs(seed: int=0):
    np.random.seed(seed)
    _w = jnp.asarray

    def _rec_inputs():
        import jax
        import jax.numpy as jnp
        _rk = jax.random.key(seed)
        x = 7.22e-05 + 1 * jax.random.normal(jax.random.fold_in(_rk, 1), (8, 256, 512), jnp.float32)
        _lenS = 256 - jax.random.randint(jax.random.fold_in(_rk, 7), (8,), 0, max(1, 256 // 4) + 1, jnp.int32)
        _lenS2 = 256 - jax.random.randint(jax.random.fold_in(_rk, 8), (8,), 0, max(1, 256 // 4) + 1, jnp.int32)
        _ctx_2048P = jax.random.normal(jax.random.fold_in(_rk, 11), (8, 16, 512), jnp.float32)
        _ctx_2048c = jax.random.dirichlet(jax.random.fold_in(_rk, 511), 0.3 * jnp.ones((16,), jnp.float32), (8, 256))
        _ctx_2048t = jnp.einsum('bsk,bkd->bsd', _ctx_2048c, _ctx_2048P)
        _ctx_2048t = _ctx_2048t * jax.lax.rsqrt(jnp.mean(jnp.square(_ctx_2048t)) + 1e-12) * 0.953939
        ctx_2048 = 4.13588e-05 + 0.999923 * (_ctx_2048t + 0.3 * jax.random.normal(jax.random.fold_in(_rk, 611), (8, 256, 512), jnp.float32))
        _g = jax.random.normal(jax.random.fold_in(_rk, 9001), (2, 2), jnp.float32)
        _g = jnp.sign(_g) * jnp.maximum(jnp.abs(_g), 1.0) + (_g == 0) * 1.0
        g_xattn = _g[0]
        g_ffn = _g[1]
        return (x, ctx_2048, g_xattn, g_ffn)
    x, ctx_2048, g_xattn, g_ffn = _rec_inputs()

    def _L0_xattn_setup():
        import jax, jax.numpy as jnp
        import numpy as np
        B, S, DIM, HD = (4, 256, 512, 128)
        H = DIM // HD
        GN_EPS = 0.001

        def _decay_masks(n_heads, seq_len):
            gam = 1.0 - 2.0 ** (-5.0 - jnp.arange(n_heads, dtype=jnp.float32))
            idx = jnp.arange(seq_len, dtype=jnp.float32)
            expo = idx[None, :] - idx[:, None]
            D = jnp.where(expo[None, :, :] <= 0, gam[:, None, None] ** expo[None, :, :], 0.0)
            return D / jnp.sqrt(D.sum(axis=-1))[:, None, :]
        key = jax.random.key(seed)
        ks = jax.random.split(key, 8)
        x = jax.random.normal(ks[0], (B, S, DIM), dtype=jnp.float32)
        k = jax.random.normal(ks[1], (B, S, DIM), dtype=jnp.float32)
        v = jax.random.normal(ks[2], (B, S, DIM), dtype=jnp.float32)
        Wh = jax.random.normal(ks[3], (H, HD, HD), dtype=jnp.float32) / np.sqrt(HD)
        wg_w = jax.random.normal(ks[4], (DIM, DIM), dtype=jnp.float32) / np.sqrt(DIM)
        wo_w = jax.random.normal(ks[5], (DIM, DIM), dtype=jnp.float32) / np.sqrt(DIM)
        gn_gamma = jnp.ones((DIM,), dtype=jnp.float32)
        gn_beta = jnp.zeros((DIM,), dtype=jnp.float32)
        return {'x': x, 'k': k, 'v': v, 'Wh': Wh, 'wg_w': wg_w, 'wo_w': wo_w, 'gn_gamma': gn_gamma, 'gn_beta': gn_beta}
    _L0_xattn_all = _L0_xattn_setup()
    _L0_xattn_in = {k: v for k, v in _L0_xattn_all.items() if k in ('Wh', 'wg_w', 'wo_w', 'gn_gamma', 'gn_beta')}
    del _L0_xattn_all

    def _L0_ffn_setup():
        import jax, jax.numpy as jnp
        import numpy as np
        DIM = 512
        N_EXPERTS = 8
        TOP_K = 2
        key = jax.random.key(seed)
        ks = jax.random.split(key, 5)
        x = jax.random.normal(ks[0], (4, 1024, DIM), dtype=jnp.float32)
        W_up = jax.random.normal(ks[1], (DIM, DIM), dtype=jnp.float32) * (1.0 / np.sqrt(DIM))
        W_down = jax.random.normal(ks[2], (DIM, DIM), dtype=jnp.float32) * (1.0 / np.sqrt(DIM))
        W_gate = jax.random.normal(ks[3], (N_EXPERTS, DIM), dtype=jnp.float32) * (1.0 / np.sqrt(DIM))
        W_expert = jax.random.normal(ks[4], (DIM, DIM), dtype=jnp.float32) * (1.0 / np.sqrt(DIM))
        return {'x': x, 'W_up': W_up, 'W_down': W_down, 'W_gate': W_gate, 'W_expert': W_expert}
    _L0_ffn_all = _L0_ffn_setup()
    _L0_ffn_in = {k: v for k, v in _L0_ffn_all.items() if k in ('W_up', 'W_down', 'W_gate', 'W_expert')}
    del _L0_ffn_all

    def _L1_xattn_setup():
        import jax, jax.numpy as jnp
        import numpy as np
        N_HEAD = 8
        key = jax.random.key(seed)
        k1, k2, k3 = jax.random.split(key, 3)
        b, d, m = (4, 256, 512)
        c, n = (256, 512)
        q = jax.random.normal(k1, (b, d, m), dtype=jnp.float32)
        k = jax.random.normal(k2, (d // d * b, d, n), dtype=jnp.float32).reshape(b, d, n)
        v = jax.random.normal(k3, (b, c, n), dtype=jnp.float32)
        return {'q': q, 'k': k, 'v': v}
    _L1_xattn_all = _L1_xattn_setup()
    _L1_xattn_in = {k: v for k, v in _L1_xattn_all.items() if k in ()}
    del _L1_xattn_all

    def _L1_ffn_setup():
        import jax, jax.numpy as jnp
        import numpy as np
        TOPK = 6
        CAP = 256
        ROUTE_SCALE = 1.0
        key = jax.random.key(seed)
        k = jax.random.split(key, 6)
        B, T, C = (2, 512, 512)
        E, H, HS = (64, 64, 128)
        std = 0.01
        return {'x': jax.random.normal(k[0], (B, T, C), jnp.float32), 'w_gate': jax.random.normal(k[1], (C, E), jnp.float32) * std, 'w_shared_up': jax.random.normal(k[2], (C, 2 * HS), jnp.float32) * std, 'w_shared_down': jax.random.normal(k[3], (HS, C), jnp.float32) * std, 'w_up': jax.random.normal(k[4], (E, C, 2 * H), jnp.float32) * std, 'w_down': jax.random.normal(k[5], (E, H, C), jnp.float32) * std}
    _L1_ffn_all = _L1_ffn_setup()
    _L1_ffn_in = {k: v for k, v in _L1_ffn_all.items() if k in ('w_gate', 'w_shared_up', 'w_shared_down', 'w_up', 'w_down')}
    del _L1_ffn_all
    return {'x': x, 'ctx_2048': ctx_2048, 'g_xattn': g_xattn, 'g_ffn': g_ffn, 'L0_xattn_Wh': _L0_xattn_in['Wh'], 'L0_xattn_wg_w': _L0_xattn_in['wg_w'], 'L0_xattn_wo_w': _L0_xattn_in['wo_w'], 'L0_xattn_gn_gamma': _L0_xattn_in['gn_gamma'], 'L0_xattn_gn_beta': _L0_xattn_in['gn_beta'], 'L0_ffn_W_up': _L0_ffn_in['W_up'], 'L0_ffn_W_down': _L0_ffn_in['W_down'], 'L0_ffn_W_gate': _L0_ffn_in['W_gate'], 'L0_ffn_W_expert': _L0_ffn_in['W_expert'], 'L1_ffn_w_gate': _L1_ffn_in['w_gate'], 'L1_ffn_w_shared_up': _L1_ffn_in['w_shared_up'], 'L1_ffn_w_shared_down': _L1_ffn_in['w_shared_down'], 'L1_ffn_w_up': _L1_ffn_in['w_up'], 'L1_ffn_w_down': _L1_ffn_in['w_down']}

def reference(x, ctx_2048, g_xattn, g_ffn, L0_xattn_Wh, L0_xattn_wg_w, L0_xattn_wo_w, L0_xattn_gn_gamma, L0_xattn_gn_beta, L0_ffn_W_up, L0_ffn_W_down, L0_ffn_W_gate, L0_ffn_W_expert, L1_ffn_w_gate, L1_ffn_w_shared_up, L1_ffn_w_shared_down, L1_ffn_w_up, L1_ffn_w_down):
    import jax
    import jax.numpy as jnp

    def _L0_xattn_ref(x, k, v, Wh, wg_w, wo_w, gn_gamma, gn_beta):
        import jax, jax.numpy as jnp
        import numpy as np
        B, S, DIM, HD = (4, 256, 512, 128)
        H = DIM // HD
        GN_EPS = 0.001

        def _decay_masks(n_heads, seq_len):
            gam = 1.0 - 2.0 ** (-5.0 - jnp.arange(n_heads, dtype=jnp.float32))
            idx = jnp.arange(seq_len, dtype=jnp.float32)
            expo = idx[None, :] - idx[:, None]
            D = jnp.where(expo[None, :, :] <= 0, gam[:, None, None] ** expo[None, :, :], 0.0)
            return D / jnp.sqrt(D.sum(axis=-1))[:, None, :]
        b, s, dim = x.shape
        h, hd, _ = Wh.shape
        xh = x.reshape(b, s, h, hd)
        kh = k.reshape(b, s, h, hd)
        vh = v.reshape(b, s, h, hd)
        Q = jnp.einsum('bshd,hde->bshe', xh, Wh)
        K = jnp.einsum('bshd,hde->bshe', kh, Wh)
        V = jnp.einsum('bshd,hde->bshe', vh, Wh)
        scores = jnp.einsum('bshe,bthe->bhst', Q, K) / jnp.sqrt(jnp.float32(hd))
        Dn = _decay_masks(h, s)
        masked = scores * Dn[None, :, :, :]
        A = jnp.maximum(jnp.abs(masked.sum(axis=0)), 1.0)
        O = jnp.einsum('hst,bthe->bshe', A, V).reshape(b, s, dim)
        mu = O.mean(axis=-1, keepdims=True)
        var = O.var(axis=-1, keepdims=True)
        Y = (O - mu) / jnp.sqrt(var + GN_EPS) * gn_gamma + gn_beta
        W = jax.nn.relu(x @ wg_w)
        return W * Y @ wo_w

    def _L0_ffn_ref(x, W_up, W_down, W_gate, W_expert):
        import jax, jax.numpy as jnp
        import numpy as np
        DIM = 512
        N_EXPERTS = 8
        TOP_K = 2
        logits = jnp.einsum('bsd,ed->bse', x, W_gate)
        routing_weights, selected_experts = jax.lax.top_k(logits, TOP_K)
        shared_out = jnp.einsum('bsd,od->bso', jax.nn.relu(jnp.einsum('bsd,od->bso', x, W_up)), W_down)
        rw = jax.nn.softmax(routing_weights, axis=-1)
        expert_out = jnp.einsum('bsd,do->bso', x, W_expert)
        moe_out = jnp.sum(rw, axis=-1, keepdims=True) * expert_out
        return shared_out + moe_out

    def _L1_xattn_ref(q, k, v):
        import jax, jax.numpy as jnp
        import numpy as np
        N_HEAD = 8
        b, d, m = q.shape
        c = v.shape[1]
        h = N_HEAD
        qh = q.reshape(b * h, d // h, m)
        kh = k.reshape(b * h, d // h, -1)
        vh = v.reshape(b * h, c // h, -1)
        scale = 1.0 / jnp.sqrt(jnp.asarray(d // h, dtype=q.dtype))
        qk = jnp.einsum('bdm,bdn->bmn', qh, kh) * scale
        sm = jax.nn.softmax(qk, axis=-1)
        ret = jnp.einsum('bmn,bcn->bcm', sm, vh)
        return ret.reshape(b, c, m)

    def _L1_ffn_ref(x, w_gate, w_shared_up, w_shared_down, w_up, w_down):
        import jax, jax.numpy as jnp
        import numpy as np
        TOPK = 6
        CAP = 256
        ROUTE_SCALE = 1.0
        B, T, C = x.shape
        E = w_gate.shape[1]
        x_flat = x.reshape(-1, C)
        N = x_flat.shape[0]
        su = x_flat @ w_shared_up
        y_s, g_s = jnp.split(su, 2, axis=-1)
        shared = jax.nn.silu(g_s) * y_s @ w_shared_down
        scores = jax.nn.sigmoid(x_flat @ w_gate)
        _, topk_idx = jax.lax.top_k(scores, TOPK)
        w = jnp.take_along_axis(scores, topk_idx, axis=-1)
        w = w / w.sum(-1, keepdims=True) * ROUTE_SCALE
        flat_e = topk_idx.reshape(-1)
        oh = jax.nn.one_hot(flat_e, E, dtype=jnp.int32)
        pos = jnp.take_along_axis(jnp.cumsum(oh, axis=0), flat_e[:, None], axis=1)[:, 0] - 1
        valid = pos < CAP
        pos_c = jnp.where(valid, pos, CAP - 1)
        token_ids = jnp.repeat(jnp.arange(N), TOPK)
        x_disp = jnp.zeros((E, CAP, C), x.dtype).at[flat_e, pos].set(x_flat[token_ids], mode='drop')
        up = jnp.einsum('ecd,edh->ech', x_disp, w_up)
        g_r, v_r = jnp.split(up, 2, axis=-1)
        h_r = jax.nn.silu(g_r) * v_r
        out_r = jnp.einsum('ech,ehd->ecd', h_r, w_down)
        y_ts = out_r[flat_e, pos_c]
        y_ts = jnp.where(valid[:, None], y_ts, 0.0)
        routed = (y_ts.reshape(N, TOPK, C) * w[:, :, None]).sum(axis=1)
        return (shared + routed).reshape(B, T, C)
    x = x + jnp.tanh(g_xattn[0]) * _L0_xattn_ref(_layernorm(x, axis=-1), ctx_2048, ctx_2048, L0_xattn_Wh, L0_xattn_wg_w, L0_xattn_wo_w, L0_xattn_gn_gamma, L0_xattn_gn_beta)
    x = x + jnp.tanh(g_ffn[0]) * _L0_ffn_ref(_layernorm(x, axis=-1), L0_ffn_W_up, L0_ffn_W_down, L0_ffn_W_gate, L0_ffn_W_expert)
    x = x + jnp.tanh(g_xattn[1]) * _L1_xattn_ref(_layernorm(x, axis=-1), ctx_2048, ctx_2048)
    x = x + jnp.tanh(g_ffn[1]) * _L1_ffn_ref(_layernorm(x, axis=-1), L1_ffn_w_gate, L1_ffn_w_shared_up, L1_ffn_w_shared_down, L1_ffn_w_up, L1_ffn_w_down)
    return x

_drawn_inputs = setup_inputs


def setup_inputs(seed=0):
    import zlib

    import numpy as np

    out = dict(_drawn_inputs(seed))
    spreads = {'g_ffn': (-1.0, 0.6), 'L0_xattn_gn_gamma': (1.0, 0.2), 'L0_xattn_gn_beta': (0.0, 0.1)}
    factors = {'L0_ffn_W_gate': 8.0,
     'L1_ffn_w_gate': 8.0,
     'L1_ffn_w_shared_up': 8.0,
     'L1_ffn_w_shared_down': 8.0,
     'L1_ffn_w_up': 8.0,
     'L1_ffn_w_down': 8.0}
    for name, (base, spread) in spreads.items():
        noise = np.random.default_rng([zlib.crc32(name.encode()), seed]).standard_normal(out[name].shape)
        drawn = base * np.exp(spread * noise) if base else spread * noise
        out[name] = jnp.asarray(drawn.astype(out[name].dtype))
    for name, factor in factors.items():
        out[name] = (out[name] * factor).astype(out[name].dtype)
    return out
```

```python
from contextlib import ExitStack

import numpy as np

import concourse.bass as bass
from concourse import mybir

F32 = mybir.dt.float32
BF16 = mybir.dt.bfloat16
U32 = mybir.dt.uint32
ALU = mybir.AluOpType
ACT = mybir.ActivationFunctionType
AX = mybir.AxisListType

P = 128
NB, S, D = 8, 256, 512
T = S // P
NT = NB * T
KC = D // P
H0 = 4
HS = 8
HD = S // HS
G = 4
NG = HS // G
E0 = 8
E1, HE, TOPK, CAP = 64, 64, 6, 256
HT = CAP // P
SH = 128
GN_EPS, LN_EPS = 1e-3, 1e-5
SCALE1 = float(1.0 / np.sqrt(np.float32(HD)))
SKIP = 1.0e6
PAIRS = E1 // 2


def decay_mask():
    gam = (1.0 - 2.0 ** (-5.0 - np.arange(H0, dtype=np.float32))).astype(np.float32)
    idx = np.arange(S, dtype=np.float32)
    expo = idx[None, :] - idx[:, None]
    d = np.where(expo[None] <= 0, gam[:, None, None] ** np.minimum(expo, 0.0)[None], 0.0).astype(np.float32)
    dn = d / np.sqrt(d.sum(-1))[:, None, :]
    m = (dn / np.sqrt(np.float32(P))).transpose(2, 0, 1)
    return np.ascontiguousarray(m.reshape(T, P, H0, S).transpose(1, 0, 2, 3)).astype(np.float32)


def build(nc, io, out):
    dram = lambda name, shape, dt=F32: nc.dram_tensor(name, shape, dt, kind="Internal").ap()
    xnT_d = dram("xnT_d", (NB, P, KC * S))
    v_d = dram("v_d", (NB, P, T * D))
    kparts_d = dram("kparts_d", (3, NB * S, D), BF16)
    qparts_d = dram("qparts_d", (2, 3, S, D), BF16)
    xn4_d = dram("xn4_d", (NB * S, D))
    acc_d = dram("acc_d", (NT, P, D))
    ids_d = dram("ids_d", (P * P, 1), U32)
    eout_d = dram("eout_d", (E1 * CAP, D))

    with ExitStack() as outer:
        def sem(name):
            return outer.enter_context(nc.semaphore(name))

        def sb(name, shape, dt=F32, ctx=outer):
            return ctx.enter_context(nc.sbuf_tensor(name, shape, dt))

        ident = sb("ident", [P, P])
        ident16 = sb("ident16", [P, P], BF16)
        ones32 = sb("ones32", [P, HD])
        ones16 = sb("ones16", [P, P], BF16)
        before16 = sb("before16", [P, P], BF16)
        mhalf = sb("mhalf", [P, T])
        iota_e = sb("iota_e", [P, E1])
        tok_f = sb("tok_f", [P, 1])
        tg_x = sb("tg_x", [P, 2])
        tg_f = sb("tg_f", [P, 2])
        slots_all = sb("slots_all", [P, NT, TOPK], U32)
        comb_all = sb("comb_all", [P, NT, TOPK])

        with ExitStack() as mid:
            wg = sb("wg", [P, KC, D], ctx=mid)
            wo = sb("wo", [P, KC, D], ctx=mid)
            wupT = sb("wupT", [P, KC, D], ctx=mid)
            wdnT = sb("wdnT", [P, KC, D], ctx=mid)
            wexp = sb("wexp", [P, KC, D], ctx=mid)
            wg0 = sb("wg0", [P, KC, E0], ctx=mid)
            wg1 = sb("wg1", [P, KC, E1], ctx=mid)
            wsu = sb("wsu", [P, KC, 2 * SH], ctx=mid)
            wsd = sb("wsd", [P, D], ctx=mid)
            gamma = sb("gamma", [P, KC], ctx=mid)
            beta = sb("beta", [P, KC], ctx=mid)
            AT = sb("AT", [P, T, H0, S], ctx=mid)
            setup_and_scores(nc, io, outer, mid, locals())
            main_loop(nc, io, locals())
        experts(nc, io, out, locals())


def at(i, u, k=1, per=1):
    return i * (2 * per) + (u * per + k)


def hold(eng, s, n, passed):
    eng.wait_ge(s, n)
    eng.sem_inc(passed, 1)


def setup_and_scores(nc, io, outer, mid, v):
    ident, ident16, ones32, ones16, before16 = (v[n] for n in "ident ident16 ones32 ones16 before16".split())
    mhalf, iota_e, tok_f, tg_x, tg_f, AT = (v[n] for n in "mhalf iota_e tok_f tg_x tg_f AT".split())
    xnT_d, v_d, kparts_d, ids_d = (v[n] for n in "xnT_d v_d kparts_d ids_d".split())
    with ExitStack() as ctx:
        sem = lambda n: outer.enter_context(nc.semaphore(n))
        sb = lambda n, s, d=F32: ctx.enter_context(nc.sbuf_tensor(n, s, d))
        ps = lambda n, s, d=F32: ctx.enter_context(nc.psum_tensor(n, s, d))
        wh = sb("wh", [P, H0, P])
        whT = sb("whT", [P, H0, P])
        gram = sb("gram", [P, H0, P])
        mask = sb("mask", [P, T, H0, S])
        gates = sb("gates", [P, 4])
        zeros = sb("zeros", [P, D], BF16)
        zids = sb("zids", [P, P], U32)
        xin = [sb(f"a_x{u}", [P, T, D]) for u in range(2)]
        cin = [sb(f"a_c{u}", [P, T, D]) for u in range(2)]
        cT = [sb(f"a_cT{u}", [P, KC, S]) for u in range(2)]
        xn = [sb(f"a_xn{u}", [P, T, D]) for u in range(2)]
        xnT = [sb(f"a_xnT{u}", [P, KC, S]) for u in range(2)]
        qT = sb("a_qT", [P, H0, S])
        val = [sb(f"a_val{u}", [P, T, D]) for u in range(2)]
        parts = [sb(f"a_parts{u}", [P, 3, T, D], BF16) for u in range(2)]
        res = sb("a_res", [P, T, D])
        st = sb("a_st", [P, T, 6])
        mv = sb("a_mv", [P, T, 2])
        veps = sb("a_veps", [P, T])
        rstd = sb("a_rstd", [P, T])
        pX = ps("a_pX", [P, KC * S])
        pY = ps("a_pY", [P, KC * S])
        pS = [ps(f"a_pS{k}", [P, 512]) for k in range(3)]

        weights_in, gates_in, wh_in, mask_in = sem("weights_in"), sem("gates_in"), sem("wh_in"), sem("mask_in")
        ids_zeroed, pool_c, zero_set, tg_done = sem("ids_zeroed"), sem("pool_c"), sem("zero_set"), sem("tg_done")
        gram_mm, gram_ok = sem("gram_mm"), sem("gram_ok")
        x_in = [sem(f"ax_in{u}") for u in range(2)]
        c_in = [sem(f"ac_in{u}") for u in range(2)]
        cT_in = [sem(f"acT_in{u}") for u in range(2)]
        x_free, c_free, cT_free = sem("ax_free"), sem("ac_free"), sem("acT_free")
        chain, var_ok, rstd_ok, xn_ok = sem("a_chain"), sem("a_var"), sem("a_rstd_s"), sem("a_xn_s")
        xT_mm, xT_ok, q_mm, q_ok, v_mm, v_ok, s_mm = (sem("a_" + n) for n in "xT_mm xT_ok q_mm q_ok v_mm v_ok s_mm".split())
        k_chain, parts_ok = sem("a_kchain"), sem("a_parts_ok")
        stored = [sem(f"a_stored{u}") for u in range(2)]
        sc_chain, at_done, passed = sem("a_sc_chain"), sem("a_at_done"), sem("a_passed")
        block = ctx.enter_context(nc.Block())

        @block.sync
        def _(sp):
            def load(b, u):
                sp.dma_start(xin[u][:, :, :], io["x"][bass.ds(b, 1), :, :].rearrange("o (t p) d -> p (o t) d", p=P)).then_inc(x_in[u], 16)
                sp.dma_start(cin[u][:, :, :], io["ctx"][bass.ds(b, 1), :, :].rearrange("o (t p) d -> p (o t) d", p=P)).then_inc(c_in[u], 16)
                sp.dma_start(cT[u][:, :, :], io["ctxT"][bass.ds(b, 1), :, :].rearrange("o p (k s) -> (o p) k s", k=KC)).then_inc(cT_in[u], 16)

            def store(i, b, u):
                sp.wait_ge(xT_ok, at(i, u))
                sp.dma_start(xnT_d[bass.ds(b, 1), :, :].rearrange("o p (k s) -> (o p) k s", k=KC), xnT[u][:, :, :]).then_inc(stored[u], 16)
                sp.wait_ge(v_ok, at(i, u))
                sp.dma_start(v_d[bass.ds(b, 1), :, :].rearrange("o p (t d) -> (o p) t d", t=T), val[u][:, :, :]).then_inc(stored[u], 16)
                sp.wait_ge(parts_ok, at(i, u))
                for k in range(3):
                    sp.dma_start(kparts_d[k, bass.ds(b * S, S), :].rearrange("(t p) d -> p t d", p=P), parts[u][:, k, :, :]).then_inc(stored[u], 16)

            sp.dma_start(wh[:, :, :], io["wh"]).then_inc(wh_in, 16)
            sp.dma_start(whT[:, :, :], io["whT"]).then_inc(wh_in, 16)
            for u in range(2):
                load(u, u)
            sp.dma_start(gates[:, :], io["gates"]).then_inc(gates_in, 16)
            sp.dma_start(mask[:, :, :, :], io["mask"]).then_inc(mask_in, 16)
            sp.wait_ge(pool_c, 1)
            sp.dma_start(ids_d.rearrange("(p n) o -> p (n o)", p=P), zids[:, :]).then_inc(ids_zeroed, 16)
            for name in ("wg", "wo", "wupT", "wdnT", "wexp", "wg0", "wg1", "wsu", "wsd", "gamma", "beta"):
                t = v[name]
                ap = t[:, :, :] if len(t.shape) == 3 else t[:, :]
                sp.dma_start(ap, io[name]).then_inc(weights_in, 16)
            with sp.Fori(0, NB // 2 - 1) as i:
                for u in range(2):
                    store(i, i * 2 + u, u)
                    sp.wait_ge(stored[u], i * 80 + 80)
                    sp.wait_ge(x_free, at(i, u))
                    sp.wait_ge(c_free, at(i, u))
                    sp.wait_ge(cT_free, at(i, u))
                    load(i * 2 + (2 + u), u)
            last = NB // 2 - 1
            for u in range(2):
                store(last, 2 * last + u, u)
            for u in range(2):
                sp.wait_ge(stored[u], 5 * 16 * (NB // 2))
            sp.wait_ge(weights_in, 16 * 11)
            sp.wait_ge(ids_zeroed, 16)

        @block.gpsimd
        def _(pool):
            g = nc.gpsimd
            g.memset(zids[:, :], 0).then_inc(pool_c, 1)
            g.memset(ident[:, :], 0.0).then_inc(pool_c, 1)
            g.memset(ident16[:, :], 0.0).then_inc(pool_c, 1)
            g.memset(before16[:, :], 1.0).then_inc(pool_c, 1)
            g.memset(ones32[:, :], 1.0)
            g.memset(ones16[:, :], 1.0)
            g.memset(mhalf[:, :], -0.5).then_inc(pool_c, 1)
            g.iota(iota_e[:, :], pattern=[[1, E1]], base=0, channel_multiplier=0, allow_small_or_imprecise_dtypes=True)
            g.iota(tok_f[:, :], pattern=[[0, 1]], base=0, channel_multiplier=1, allow_small_or_imprecise_dtypes=True)
            pool.wait_ge(pool_c, 5)
            for m in (ident, ident16):
                g.affine_select(out=m[:, :], in_=m[:, :], compare_op=ALU.not_equal, fill=1.0, base=0,
                                pattern=[[-1, P]], channel_multiplier=1).then_inc(pool_c, 1)
            g.affine_select(out=before16[:, :], in_=before16[:, :], compare_op=ALU.is_gt, fill=0.0, base=0,
                            pattern=[[1, P]], channel_multiplier=-1).then_inc(pool_c, 1)
            with pool.Fori(0, NB // 2) as i:
                for u in range(2):
                    pool.wait_ge(var_ok, at(i, u))
                    g.tensor_tensor(rstd[:, :], veps[:, :], mhalf[:, :], ALU.pow).then_inc(rstd_ok, 1)
                    pool.wait_ge(k_chain, at(i, u, 1, 4))
                    g.tensor_tensor(res[:, :, :], cin[u][:, :, :], parts[u][:, 0, :, :], ALU.subtract).then_inc(k_chain, 1)
                    pool.wait_ge(k_chain, at(i, u, 3, 4))
                    g.tensor_tensor(parts[u][:, 2, :, :], res[:, :, :], parts[u][:, 1, :, :], ALU.subtract).then_inc(parts_ok, 1)
                    pool.wait_ge(parts_ok, at(i, u))
                    pool.sem_inc(k_chain, 1)
                    pool.sem_inc(c_free, 1)

        @block.scalar
        def _(act):
            act.preload_act_table(ACT.Exp)
            act.wait_ge(gates_in, 16)
            nc.scalar.activation(tg_x[:, :], gates[:, 0:2], ACT.Tanh).then_inc(tg_done, 1)
            nc.scalar.activation(tg_f[:, :], gates[:, 2:4], ACT.Tanh).then_inc(tg_done, 1)
            act.wait_ge(gram_mm, 1)
            nc.scalar.activation(gram[:, :, :], pX[:, 0:H0 * P].rearrange("p (h e) -> p h e", h=H0), ACT.Copy).then_inc(gram_ok, 1)
            with act.Fori(0, NB // 2) as i:
                for u in range(2):
                    act.wait_ge(xT_mm, at(i, u))
                    nc.scalar.activation(xnT[u][:, :, :], pX[:, :].rearrange("p (k s) -> p k s", k=KC), ACT.Copy).then_inc(xT_ok, 1)
                    act.wait_ge(q_mm, at(i, u))
                    nc.scalar.activation(qT[:, :, :], pX[:, :].rearrange("p (k s) -> p k s", k=KC), ACT.Copy).then_inc(q_ok, 1)
                    act.wait_ge(v_mm, at(i, u))
                    nc.scalar.activation(val[u][:, :, :], pY[:, :].rearrange("p (t d) -> p t d", t=T), ACT.Copy).then_inc(v_ok, 1)

        @block.vector
        def _(dve):
            n = [0]

            def link(ins, sem_, base):
                n[0] += 1
                ins.then_inc(sem_, 1)
                hold(dve, sem_, base + n[0], passed)

            nc.vector.memset(zeros[:, :], 0.0).then_inc(zero_set, 1)
            PER = 3
            with dve.Fori(0, NB // 2) as i:
                for u in range(2):
                    n[0] = u * PER
                    base = i * (2 * PER)
                    dve.wait_ge(x_in[u], i * 16 + 16)
                    for t in range(T):
                        last = nc.vector.bn_stats(st[:, t, :], xin[u][:, t, :])
                    link(last, chain, base)
                    for t in range(T):
                        last = nc.vector.bn_aggr(mv[:, t, :], st[:, t, :])
                    link(last, chain, base)
                    nc.vector.tensor_scalar(veps[:, :], mv[:, :, 1], LN_EPS, None, ALU.add).then_inc(var_ok, 1)
                    dve.wait_ge(c_in[u], i * 16 + 16)
                    nc.vector.tensor_copy(parts[u][:, 0, :, :], cin[u][:, :, :]).then_inc(k_chain, 1)
                    dve.wait_ge(rstd_ok, at(i, u))
                    for t in range(T):
                        last = nc.vector.tensor_scalar(xn[u][:, t, :], xin[u][:, t, :], mv[:, t, 0:1], rstd[:, t:t + 1], ALU.subtract, ALU.mult)
                    link(last, chain, base)
                    assert n[0] == (u + 1) * PER
                    dve.sem_inc(xn_ok, 1)
                    dve.sem_inc(x_free, 1)
                    dve.wait_ge(k_chain, at(i, u, 2, 4))
                    nc.vector.tensor_copy(parts[u][:, 1, :, :], res[:, :, :]).then_inc(k_chain, 1)
            dve.wait_ge(mask_in, 16)
            dve.wait_ge(s_mm, 1)
            k = 0
            for j in range(2):
                nc.vector.tensor_tensor(AT[:, 0, 2 * j:2 * j + 2, :], pS[j][:, :].rearrange("p (h s) -> p h s", h=2),
                                        mask[:, 0, 2 * j:2 * j + 2, :], ALU.mult).then_inc(sc_chain, 1)
            nc.vector.memset(AT[:, 1, :, 0:P], 1.0)
            nc.vector.tensor_tensor(AT[:, 1, :, P:S], pS[2][:, :].rearrange("p (h s) -> p h s", h=H0),
                                    mask[:, 1, :, P:S], ALU.mult).then_inc(sc_chain, 1)
            dve.wait_ge(sc_chain, 3)
            flat = lambda t: t[:, :, :, :].rearrange("p t h s -> p (t h s)")
            nc.vector.scalar_tensor_tensor(out=flat(mask), in0=flat(AT), scalar=-1.0, in1=flat(AT), op0=ALU.mult, op1=ALU.max).then_inc(at_done, 1)
            dve.wait_ge(at_done, 1)
            nc.vector.tensor_scalar(flat(AT), flat(mask), 1.0, None, ALU.max).then_inc(at_done, 1)
            dve.wait_ge(at_done, 2)

        @block.tensor
        def _(pe):
            mm = nc.tensor.matmul
            pe.wait_ge(wh_in, 32)
            for h in range(H0):
                last = mm(pX[:, h * P:(h + 1) * P], whT[:, h, :], whT[:, h, :], start=True, stop=True)
            last.then_inc(gram_mm, 1)
            pe.wait_ge(zero_set, 1)
            for k in range(3):
                mm(pS[k][:, :], zeros[:, 0:P], zeros[:, :], start=True, stop=False, skip_group_check=True)
            pe.wait_ge(pool_c, 8)
            pe.wait_ge(gram_ok, 1)
            with pe.Fori(0, NB // 2) as i:
                for u in range(2):
                    pe.wait_ge(xn_ok, at(i, u))
                    for t in range(T):
                        for k in range(KC):
                            last = nc.tensor.transpose(pX[:, k * S + t * P:k * S + (t + 1) * P], xn[u][:, t, k * P:(k + 1) * P], ident[:, :])
                    last.then_inc(xT_mm, 1)
                    pe.wait_ge(cT_in[u], i * 16 + 16)
                    if u:
                        pe.wait_ge(v_ok, at(i, 0))
                    for t in range(T):
                        for h in range(H0):
                            last = mm(pY[:, t * D + h * P:t * D + (h + 1) * P], cT[u][:, h, t * P:(t + 1) * P], wh[:, h, :], start=True, stop=True)
                    last.then_inc(v_mm, 1)
                    pe.wait_ge(xT_ok, at(i, u))
                    for h in range(H0):
                        last = mm(pX[:, h * S:(h + 1) * S], gram[:, h, :], xnT[u][:, h, :], start=True, stop=True)
                    last.then_inc(q_mm, 1)
                    pe.wait_ge(q_ok, at(i, u))
                    for h in range(H0):
                        mm(pS[h // 2][:, (h % 2) * S:(h % 2 + 1) * S], cT[u][:, h, 0:P], qT[:, h, :], start=False, stop=False, skip_group_check=True)
                        last = mm(pS[2][:, h * P:(h + 1) * P], cT[u][:, h, P:S], qT[:, h, P:S], start=False, stop=False, skip_group_check=True)
                    last.then_inc(cT_free, 1)
                    pe.wait_ge(v_ok, at(i, u))
            for k in range(3):
                last = mm(pS[k][:, :], zeros[:, 0:P], zeros[:, :], start=False, stop=True, skip_group_check=True)
            last.then_inc(s_mm, 1)


def main_loop(nc, io, v):
    outer = v["outer"]
    with ExitStack() as ctx:
        sem = lambda n: outer.enter_context(nc.semaphore(n))
        sb = lambda n, s, d=F32: ctx.enter_context(nc.sbuf_tensor(n, s, d))
        ps = lambda n, s, d=F32: ctx.enter_context(nc.psum_tensor(n, s, d))
        ident, ident16, ones32, ones16, before16 = (v[n] for n in "ident ident16 ones32 ones16 before16".split())
        mhalf, iota_e, tok_f, tg_x, tg_f, AT = (v[n] for n in "mhalf iota_e tok_f tg_x tg_f AT".split())
        wg, wo, wupT, wdnT, wexp, wg0, wg1, wsu, wsd = (v[n] for n in "wg wo wupT wdnT wexp wg0 wg1 wsu wsd".split())
        gamma, beta, slots_all, comb_all = (v[n] for n in "gamma beta slots_all comb_all".split())
        xnT_d, v_d, kparts_d, qparts_d, xn4_d, acc_d, ids_d = (
            v[n] for n in "xnT_d v_d kparts_d qparts_d xn4_d acc_d ids_d".split())

        xin = [sb(f"b_x{u}", [P, T, D]) for u in range(2)]
        xnT = [sb(f"b_xnT{u}", [P, KC, S]) for u in range(2)]
        val = [sb(f"b_val{u}", [P, T, D]) for u in range(2)]
        cT = [sb(f"b_cT{u}", [P, KC, S]) for u in range(2)]
        ka = [sb(f"b_ka{u}", [P, HS, D], BF16) for u in range(2)]
        kb = [sb(f"b_kb{u}", [P, HS, D], BF16) for u in range(2)]
        qa = sb("b_qa", [P, HS, D], BF16)
        qb = sb("b_qb", [P, HS, D], BF16)
        KB = 3 * HD + 3
        norm = sb("b_norm", [P, T, D])
        normT = sb("b_normT", [P, KC, S])
        hT = sb("b_hT", [P, KC, S])
        zT = sb("b_zT", [P, KC, S])
        xs = sb("b_xs", [P, T, D])
        tmp = sb("b_tmp", [P, T, D])
        qp = sb("b_qp", [P, 3, T, D], BF16)
        probs = [sb(f"b_probs{k}", [P, G, D]) for k in range(2)]
        rsum = sb("b_rsum", [P, D])
        att = sb("b_att", [P, D])
        acc = sb("b_acc", [P, T, D])
        st = sb("b_st", [P, T, 6])
        mv = sb("b_mv", [P, T, 2])
        veps = sb("b_veps", [P, T])
        rstd = sb("b_rstd", [P, T])
        m8 = sb("b_m8", [P, T, 8])
        gap = sb("b_gap", [P, T, 1])
        egap = sb("b_egap", [P, T, 1])
        rw = sb("b_rw", [P, 3, T])
        nmx = sb("b_nmx", [P, T * 2, G])
        nmr = sb("b_nmr", [P, 2, T * 2, G])
        nmp = sb("b_nmp", [P, T * 2, 3, G], BF16)
        mrow = sb("b_mrow", [3 * G, D], BF16)
        eg = sb("b_eg", [P, T, E1])
        score = sb("b_score", [P, T, E1])
        top = sb("b_top", [P, T, 8])
        topi = sb("b_topi", [P, T, 8], U32)
        topf = sb("b_topf", [P, T, TOPK])
        onehot = sb("b_onehot", [P, T, TOPK, E1])
        chosen = sb("b_chosen", [P, T, E1])
        chosen16 = sb("b_chosen16", [P, T, E1], BF16)
        cum = sb("b_cum", [P, E1])
        cum16 = sb("b_cum16", [P, T, E1], BF16)
        ohp = sb("b_ohp", [P, T, TOPK, E1])
        pos = sb("b_pos", [P, T, TOPK])
        small = sb("b_small", [P, 6, T, TOPK])
        wsum = sb("b_wsum", [P, 2, T])
        addr = sb("b_addr", [P, T, TOPK], U32)
        tok = sb("b_tok", [P, T], U32)
        es = sb("b_es", [P, S])
        es2 = sb("b_es2", [P, S])
        shT = sb("b_shT", [P, S])

        pA = ps("b_pA", [P, 1024])
        pB = ps("b_pB", [P, 1024])
        pL = ps("b_pL", [P, 512])
        pL16 = ps("b_pL16", [P, 1024], BF16)
        pV = ps("b_pV", [P, 512])
        pZ = ps("b_pZ", [P, 512])
        a3 = lambda t: t[:, :].rearrange("p (k s) -> p k s", k=KC)
        t3 = lambda t: t[:, :].rearrange("p (t d) -> p t d", t=T)

        x_in, xnT_in, val_in, cT_in, k_in = ([sem(f"b_{n}_in{u}") for u in range(2)] for n in ("x", "xnT", "val", "cT", "k"))
        S_ = {}
        for name in ("wT_mm", "o_mm", "nT_mm", "x1_mm", "x2T_mm", "lg_mm", "up_mm", "ex_mm", "dn_mm",
                     "s_mm", "mT_mm", "st_mm", "pv_step", "x4T_mm", "gt_mm", "su_mm", "pos_mm", "sd_mm",
                     "chain", "var_ok", "rstd_ok", "n_ok", "zT_ok", "x2n_ok", "gap_ok", "x2_ok", "q_chain",
                     "mx_ok", "nmp_ok", "att_ok", "x3_ok", "x4n_ok", "m_ok", "route_ok", "shT_ok", "acc_ok",
                     "yT_ok", "x2T_ok", "uT_ok", "egap_ok", "mrow_ok", "exp_ok", "x4T_ok", "eg_ok", "es_ok",
                     "ones_ok", "cum_ok", "addr_free", "passed", "pool_passed"):
            S_[name] = sem("b_" + name)
        qst, qld, mld, x4st, accst, scat = (sem("b_" + n) for n in "qst qld mld x4st accst scat".split())
        block = ctx.enter_context(nc.Block())
        W = S_

        @block.sync
        def _(sp):
            def load(b, u):
                sp.dma_start(xnT[u][:, :, :], xnT_d[bass.ds(b, 1), :, :].rearrange("o p (k s) -> (o p) k s", k=KC)).then_inc(xnT_in[u], 16)
                sp.dma_start(val[u][:, :, :], v_d[bass.ds(b, 1), :, :].rearrange("o p (t d) -> (o p) t d", t=T)).then_inc(val_in[u], 16)
                sp.dma_start(xin[u][:, :, :], io["x"][bass.ds(b, 1), :, :].rearrange("o (t p) d -> p (o t) d", p=P)).then_inc(x_in[u], 16)
                sp.dma_start(cT[u][:, :, :], io["ctxT"][bass.ds(b, 1), :, :].rearrange("o p (k s) -> (o p) k s", k=KC)).then_inc(cT_in[u], 16)
                for blk, part in enumerate((0, 1, 0, 1)):
                    sp.dma_start(ka[u][HD * blk:HD * (blk + 1), :, :],
                                 kparts_d[part, bass.ds(b * S, S), :].rearrange("(h r) d -> r h d", r=HD)).then_inc(k_in[u], 16)
                for blk, part in enumerate((0, 2, 2)):
                    sp.dma_start(kb[u][HD * blk:HD * (blk + 1), :, :],
                                 kparts_d[part, bass.ds(b * S, S), :].rearrange("(h r) d -> r h d", r=HD)).then_inc(k_in[u], 16)

            def work(i, u):
                b = i * 2 + u
                sp.wait_ge(W["q_chain"], at(i, u, 4, 4))
                for k in range(3):
                    sp.dma_start(qparts_d[u, k, :, :].rearrange("(t p) d -> p t d", p=P), qp[:, k, :, :]).then_inc(qst, 16)
                sp.wait_ge(qst, at(i, u) * 48)
                for blk, part in enumerate((0, 0, 1, 1)):
                    sp.dma_start(qa[HD * blk:HD * (blk + 1), :, :],
                                 qparts_d[u, part, :, :].rearrange("(h r) d -> r h d", r=HD)).then_inc(qld, 16)
                for blk, part in enumerate((2, 0, 1)):
                    sp.dma_start(qb[HD * blk:HD * (blk + 1), :, :],
                                 qparts_d[u, part, :, :].rearrange("(h r) d -> r h d", r=HD)).then_inc(qld, 16)
                for g in range(NG):
                    sp.wait_ge(W["mrow_ok"], at(i, u, g + 1, NG))
                    for k in range(3):
                        sp.dma_start(qb[3 * HD + k:3 * HD + k + 1, G * g:G * (g + 1), :], mrow[G * k:G * (k + 1), :]).then_inc(mld, 16)
                sp.wait_ge(W["x4n_ok"], at(i, u))
                sp.dma_start(xn4_d[bass.ds(b * S, S), :].rearrange("(t p) d -> p t d", p=P), norm[:, :, :]).then_inc(x4st, 16)
                sp.wait_ge(W["acc_ok"], at(i, u) + 1)
                sp.dma_start(acc_d[bass.ds(b * T, T), :, :].rearrange("t p d -> p t d"), acc[:, :, :]).then_inc(accst, 16)

            sp.sem_inc(x4st, 16)
            sp.sem_inc(accst, 16)
            sp.wait_ge(W["ones_ok"], 1)
            for u in range(2):
                load(u, u)
            with sp.Fori(0, NB // 2 - 1) as i:
                for u in range(2):
                    work(i, u)
                    sp.wait_ge(W["pv_step"], at(i, u, NG * KC, NG * KC))
                    load(i * 2 + (2 + u), u)
            for u in range(2):
                work(NB // 2 - 1, u)
            sp.wait_ge(x4st, 16 * (NB + 1))
            sp.wait_ge(accst, 16 * (NB + 1))
            sp.wait_ge(qst, 48 * NB)

        @block.gpsimd
        def _(pool):
            g_ = nc.gpsimd
            for u in range(2):
                last = g_.memset(kb[u][3 * HD:3 * HD + 3, :, :], 1.0)
            last.then_inc(W["ones_ok"], 1)
            pool.wait_ge(W["ones_ok"], 1)
            g_.memset(cum[:, :], 0.0).then_inc(W["cum_ok"], 1)
            pool.sem_inc(W["addr_free"], 1)

            def rsqrt(i, u, k):
                pool.wait_ge(W["var_ok"], at(i, u, k, 4))
                g_.tensor_tensor(rstd[:, :], veps[:, :], mhalf[:, :], ALU.pow).then_inc(W["rstd_ok"], 1)

            with pool.Fori(0, NB // 2) as i:
                for u in range(2):
                    for k in range(1, 4):
                        rsqrt(i, u, k)
                    pool.wait_ge(W["q_chain"], at(i, u, 1, 4))
                    g_.tensor_tensor(tmp[:, :, :], norm[:, :, :], qp[:, 0, :, :], ALU.subtract).then_inc(W["q_chain"], 1)
                    pool.wait_ge(W["q_chain"], at(i, u, 3, 4))
                    g_.tensor_tensor(qp[:, 2, :, :], tmp[:, :, :], qp[:, 1, :, :], ALU.subtract).then_inc(W["q_chain"], 1)
                    for g in range(NG):
                        pool.wait_ge(W["att_ok"], at(i, u, g + 1, NG))
                        g_.tensor_tensor(xs[:, g, :], xs[:, g, :], att[:, :], ALU.add).then_inc(W["x3_ok"], 1)
                    rsqrt(i, u, 4)
                    hold(pool, W["route_ok"], at(i, u), W["pool_passed"])
                    for t in range(T):
                        for k in range(TOPK):
                            g_.indirect_dma_start(out=ids_d, out_offset=bass.IndirectOffsetOnAxis(ap=addr[:, t, k:k + 1], axis=0),
                                                  in_=tok[:, t:t + 1], in_offset=None, bounds_check=P * P - 1,
                                                  oob_is_err=False).then_inc(scat, 16)
                    hold(pool, scat, at(i, u) * (16 * T * TOPK), W["addr_free"])

        @block.scalar
        def _(act):
            A = nc.scalar.activation
            act.preload_act_table(ACT.Exp)
            with act.Fori(0, NB // 2) as i:
                for u in range(2):
                    act.wait_ge(W["nT_mm"], at(i, u))
                    for k in range(KC):
                        last = A(hT[:, k, :], a3(pB)[:, k, :], ACT.Identity, bias=beta[:, k:k + 1], scale=gamma[:, k:k + 1])
                    last.then_inc(W["yT_ok"], 1)
                    act.wait_ge(W["x2T_mm"], at(i, u))
                    A(normT[:, :, :], a3(pB), ACT.Copy).then_inc(W["x2T_ok"], 1)
                    act.wait_ge(W["gap_ok"], at(i, u))
                    A(egap[:, :, :], gap[:, :, :], ACT.Exp).then_inc(W["egap_ok"], 1)
                    act.wait_ge(W["up_mm"], at(i, u))
                    A(hT[:, :, :], a3(pA), ACT.Relu).then_inc(W["uT_ok"], 1)

                    def maxima(g):
                        act.wait_ge(W["mT_mm"], at(i, u, g + 1, NG))
                        if g:
                            act.wait_ge(mld, at(i, u, 1, NG) * 48)
                        A(mrow[:, :], pL16[0:3 * G, 0:D], ACT.Copy).then_inc(W["mrow_ok"], 1)

                    maxima(0)
                    for j in range(NG * KC * 2):
                        c, pair = j // 2, j % 2
                        act.wait_ge(W["st_mm"], at(i, u, j + 1, NG * KC * 2))
                        if pair == 0 and c >= 2:
                            act.wait_ge(W["pv_step"], at(i, u, c - 1, NG * KC))
                        A(probs[c % 2][:, 2 * pair:2 * pair + 2, :], t3((pA, pB)[pair]), ACT.Exp, scale=SCALE1).then_inc(W["exp_ok"], 1)
                        if j == 2:
                            maxima(1)
                    act.wait_ge(W["x4T_mm"], at(i, u))
                    A(normT[:, :, :], a3(pA), ACT.Copy).then_inc(W["x4T_ok"], 1)
                    act.wait_ge(W["gt_mm"], at(i, u))
                    A(eg[:, :, :], pL[:, 0:T * E1].rearrange("p (t e) -> p t e", t=T), ACT.Exp, scale=-1.0).then_inc(W["eg_ok"], 1)
                    act.wait_ge(W["su_mm"], at(i, u))
                    A(es[:, :], pB[:, S:2 * S], ACT.Exp, scale=-1.0).then_inc(W["es_ok"], 1)

        @block.vector
        def _(dve):
            V = nc.vector
            n = [0]
            PER = 52

            def link(ins, base, alone=False):
                n[0] += 1
                ins.then_inc(W["chain"], 1)
                if alone:
                    hold(dve, W["chain"], base + n[0], W["passed"])
                else:
                    dve.wait_ge(W["chain"], base + n[0])

            def layernorm(i, u, base, src, k, eps, ok):
                for t in range(T):
                    last = V.bn_stats(st[:, t, :], src(t))
                link(last, base, alone=True)
                for t in range(T):
                    last = V.bn_aggr(mv[:, t, :], st[:, t, :])
                link(last, base)
                V.tensor_scalar(veps[:, :], mv[:, :, 1], eps, None, ALU.add).then_inc(W["var_ok"], 1)
                dve.wait_ge(W["rstd_ok"], at(i, u, k, 4))
                for t in range(T):
                    last = V.tensor_scalar(norm[:, t, :], src(t), mv[:, t, 0:1], rstd[:, t:t + 1], ALU.subtract, ALU.mult)
                return last.then_inc(W[ok], 1)

            dve.sem_inc(W["acc_ok"], 1)
            with dve.Fori(0, NB // 2) as i:
                for u in range(2):
                    n[0] = u * PER
                    base = i * (2 * PER)
                    dve.wait_ge(W["o_mm"], at(i, u))
                    dve.wait_ge(x4st, at(i, u) * 16)
                    layernorm(i, u, base, lambda t: pB[:, t * D:(t + 1) * D], 1, GN_EPS, "n_ok")
                    dve.wait_ge(W["yT_ok"], at(i, u))
                    dve.wait_ge(W["wT_mm"], at(i, u))
                    V.scalar_tensor_tensor(out=zT[:, :, :], in0=a3(pA), scalar=0.0, in1=hT[:, :, :],
                                           op0=ALU.max, op1=ALU.mult).then_inc(W["zT_ok"], 1)
                    dve.wait_ge(W["x1_mm"], at(i, u))
                    dve.wait_ge(x_in[u], i * 16 + 16)
                    link(V.scalar_tensor_tensor(out=xs[:, :, :], in0=t3(pA), scalar=tg_x[:, 0:1], in1=xin[u][:, :, :],
                                                op0=ALU.mult, op1=ALU.add), base)
                    layernorm(i, u, base, lambda t: xs[:, t, :], 2, LN_EPS, "x2n_ok")
                    hold(dve, W["lg_mm"], at(i, u), W["passed"])
                    for t in range(T):
                        last = V.max(m8[:, t, :], pL[:, t * E0:(t + 1) * E0])
                    link(last, base)
                    V.tensor_tensor(gap[:, :, :], m8[:, :, 1:2], m8[:, :, 0:1], ALU.subtract).then_inc(W["gap_ok"], 1)
                    dve.wait_ge(W["egap_ok"], at(i, u))
                    e_ = egap[:, :, 0]
                    link(V.tensor_scalar(rw[:, 0, :], e_, 1.0, None, ALU.add), base)
                    link(V.reciprocal(rw[:, 1, :], rw[:, 0, :]), base)
                    link(V.tensor_tensor(rw[:, 2, :], rw[:, 1, :], e_, ALU.mult), base)
                    link(V.tensor_tensor(rw[:, 0, :], rw[:, 1, :], rw[:, 2, :], ALU.add), base)
                    link(V.tensor_scalar(rw[:, 2, :], rw[:, 0, :], tg_f[:, 0:1], None, ALU.mult), base)
                    dve.wait_ge(W["ex_mm"], at(i, u))
                    for t in range(T):
                        last = V.scalar_tensor_tensor(out=xs[:, t, :], in0=pB[:, t * D:(t + 1) * D], scalar=rw[:, 2, t:t + 1],
                                                      in1=xs[:, t, :], op0=ALU.mult, op1=ALU.add)
                    link(last, base)
                    dve.wait_ge(W["dn_mm"], at(i, u))
                    link(V.scalar_tensor_tensor(out=xs[:, :, :], in0=t3(pA), scalar=tg_f[:, 0:1], in1=xs[:, :, :],
                                                op0=ALU.mult, op1=ALU.add), base)
                    layernorm(i, u, base, lambda t: xs[:, t, :], 3, LN_EPS, "x2_ok")
                    dve.wait_ge(W["x2_ok"], at(i, u))
                    V.tensor_copy(qp[:, 0, :, :], norm[:, :, :]).then_inc(W["q_chain"], 1)
                    dve.wait_ge(W["q_chain"], at(i, u, 2, 4))
                    V.tensor_copy(qp[:, 1, :, :], tmp[:, :, :]).then_inc(W["q_chain"], 1)

                    def maxima(g):
                        link(V.tensor_copy(nmp[:, :, 0, :], nmx[:, :, :]), base)
                        link(V.tensor_tensor(nmr[:, 0, :, :], nmx[:, :, :], nmp[:, :, 0, :], ALU.subtract), base)
                        link(V.tensor_copy(nmp[:, :, 1, :], nmr[:, 0, :, :]), base)
                        link(V.tensor_tensor(nmr[:, 1, :, :], nmr[:, 0, :, :], nmp[:, :, 1, :], ALU.subtract), base)
                        V.tensor_copy(nmp[:, :, 2, :], nmr[:, 1, :, :]).then_inc(W["nmp_ok"], 1)

                    for j in range(2 * HS):
                        h, half = j // 2, j % 2
                        dve.wait_ge(W["s_mm"], at(i, u, j + 1, 2 * HS))
                        r = V.tensor_reduce(nmx[:, 2 * half:2 * half + 2, h % G], t3((pA, pB)[half]), axis=AX.X, op=ALU.max, negate=True)
                        r.then_inc(W["mx_ok"], 1)
                        if h % G == G - 1 and half:
                            dve.wait_ge(W["mx_ok"], at(i, u, j + 1, 2 * HS))
                            if h == HS - 1:
                                dve.wait_ge(W["mT_mm"], at(i, u, 1, NG))
                            maxima(h // G)
                    for g in range(NG):
                        dve.wait_ge(W["pv_step"], at(i, u, KC * (g + 1), NG * KC))
                        if g:
                            dve.wait_ge(W["x3_ok"], at(i, u, g, NG))
                        link(V.reciprocal(rsum[:, :], pZ[:, :]), base)
                        V.scalar_tensor_tensor(out=att[:, :], in0=pV[:, :], scalar=tg_x[:, 1:2], in1=rsum[:, :],
                                               op0=ALU.mult, op1=ALU.mult).then_inc(W["att_ok"], 1)
                    dve.wait_ge(W["x3_ok"], at(i, u, NG, NG))
                    layernorm(i, u, base, lambda t: xs[:, t, :], 4, LN_EPS, "x4n_ok")
                    dve.wait_ge(W["eg_ok"], at(i, u))
                    link(V.tensor_scalar(eg[:, :, :], eg[:, :, :], 1.0, None, ALU.add), base)
                    link(V.reciprocal(score[:, :, :], eg[:, :, :]), base, alone=True)
                    for t in range(T):
                        last = V.max(top[:, t, :], score[:, t, :])
                    link(last, base, alone=True)
                    for t in range(T):
                        last = V.max_index(topi[:, t, :], top[:, t, :], score[:, t, :])
                    link(last, base)
                    link(V.tensor_copy(topf[:, :, :], topi[:, :, 0:TOPK]), base)
                    for t in range(T):
                        last = V.tensor_tensor(onehot[:, t, :, :], iota_e[:, :].unsqueeze(1).broadcast_to([P, TOPK, E1]),
                                               topf[:, t, :].unsqueeze(2).broadcast_to([P, TOPK, E1]), ALU.is_equal)
                    link(last, base)
                    link(V.tensor_reduce(chosen[:, :, :], onehot[:, :, :, :].rearrange("p t k e -> p t e k"), axis=AX.X, op=ALU.add), base)
                    V.tensor_copy(chosen16[:, :, :], chosen[:, :, :])
                    if u == 0:
                        dve.wait_ge(W["cum_ok"], 1)
                    for t in range(T):
                        V.tensor_copy(cum16[:, t, :], cum[:, :])
                        last = V.tensor_tensor(cum[:, :], cum[:, :], chosen[:, t, :], ALU.add)
                        if t < T - 1:
                            link(last, base)
                    link(last, base)
                    dve.sem_inc(W["m_ok"], 1)
                    link(V.tensor_reduce(wsum[:, 0, :], top[:, :, 0:TOPK], axis=AX.X, op=ALU.add), base)
                    link(V.reciprocal(wsum[:, 1, :], wsum[:, 0, :]), base)
                    dve.wait_ge(W["es_ok"], at(i, u))
                    link(V.tensor_scalar(es[:, :], es[:, :], 1.0, None, ALU.add), base)
                    link(V.reciprocal(es2[:, :], es[:, :]), base)
                    link(V.tensor_tensor(es[:, :], pB[:, S:2 * S], es2[:, :], ALU.mult), base)
                    V.tensor_tensor(shT[:, :], pB[:, 0:S], es[:, :], ALU.mult).then_inc(W["shT_ok"], 1)
                    dve.wait_ge(W["pos_mm"], at(i, u))
                    for t in range(T):
                        last = V.tensor_tensor(ohp[:, t, :, :], onehot[:, t, :, :],
                                               pL[:, t * E1:(t + 1) * E1].unsqueeze(1).broadcast_to([P, TOPK, E1]), ALU.mult)
                    link(last, base)
                    link(V.tensor_reduce(pos[:, :, :], ohp[:, :, :, :], axis=AX.X, op=ALU.add), base)
                    fits, high, a_, b_, c_, d_ = (small[:, k, :, :] for k in range(6))
                    V.tensor_scalar(fits, pos[:, :, :], float(CAP), None, ALU.is_lt)
                    V.tensor_scalar(high, pos[:, :, :], float(P), None, ALU.is_ge)
                    V.tensor_scalar(a_, topf[:, :, :], 2.0, None, ALU.mult)
                    link(V.tensor_scalar(b_, pos[:, :, :], float(CAP - 1), None, ALU.min), base)
                    V.scalar_tensor_tensor(out=slots_all[:, bass.ds(i * (2 * T) + u * T, T), :], in0=topf[:, :, :], scalar=float(CAP), in1=b_, op0=ALU.mult, op1=ALU.add)
                    link(V.scalar_tensor_tensor(out=c_, in0=pos[:, :, :], scalar=float(P), in1=a_, op0=ALU.mult, op1=ALU.add), base)
                    link(V.scalar_tensor_tensor(out=d_, in0=high, scalar=-float(P * P - 1), in1=c_, op0=ALU.mult, op1=ALU.add), base)
                    link(V.tensor_scalar(a_, fits, -SKIP, SKIP, ALU.mult, ALU.add), base)
                    link(V.tensor_tensor(b_, fits, top[:, :, 0:TOPK], ALU.mult), base)
                    for t in range(T):
                        V.tensor_scalar(comb_all[:, bass.ds(i * (2 * T) + (u * T + t), 1), :].rearrange("p o k -> p (o k)"),
                                        b_[:, t, :], wsum[:, 1, t:t + 1], tg_f[:, 1:2], ALU.mult, ALU.mult)
                    dve.wait_ge(W["addr_free"], at(i, u))
                    V.tensor_tensor(addr[:, :, :], d_, a_, ALU.add)
                    for t in range(T):
                        last = V.tensor_copy(tok[:, t:t + 1], tok_f[:, :])
                        link(last, base)
                        last = V.tensor_scalar(tok_f[:, :], tok_f[:, :], float(P), None, ALU.add)
                        link(last, base)
                    dve.sem_inc(W["route_ok"], 1)
                    dve.wait_ge(accst, at(i, u) * 16)
                    dve.wait_ge(W["sd_mm"], at(i, u))
                    V.scalar_tensor_tensor(out=acc[:, :, :], in0=t3(pA), scalar=tg_f[:, 1:2], in1=xs[:, :, :],
                                           op0=ALU.mult, op1=ALU.add).then_inc(W["acc_ok"], 1)
                    assert n[0] == (u + 1) * PER, n[0]

        @block.tensor
        def _(pe):
            mm, tr = nc.tensor.matmul, nc.tensor.transpose

            def transposes(dst, src):
                for t in range(T):
                    for k in range(KC):
                        last = tr(dst[:, k * S + t * P:k * S + (t + 1) * P], src[:, t, k * P:(k + 1) * P], ident[:, :])
                return last

            def by_rows(dst, lhs, w, n, k_all=KC):
                for t in range(T):
                    for k in range(k_all):
                        last = mm(dst[:, t * n:(t + 1) * n], lhs(k)[:, t * P:(t + 1) * P], w(k), start=(k == 0), stop=(k == k_all - 1))
                return last

            def by_features(dst, w, rhs, n_out):
                for o in range(n_out):
                    for k in range(KC):
                        last = mm(dst[:, o * S:(o + 1) * S], w[:, k, o * P:(o + 1) * P], rhs[:, k, :], start=(k == 0), stop=(k == KC - 1))
                return last

            with pe.Fori(0, NB // 2) as i:
                for u in range(2):
                    in_u = i * 16 + 16
                    pe.wait_ge(W["acc_ok"], at(i, u))
                    pe.wait_ge(xnT_in[u], in_u)
                    by_features(pA, wg, xnT[u], KC).then_inc(W["wT_mm"], 1)
                    pe.wait_ge(val_in[u], in_u)
                    for s in range(T):
                        for h in range(H0):
                            for t in range(T):
                                last = mm(pB[:, s * D + h * P:s * D + (h + 1) * P], AT[:, t, h, s * P:(s + 1) * P],
                                          val[u][:, t, h * P:(h + 1) * P], start=(t == 0), stop=(t == T - 1))
                    last.then_inc(W["o_mm"], 1)
                    pe.wait_ge(W["n_ok"], at(i, u))
                    transposes(pB, norm).then_inc(W["nT_mm"], 1)
                    pe.wait_ge(W["zT_ok"], at(i, u))
                    by_rows(pA, lambda k: zT[:, k, :], lambda k: wo[:, k, :], D).then_inc(W["x1_mm"], 1)
                    pe.wait_ge(W["x2n_ok"], at(i, u))
                    transposes(pB, norm).then_inc(W["x2T_mm"], 1)
                    pe.wait_ge(W["x2T_ok"], at(i, u))
                    by_rows(pL, lambda k: normT[:, k, :], lambda k: wg0[:, k, :], E0).then_inc(W["lg_mm"], 1)
                    by_features(pA, wupT, normT, KC).then_inc(W["up_mm"], 1)
                    by_rows(pB, lambda k: normT[:, k, :], lambda k: wexp[:, k, :], D).then_inc(W["ex_mm"], 1)
                    pe.wait_ge(W["uT_ok"], at(i, u))
                    by_rows(pA, lambda k: hT[:, k, :], lambda k: wdnT[:, k, :], D).then_inc(W["dn_mm"], 1)

                    def maxima(g):
                        pe.wait_ge(W["nmp_ok"], at(i, u, g + 1, NG))
                        if g:
                            pe.wait_ge(W["mrow_ok"], at(i, u, 1, NG))
                        for m in range(KC):
                            last = tr(pL16[0:3 * G, m * P:(m + 1) * P], nmp[:, m, :, :].rearrange("p k h -> p (k h)"), ident16[:, :])
                        last.then_inc(W["mT_mm"], 1)

                    pe.wait_ge(k_in[u], in_u * 7)
                    pe.wait_ge(qld, at(i, u) * 112)
                    for j in range(2 * HS):
                        h, half = j // 2, j % 2
                        if j >= 2:
                            pe.wait_ge(W["mx_ok"], at(i, u, j - 1, 2 * HS))
                        for c in range(2):
                            m = 2 * half + c
                            last = mm((pA, pB)[half][:, c * D:(c + 1) * D], qa[:, h, m * P:(m + 1) * P], ka[u][:, h, :], start=True, stop=True)
                        last.then_inc(W["s_mm"], 1)
                        if j == 2 * G + G - 1:
                            maxima(0)

                    def weighted(s):
                        g, c = s // KC, s % KC
                        pe.wait_ge(W["exp_ok"], at(i, u, 2 * (s + 1), 2 * NG * KC))
                        if g and c == 0:
                            pe.wait_ge(W["att_ok"], at(i, u, 1, NG))
                        for q in range(G):
                            r = (g * G + q) * HD
                            mm(pV[q * HD:(q + 1) * HD, :], cT[u][:, c, r:r + HD], probs[s % 2][:, q, :], start=(c == 0), stop=(c == KC - 1))
                        for q in range(G):
                            last = mm(pZ[q * HD:(q + 1) * HD, :], ones32[:, :], probs[s % 2][:, q, :], start=(c == 0), stop=(c == KC - 1))
                        last.then_inc(W["pv_step"], 1)

                    pe.wait_ge(cT_in[u], in_u)
                    for s in range(NG * KC):
                        g, c = s // KC, s % KC
                        if c == 0:
                            pe.wait_ge(mld, at(i, u, g + 1, NG) * 48)
                        for pair in range(2):
                            j = 2 * s + pair
                            if j < 2:
                                pe.wait_ge(W["mx_ok"], at(i, u, 2 * HS - 1 + j, 2 * HS))
                            else:
                                pe.wait_ge(W["exp_ok"], at(i, u, j - 1, 2 * NG * KC))
                            for x in range(2):
                                h = g * G + 2 * pair + x
                                dst = (pA, pB)[pair][:, x * D:(x + 1) * D]
                                mm(dst, ka[u][:, h, c * P:(c + 1) * P], qa[:, h, :], start=True, stop=False)
                                last = mm(dst, kb[u][0:KB, h, c * P:(c + 1) * P], qb[0:KB, h, :], start=False, stop=True)
                            last.then_inc(W["st_mm"], 1)
                        if s == 1:
                            maxima(1)
                        if s >= 1:
                            weighted(s - 1)
                    weighted(NG * KC - 1)
                    pe.wait_ge(W["x4n_ok"], at(i, u))
                    transposes(pA, norm).then_inc(W["x4T_mm"], 1)
                    pe.wait_ge(W["x4T_ok"], at(i, u))
                    by_rows(pL, lambda k: normT[:, k, :], lambda k: wg1[:, k, :], E1).then_inc(W["gt_mm"], 1)
                    by_features(pB, wsu, normT, 2).then_inc(W["su_mm"], 1)
                    pe.wait_ge(W["m_ok"], at(i, u))
                    for t in range(T):
                        mm(pL[:, t * E1:(t + 1) * E1], before16[:, :], chosen16[:, t, :], start=True, stop=False)
                        last = mm(pL[:, t * E1:(t + 1) * E1], ones16[:, :], cum16[:, t, :], start=False, stop=True)
                    last.then_inc(W["pos_mm"], 1)
                    pe.wait_ge(W["shT_ok"], at(i, u))
                    by_rows(pA, lambda k: shT[:, :], lambda k: wsd[:, :], D, 1).then_inc(W["sd_mm"], 1)


def experts(nc, io, out, v):
    outer = v["outer"]
    with ExitStack() as ctx:
        sem = lambda n: outer.enter_context(nc.semaphore(n))
        sb = lambda n, s, d=F32: ctx.enter_context(nc.sbuf_tensor(n, s, d))
        ps = lambda n, s, d=F32: ctx.enter_context(nc.psum_tensor(n, s, d))
        ident, slots_all, comb_all = v["ident"], v["slots_all"], v["comb_all"]
        ids_d, xn4_d, eout_d, acc_d = v["ids_d"], v["xn4_d"], v["eout_d"], v["acc_d"]
        TP = 2 * HT
        ids = sb("e_ids", [P, P], U32)
        two = lambda name, shape, dt=F32: [sb(f"e_{name}{u}", shape, dt) for u in range(2)]
        idx = two("idx", [P, TP], U32)
        xg = two("xg", [P, TP, D])
        xT = two("xT", [P, 2, KC, CAP])
        wu = two("wu", [P, 2, KC, 2 * HE])
        wd = two("wd", [2 * HE, D])
        gate = two("gate", [2 * HE, CAP])
        hT = two("hT", [2 * HE, CAP])
        eo = two("eo", [P, TP, D])
        cidx = two("cidx", [P, TOPK], U32)
        rows_ = two("rows", [P, TOPK, D])
        tot = two("tot", [P, D])
        pT = [ps(f"e_pT{e}", [P, KC * CAP]) for e in range(2)]
        pU = ps("e_pU", [P, 2 * CAP])
        pD = [ps(f"e_pD{k}", [P, D]) for k in range(2)]

        ids_in = sem("e_ids_in")
        gath, wu_in, wd_in, est, cg, acc_in, ost = ([sem(f"e_{n}{u}") for u in range(2)] for n in "gath wu_in wd_in est cg acc_in ost".split())
        pool_passed = sem("e_pool_passed")
        idx_ok, cidx_ok, T_mm, up_mm, dn_mm = (sem("e_" + n) for n in "idx_ok cidx_ok T_mm up_mm dn_mm".split())
        xA_ok, xB_ok, gate_ok, h_ok, oe_ok, oo_ok, tchain, tot_ok = (sem("e_" + n) for n in "xA_ok xB_ok gate_ok h_ok oe_ok oo_ok tchain tot_ok".split())
        block = ctx.enter_context(nc.Block())

        def pipelined(eng, transpose, up, down):
            transpose(0, 0)
            transpose(0, 1)
            up(0, 0)
            with eng.Fori(0, PAIRS // 2 - 1) as i:
                for c in range(2):
                    transpose(i, c + 2)
                    down(i, c)
                    up(i, c + 1)
            last = PAIRS // 2 - 1
            down(last, 0)
            up(last, 1)
            down(last, 1)

        def pair_of(i, c):
            return i * 2 + c

        def wait_count(eng, s, i, c, per=1, less=0):
            if isinstance(i, int) and (2 * i + c + 1) * per - less <= 0:
                return
            eng.wait_ge(s, i * (2 * per) + ((c + 1) * per - less))

        @block.sync
        def _(sp):
            def load(i, c):
                u = c % 2
                sp.dma_start(wu[u][:, :, :, :], io["wu"][bass.ds(pair_of(i, c), 1), :, :].rearrange("o p (e k n) -> (o p) e k n", e=2, k=KC)).then_inc(wu_in[u], 16)
                sp.dma_start(wd[u][:, :], io["wd"][bass.ds(pair_of(i, c), 1), :, :].rearrange("o p n -> (o p) n")).then_inc(wd_in[u], 16)

            def store(i, c):
                u = c % 2
                wait_count(sp, oe_ok, i, c, 2)
                wait_count(sp, oo_ok, i, c, 2)
                sp.dma_start(eout_d[bass.ds(pair_of(i, c) * (2 * CAP), 2 * CAP), :].rearrange("(t p) d -> p t d", p=P), eo[u][:, :, :]).then_inc(est[u], 16)

            sp.dma_start(ids[:, :], v["ids_d"].rearrange("(p n) o -> p (n o)", p=P)).then_inc(ids_in, 16)
            for c in range(2):
                load(0, c)
            with sp.Fori(0, PAIRS // 2 - 1) as i:
                for c in range(2):
                    store(i, c)
                    load(i, c + 2)
            for c in range(2):
                store(PAIRS // 2 - 1, c)
            def load_acc(i, u):
                sp.dma_start(tot[u][:, :], acc_d[bass.ds(i * 2 + u, 1), :, :].rearrange("o p d -> (o p) d")).then_inc(acc_in[u], 16)

            def store_out(i, u):
                sp.wait_ge(tot_ok, i * 2 + (u + 1))
                sp.dma_start(out.rearrange("b (t p) d -> (b t) p d", p=P)[bass.ds(i * 2 + u, 1), :, :].rearrange("o p d -> (o p) d"),
                             tot[u][:, :]).then_inc(ost[u], 16)

            for u in range(2):
                load_acc(0, u)
            with sp.Fori(0, NT // 2 - 1) as i:
                for u in range(2):
                    store_out(i, u)
                    sp.wait_ge(ost[u], i * 16 + 16)
                    load_acc(i + 1, u)
            for u in range(2):
                store_out(NT // 2 - 1, u)
            for u in range(2):
                sp.wait_ge(ost[u], 16 * (NT // 2))
                sp.wait_ge(est[u], 16 * (PAIRS // 2))

        @block.gpsimd
        def _(pool):
            g_ = nc.gpsimd

            def gather(i, c):
                u = c % 2
                wait_count(pool, T_mm, i, c - 2)
                g_.tensor_copy(idx[u][:, :], ids[:, bass.ds(pair_of(i, c) * TP, TP)]).then_inc(idx_ok, 1)
                wait_count(pool, idx_ok, i, c)
                pool.sem_inc(pool_passed, 1)
                for t in range(TP):
                    g_.indirect_dma_start(out=xg[u][:, t, :], out_offset=None, in_=xn4_d,
                                          in_offset=bass.IndirectOffsetOnAxis(ap=idx[u][:, t:t + 1], axis=0)).then_inc(gath[u], 16)

            pool.wait_ge(ids_in, 16)
            gather(0, 0)
            gather(0, 1)
            with pool.Fori(0, PAIRS // 2 - 1) as i:
                for c in range(2):
                    gather(i, c + 2)
            for u in range(2):
                pool.wait_ge(est[u], 16 * (PAIRS // 2))

            def collect(i, u):
                wait_tile = i * 2 + u
                g_.tensor_copy(cidx[u][:, :], slots_all[:, bass.ds(wait_tile, 1), :].rearrange("p o k -> p (o k)")).then_inc(cidx_ok, 1)
                hold(pool, cidx_ok, i * 2 + (u + 1), pool_passed)
                for k in range(TOPK):
                    g_.indirect_dma_start(out=rows_[u][:, k, :], out_offset=None, in_=eout_d,
                                          in_offset=bass.IndirectOffsetOnAxis(ap=cidx[u][:, k:k + 1], axis=0)).then_inc(cg[u], 16)

            for u in range(2):
                collect(0, u)
            with pool.Fori(0, NT // 2 - 1) as i:
                for u in range(2):
                    pool.wait_ge(tot_ok, i * 2 + (u + 1))
                    collect(i + 1, u)

        @block.scalar
        def _(act):
            A = nc.scalar.activation
            act.preload_act_table(ACT.Silu)

            def transpose(i, c):
                wait_count(act, T_mm, i, c)
                wait_count(act, up_mm, i, c - 2)
                A(xT[c % 2][:, 0, :, :], pT[0][:, :].rearrange("p (k s) -> p k s", k=KC), ACT.Copy).then_inc(xA_ok, 1)

            def up(i, c):
                wait_count(act, up_mm, i, c)
                A(gate[c % 2][:, :], pU[:, 0:CAP], ACT.Silu).then_inc(gate_ok, 1)

            def down(i, c):
                if not (isinstance(i, int) and i == 0 and c < 2):
                    act.wait_ge(est[c % 2], store_count(i, c))
                for k in (0, 2):
                    wait_count(act, dn_mm, i, c, TP, TP - k - 1)
                    A(eo[c % 2][:, k, :], pD[0][:, :], ACT.Copy).then_inc(oe_ok, 1)

            pipelined(act, transpose, up, down)

        @block.vector
        def _(dve):
            V = nc.vector

            def transpose(i, c):
                wait_count(dve, T_mm, i, c)
                wait_count(dve, up_mm, i, c - 2)
                V.tensor_copy(xT[c % 2][:, 1, :, :], pT[1][:, :].rearrange("p (k s) -> p k s", k=KC)).then_inc(xB_ok, 1)

            def up(i, c):
                wait_count(dve, gate_ok, i, c)
                wait_count(dve, dn_mm, i, c - 2, TP)
                V.tensor_tensor(hT[c % 2][:, :], pU[:, CAP:2 * CAP], gate[c % 2][:, :], ALU.mult).then_inc(h_ok, 1)

            def down(i, c):
                if not (isinstance(i, int) and i == 0 and c < 2):
                    dve.wait_ge(est[c % 2], store_count(i, c))
                for k in (1, 3):
                    wait_count(dve, dn_mm, i, c, TP, TP - k - 1)
                    V.tensor_copy(eo[c % 2][:, k, :], pD[1][:, :]).then_inc(oo_ok, 1)

            pipelined(dve, transpose, up, down)
            with dve.Fori(0, NT // 2) as i:
                for u in range(2):
                    dve.wait_ge(acc_in[u], i * 16 + 16)
                    dve.wait_ge(cg[u], i * (16 * TOPK) + 16 * TOPK)
                    for k in range(TOPK):
                        w = comb_all[:, bass.ds(i * 2 + u, 1), k]
                        ins = V.scalar_tensor_tensor(out=tot[u][:, :], in0=rows_[u][:, k, :], scalar=w, in1=tot[u][:, :],
                                                     op0=ALU.mult, op1=ALU.add)
                        if k < TOPK - 1:
                            ins.then_inc(tchain, 1)
                            dve.wait_ge(tchain, i * (2 * (TOPK - 1)) + (u * (TOPK - 1) + k + 1))
                        else:
                            ins.then_inc(tot_ok, 1)

        @block.tensor
        def _(pe):
            mm, tr = nc.tensor.matmul, nc.tensor.transpose

            def transpose(i, c):
                u = c % 2
                pe.wait_ge(gath[u], (i + c // 2) * (16 * TP) + 16 * TP)
                wait_count(pe, xA_ok, i, c - 1)
                wait_count(pe, xB_ok, i, c - 1)
                for e in range(2):
                    for t in range(HT):
                        for k in range(KC):
                            last = tr(pT[e][:, k * CAP + t * P:k * CAP + (t + 1) * P], xg[u][:, HT * e + t, k * P:(k + 1) * P], ident[:, :])
                last.then_inc(T_mm, 1)

            def up(i, c):
                u = c % 2
                pe.wait_ge(wu_in[u], (i + c // 2) * 16 + 16)
                wait_count(pe, xA_ok, i, c)
                wait_count(pe, xB_ok, i, c)
                wait_count(pe, h_ok, i, c - 1)
                for j in range(2):
                    for k in range(KC):
                        for e in range(2):
                            last = mm(pU[HE * e:HE * (e + 1), j * CAP:(j + 1) * CAP], wu[u][:, e, k, j * HE:(j + 1) * HE],
                                      xT[u][:, e, k, :], start=(k == 0), stop=(k == KC - 1))
                last.then_inc(up_mm, 1)

            def down(i, c):
                u = c % 2
                pe.wait_ge(wd_in[u], (i + c // 2) * 16 + 16)
                wait_count(pe, h_ok, i, c)
                for n in range(TP):
                    e, t = n // HT, n % HT
                    wait_count(pe, (oe_ok, oo_ok)[n % 2], i, c, 2, 2 - n // 2)
                    mm(pD[n % 2][:, :], hT[u][HE * e:HE * (e + 1), t * P:(t + 1) * P], wd[u][HE * e:HE * (e + 1), :],
                       start=True, stop=True).then_inc(dn_mm, 1)

            pipelined(pe, transpose, up, down)


def store_count(i, c):
    return i * 16 + (c // 2) * 16


_SHAPE = (NB, S, D)


def rows(w):
    k = w.shape[0] // P
    return np.ascontiguousarray(w.reshape(k, P, w.shape[1]).transpose(1, 0, 2))


def kernel(x, ctx_2048, g_xattn, g_ffn, L0_xattn_Wh, L0_xattn_wg_w, L0_xattn_wo_w, L0_xattn_gn_gamma,
           L0_xattn_gn_beta, L0_ffn_W_up, L0_ffn_W_down, L0_ffn_W_gate, L0_ffn_W_expert, L1_ffn_w_gate,
           L1_ffn_w_shared_up, L1_ffn_w_shared_down, L1_ffn_w_up, L1_ffn_w_down):
    import concourse.bacc as bacc
    from concourse.bass_utils import run_bass_kernel_spmd as run

    a = lambda t: np.asarray(t)
    c = np.ascontiguousarray
    wh = a(L0_xattn_Wh)
    arrays = {
        "x": c(a(x)),
        "ctx": c(a(ctx_2048)),
        "ctxT": c(a(ctx_2048).reshape(NB, S, KC, P).transpose(0, 3, 2, 1).reshape(NB, P, KC * S)),
        "gates": c(np.concatenate([np.tile(a(g_xattn)[None, :], (P, 1)), np.tile(a(g_ffn)[None, :], (P, 1))], axis=1)),
        "mask": decay_mask(),
        "wh": c(wh.transpose(1, 0, 2)),
        "whT": c(wh.transpose(2, 0, 1)),
        "wg": rows(a(L0_xattn_wg_w)),
        "wo": rows(a(L0_xattn_wo_w)),
        "wupT": rows(a(L0_ffn_W_up).T),
        "wdnT": rows(a(L0_ffn_W_down).T),
        "wexp": rows(a(L0_ffn_W_expert)),
        "wg0": rows(a(L0_ffn_W_gate).T),
        "wg1": rows(a(L1_ffn_w_gate)),
        "wsu": rows(a(L1_ffn_w_shared_up)),
        "wsd": c(a(L1_ffn_w_shared_down)),
        "gamma": c(a(L0_xattn_gn_gamma).reshape(KC, P).T),
        "beta": c(a(L0_xattn_gn_beta).reshape(KC, P).T),
        "wu": c(a(L1_ffn_w_up).reshape(PAIRS, 2, KC, P, 2 * HE).transpose(0, 3, 1, 2, 4).reshape(PAIRS, P, 2 * KC * 2 * HE)),
        "wd": c(a(L1_ffn_w_down).reshape(PAIRS, 2 * HE, D)),
    }
    nc = bacc.Bacc("TRN2", target_bir_lowering=False, num_devices=1)
    io = {n: nc.dram_tensor("in_" + n, t.shape, F32, kind="ExternalInput").ap() for n, t in arrays.items()}
    out = nc.dram_tensor("out", _SHAPE, F32, kind="ExternalOutput").ap()
    build(nc, io, out)
    r = run(nc, [{"in_" + n: t for n, t in arrays.items()}], core_ids=[0])
    return r.results[0]["out"]
```

```python
from contextlib import ExitStack

import numpy as np

import concourse.bass as bass
from concourse import mybir

F32 = mybir.dt.float32
BF16 = mybir.dt.bfloat16
U32 = mybir.dt.uint32
ALU = mybir.AluOpType
ACT = mybir.ActivationFunctionType
AX = mybir.AxisListType

P = 128
NB, S, D = 8, 256, 512
T = S // P
NT = NB * T
KC = D // P
H0 = 4
HS = 8
HD = S // HS
G = 4
NG = HS // G
E0 = 8
E1, HE, TOPK, CAP = 64, 64, 6, 256
HT = CAP // P
SH = 128
GN_EPS, LN_EPS = 1e-3, 1e-5
SCALE1 = float(1.0 / np.sqrt(np.float32(HD)))
SKIP = 1.0e6
PAIRS = E1 // 2


def decay_mask():
    gam = (1.0 - 2.0 ** (-5.0 - np.arange(H0, dtype=np.float32))).astype(np.float32)
    idx = np.arange(S, dtype=np.float32)
    expo = idx[None, :] - idx[:, None]
    d = np.where(expo[None] <= 0, gam[:, None, None] ** np.minimum(expo, 0.0)[None], 0.0).astype(np.float32)
    dn = d / np.sqrt(d.sum(-1))[:, None, :]
    m = (dn / np.sqrt(np.float32(P))).transpose(2, 0, 1)
    return np.ascontiguousarray(m.reshape(T, P, H0, S).transpose(1, 0, 2, 3)).astype(np.float32)


def build(nc, io, out):
    dram = lambda name, shape, dt=F32: nc.dram_tensor(name, shape, dt, kind="Internal").ap()
    xnT_d = dram("xnT_d", (NB, P, KC * S))
    v_d = dram("v_d", (NB, P, T * D))
    kparts_d = dram("kparts_d", (3, NB * S, D), BF16)
    qparts_d = dram("qparts_d", (2, 3, S, D), BF16)
    xn4_d = dram("xn4_d", (NB * S, D))
    acc_d = dram("acc_d", (NT, P, D))
    ids_d = dram("ids_d", (P * P, 1), U32)
    eout_d = dram("eout_d", (E1 * CAP, D))

    with ExitStack() as outer:
        def sem(name):
            return outer.enter_context(nc.semaphore(name))

        def sb(name, shape, dt=F32, ctx=outer):
            return ctx.enter_context(nc.sbuf_tensor(name, shape, dt))

        ident = sb("ident", [P, P])
        ident16 = sb("ident16", [P, P], BF16)
        ones32 = sb("ones32", [P, HD])
        ones16 = sb("ones16", [P, P], BF16)
        before16 = sb("before16", [P, P], BF16)
        mhalf = sb("mhalf", [P, T])
        iota_e = sb("iota_e", [P, E1])
        tok_f = sb("tok_f", [P, 1])
        tg_x = sb("tg_x", [P, 2])
        tg_f = sb("tg_f", [P, 2])
        slots_all = sb("slots_all", [P, NT, TOPK], U32)
        comb_all = sb("comb_all", [P, NT, TOPK])

        with ExitStack() as mid:
            wg = sb("wg", [P, KC, D], ctx=mid)
            wo = sb("wo", [P, KC, D], ctx=mid)
            wupT = sb("wupT", [P, KC, D], ctx=mid)
            wdnT = sb("wdnT", [P, KC, D], ctx=mid)
            wexp = sb("wexp", [P, KC, D], ctx=mid)
            wg0 = sb("wg0", [P, KC, E0], ctx=mid)
            wg1 = sb("wg1", [P, KC, E1], ctx=mid)
            wsu = sb("wsu", [P, KC, 2 * SH], ctx=mid)
            wsd = sb("wsd", [P, D], ctx=mid)
            gamma = sb("gamma", [P, KC], ctx=mid)
            beta = sb("beta", [P, KC], ctx=mid)
            AT = sb("AT", [P, T, H0, S], ctx=mid)
            setup_and_scores(nc, io, outer, mid, locals())
            main_loop(nc, io, locals())
        experts(nc, io, out, locals())


def at(i, u, k=1, per=1):
    return i * (2 * per) + (u * per + k)


def hold(eng, s, n, passed):
    eng.wait_ge(s, n)
    eng.sem_inc(passed, 1)


def setup_and_scores(nc, io, outer, mid, v):
    ident, ident16, ones32, ones16, before16 = (v[n] for n in "ident ident16 ones32 ones16 before16".split())
    mhalf, iota_e, tok_f, tg_x, tg_f, AT = (v[n] for n in "mhalf iota_e tok_f tg_x tg_f AT".split())
    xnT_d, v_d, kparts_d, ids_d = (v[n] for n in "xnT_d v_d kparts_d ids_d".split())
    with ExitStack() as ctx:
        sem = lambda n: outer.enter_context(nc.semaphore(n))
        sb = lambda n, s, d=F32: ctx.enter_context(nc.sbuf_tensor(n, s, d))
        ps = lambda n, s, d=F32: ctx.enter_context(nc.psum_tensor(n, s, d))
        wh = sb("wh", [P, H0, P])
        whT = sb("whT", [P, H0, P])
        gram = sb("gram", [P, H0, P])
        mask = sb("mask", [P, T, H0, S])
        gates = sb("gates", [P, 4])
        zeros = sb("zeros", [P, D], BF16)
        zids = sb("zids", [P, P], U32)
        xin = [sb(f"a_x{u}", [P, T, D]) for u in range(2)]
        cin = [sb(f"a_c{u}", [P, T, D]) for u in range(2)]
        cT = [sb(f"a_cT{u}", [P, KC, S]) for u in range(2)]
        xn = [sb(f"a_xn{u}", [P, T, D]) for u in range(2)]
        xnT = [sb(f"a_xnT{u}", [P, KC, S]) for u in range(2)]
        qT = sb("a_qT", [P, H0, S])
        val = [sb(f"a_val{u}", [P, T, D]) for u in range(2)]
        parts = [sb(f"a_parts{u}", [P, 3, T, D], BF16) for u in range(2)]
        res = sb("a_res", [P, T, D])
        st = sb("a_st", [P, T, 6])
        mv = sb("a_mv", [P, T, 2])
        veps = sb("a_veps", [P, T])
        rstd = sb("a_rstd", [P, T])
        pX = ps("a_pX", [P, KC * S])
        pY = ps("a_pY", [P, KC * S])
        pS = [ps(f"a_pS{k}", [P, 512]) for k in range(3)]

        weights_in, gates_in, wh_in, mask_in = sem("weights_in"), sem("gates_in"), sem("wh_in"), sem("mask_in")
        ids_zeroed, pool_c, zero_set, tg_done = sem("ids_zeroed"), sem("pool_c"), sem("zero_set"), sem("tg_done")
        gram_mm, gram_ok = sem("gram_mm"), sem("gram_ok")
        x_in = [sem(f"ax_in{u}") for u in range(2)]
        c_in = [sem(f"ac_in{u}") for u in range(2)]
        cT_in = [sem(f"acT_in{u}") for u in range(2)]
        x_free, c_free, cT_free = sem("ax_free"), sem("ac_free"), sem("acT_free")
        chain, var_ok, rstd_ok, xn_ok = sem("a_chain"), sem("a_var"), sem("a_rstd_s"), sem("a_xn_s")
        xT_mm, xT_ok, q_mm, q_ok, v_mm, v_ok, s_mm = (sem("a_" + n) for n in "xT_mm xT_ok q_mm q_ok v_mm v_ok s_mm".split())
        k_chain, parts_ok = sem("a_kchain"), sem("a_parts_ok")
        stored = [sem(f"a_stored{u}") for u in range(2)]
        sc_chain, at_done, passed = sem("a_sc_chain"), sem("a_at_done"), sem("a_passed")
        block = ctx.enter_context(nc.Block())

        @block.sync
        def _(sp):
            def load(b, u):
                sp.dma_start(xin[u][:, :, :], io["x"][bass.ds(b, 1), :, :].rearrange("o (t p) d -> p (o t) d", p=P)).then_inc(x_in[u], 16)
                sp.dma_start(cin[u][:, :, :], io["ctx"][bass.ds(b, 1), :, :].rearrange("o (t p) d -> p (o t) d", p=P)).then_inc(c_in[u], 16)
                sp.dma_start(cT[u][:, :, :], io["ctxT"][bass.ds(b, 1), :, :].rearrange("o p (k s) -> (o p) k s", k=KC)).then_inc(cT_in[u], 16)

            def store(i, b, u):
                sp.wait_ge(xT_ok, at(i, u))
                sp.dma_start(xnT_d[bass.ds(b, 1), :, :].rearrange("o p (k s) -> (o p) k s", k=KC), xnT[u][:, :, :]).then_inc(stored[u], 16)
                sp.wait_ge(v_ok, at(i, u))
                sp.dma_start(v_d[bass.ds(b, 1), :, :].rearrange("o p (t d) -> (o p) t d", t=T), val[u][:, :, :]).then_inc(stored[u], 16)
                sp.wait_ge(parts_ok, at(i, u))
                for k in range(3):
                    sp.dma_start(kparts_d[k, bass.ds(b * S, S), :].rearrange("(t p) d -> p t d", p=P), parts[u][:, k, :, :]).then_inc(stored[u], 16)

            sp.dma_start(wh[:, :, :], io["wh"]).then_inc(wh_in, 16)
            sp.dma_start(whT[:, :, :], io["whT"]).then_inc(wh_in, 16)
            for u in range(2):
                load(u, u)
            sp.dma_start(gates[:, :], io["gates"]).then_inc(gates_in, 16)
            sp.dma_start(mask[:, :, :, :], io["mask"]).then_inc(mask_in, 16)
            sp.wait_ge(pool_c, 1)
            sp.dma_start(ids_d.rearrange("(p n) o -> p (n o)", p=P), zids[:, :]).then_inc(ids_zeroed, 16)
            for name in ("wg", "wo", "wupT", "wdnT", "wexp", "wg0", "wg1", "wsu", "wsd", "gamma", "beta"):
                t = v[name]
                ap = t[:, :, :] if len(t.shape) == 3 else t[:, :]
                sp.dma_start(ap, io[name]).then_inc(weights_in, 16)
            with sp.Fori(0, NB // 2 - 1) as i:
                for u in range(2):
                    store(i, i * 2 + u, u)
                    sp.wait_ge(stored[u], i * 80 + 80)
                    sp.wait_ge(x_free, at(i, u))
                    sp.wait_ge(c_free, at(i, u))
                    sp.wait_ge(cT_free, at(i, u))
                    load(i * 2 + (2 + u), u)
            last = NB // 2 - 1
            for u in range(2):
                store(last, 2 * last + u, u)
            for u in range(2):
                sp.wait_ge(stored[u], 5 * 16 * (NB // 2))
            sp.wait_ge(weights_in, 16 * 11)
            sp.wait_ge(ids_zeroed, 16)

        @block.gpsimd
        def _(pool):
            g = nc.gpsimd
            g.memset(zids[:, :], 0).then_inc(pool_c, 1)
            g.memset(ident[:, :], 0.0).then_inc(pool_c, 1)
            g.memset(ident16[:, :], 0.0).then_inc(pool_c, 1)
            g.memset(before16[:, :], 1.0).then_inc(pool_c, 1)
            g.memset(ones32[:, :], 1.0)
            g.memset(ones16[:, :], 1.0)
            g.memset(mhalf[:, :], -0.5).then_inc(pool_c, 1)
            g.iota(iota_e[:, :], pattern=[[1, E1]], base=0, channel_multiplier=0, allow_small_or_imprecise_dtypes=True)
            g.iota(tok_f[:, :], pattern=[[0, 1]], base=0, channel_multiplier=1, allow_small_or_imprecise_dtypes=True)
            pool.wait_ge(pool_c, 5)
            for m in (ident, ident16):
                g.affine_select(out=m[:, :], in_=m[:, :], compare_op=ALU.not_equal, fill=1.0, base=0,
                                pattern=[[-1, P]], channel_multiplier=1).then_inc(pool_c, 1)
            g.affine_select(out=before16[:, :], in_=before16[:, :], compare_op=ALU.is_gt, fill=0.0, base=0,
                            pattern=[[1, P]], channel_multiplier=-1).then_inc(pool_c, 1)
            with pool.Fori(0, NB // 2) as i:
                for u in range(2):
                    pool.wait_ge(var_ok, at(i, u))
                    g.tensor_tensor(rstd[:, :], veps[:, :], mhalf[:, :], ALU.pow).then_inc(rstd_ok, 1)
                    pool.wait_ge(k_chain, at(i, u, 1, 4))
                    g.tensor_tensor(res[:, :, :], cin[u][:, :, :], parts[u][:, 0, :, :], ALU.subtract).then_inc(k_chain, 1)
                    pool.wait_ge(k_chain, at(i, u, 3, 4))
                    g.tensor_tensor(parts[u][:, 2, :, :], res[:, :, :], parts[u][:, 1, :, :], ALU.subtract).then_inc(parts_ok, 1)
                    pool.wait_ge(parts_ok, at(i, u))
                    pool.sem_inc(k_chain, 1)
                    pool.sem_inc(c_free, 1)

        @block.scalar
        def _(act):
            act.preload_act_table(ACT.Exp)
            act.wait_ge(gates_in, 16)
            nc.scalar.activation(tg_x[:, :], gates[:, 0:2], ACT.Tanh).then_inc(tg_done, 1)
            nc.scalar.activation(tg_f[:, :], gates[:, 2:4], ACT.Tanh).then_inc(tg_done, 1)
            act.wait_ge(gram_mm, 1)
            nc.scalar.activation(gram[:, :, :], pX[:, 0:H0 * P].rearrange("p (h e) -> p h e", h=H0), ACT.Copy).then_inc(gram_ok, 1)
            with act.Fori(0, NB // 2) as i:
                for u in range(2):
                    act.wait_ge(xT_mm, at(i, u))
                    nc.scalar.activation(xnT[u][:, :, :], pX[:, :].rearrange("p (k s) -> p k s", k=KC), ACT.Copy).then_inc(xT_ok, 1)
                    act.wait_ge(q_mm, at(i, u))
                    nc.scalar.activation(qT[:, :, :], pX[:, :].rearrange("p (k s) -> p k s", k=KC), ACT.Copy).then_inc(q_ok, 1)
                    act.wait_ge(v_mm, at(i, u))
                    nc.scalar.activation(val[u][:, :, :], pY[:, :].rearrange("p (t d) -> p t d", t=T), ACT.Copy).then_inc(v_ok, 1)

        @block.vector
        def _(dve):
            n = [0]

            def link(ins, sem_, base):
                n[0] += 1
                ins.then_inc(sem_, 1)
                hold(dve, sem_, base + n[0], passed)

            nc.vector.memset(zeros[:, :], 0.0).then_inc(zero_set, 1)
            PER = 3
            with dve.Fori(0, NB // 2) as i:
                for u in range(2):
                    n[0] = u * PER
                    base = i * (2 * PER)
                    dve.wait_ge(x_in[u], i * 16 + 16)
                    for t in range(T):
                        last = nc.vector.bn_stats(st[:, t, :], xin[u][:, t, :])
                    link(last, chain, base)
                    for t in range(T):
                        last = nc.vector.bn_aggr(mv[:, t, :], st[:, t, :])
                    link(last, chain, base)
                    nc.vector.tensor_scalar(veps[:, :], mv[:, :, 1], LN_EPS, None, ALU.add).then_inc(var_ok, 1)
                    dve.wait_ge(c_in[u], i * 16 + 16)
                    nc.vector.tensor_copy(parts[u][:, 0, :, :], cin[u][:, :, :]).then_inc(k_chain, 1)
                    dve.wait_ge(rstd_ok, at(i, u))
                    for t in range(T):
                        last = nc.vector.tensor_scalar(xn[u][:, t, :], xin[u][:, t, :], mv[:, t, 0:1], rstd[:, t:t + 1], ALU.subtract, ALU.mult)
                    link(last, chain, base)
                    assert n[0] == (u + 1) * PER
                    dve.sem_inc(xn_ok, 1)
                    dve.sem_inc(x_free, 1)
                    dve.wait_ge(k_chain, at(i, u, 2, 4))
                    nc.vector.tensor_copy(parts[u][:, 1, :, :], res[:, :, :]).then_inc(k_chain, 1)
            dve.wait_ge(mask_in, 16)
            dve.wait_ge(s_mm, 1)
            k = 0
            for j in range(2):
                nc.vector.tensor_tensor(AT[:, 0, 2 * j:2 * j + 2, :], pS[j][:, :].rearrange("p (h s) -> p h s", h=2),
                                        mask[:, 0, 2 * j:2 * j + 2, :], ALU.mult).then_inc(sc_chain, 1)
            nc.vector.memset(AT[:, 1, :, 0:P], 1.0)
            nc.vector.tensor_tensor(AT[:, 1, :, P:S], pS[2][:, :].rearrange("p (h s) -> p h s", h=H0),
                                    mask[:, 1, :, P:S], ALU.mult).then_inc(sc_chain, 1)
            dve.wait_ge(sc_chain, 3)
            flat = lambda t: t[:, :, :, :].rearrange("p t h s -> p (t h s)")
            nc.vector.scalar_tensor_tensor(out=flat(mask), in0=flat(AT), scalar=-1.0, in1=flat(AT), op0=ALU.mult, op1=ALU.max).then_inc(at_done, 1)
            dve.wait_ge(at_done, 1)
            nc.vector.tensor_scalar(flat(AT), flat(mask), 1.0, None, ALU.max).then_inc(at_done, 1)
            dve.wait_ge(at_done, 2)

        @block.tensor
        def _(pe):
            mm = nc.tensor.matmul
            pe.wait_ge(wh_in, 32)
            for h in range(H0):
                last = mm(pX[:, h * P:(h + 1) * P], whT[:, h, :], whT[:, h, :], start=True, stop=True)
            last.then_inc(gram_mm, 1)
            pe.wait_ge(zero_set, 1)
            for k in range(3):
                mm(pS[k][:, :], zeros[:, 0:P], zeros[:, :], start=True, stop=False, skip_group_check=True)
            pe.wait_ge(pool_c, 8)
            pe.wait_ge(gram_ok, 1)
            with pe.Fori(0, NB // 2) as i:
                for u in range(2):
                    pe.wait_ge(xn_ok, at(i, u))
                    for t in range(T):
                        for k in range(KC):
                            last = nc.tensor.transpose(pX[:, k * S + t * P:k * S + (t + 1) * P], xn[u][:, t, k * P:(k + 1) * P], ident[:, :])
                    last.then_inc(xT_mm, 1)
                    pe.wait_ge(cT_in[u], i * 16 + 16)
                    if u:
                        pe.wait_ge(v_ok, at(i, 0))
                    for t in range(T):
                        for h in range(H0):
                            last = mm(pY[:, t * D + h * P:t * D + (h + 1) * P], cT[u][:, h, t * P:(t + 1) * P], wh[:, h, :], start=True, stop=True)
                    last.then_inc(v_mm, 1)
                    pe.wait_ge(xT_ok, at(i, u))
                    for h in range(H0):
                        last = mm(pX[:, h * S:(h + 1) * S], gram[:, h, :], xnT[u][:, h, :], start=True, stop=True)
                    last.then_inc(q_mm, 1)
                    pe.wait_ge(q_ok, at(i, u))
                    for h in range(H0):
                        mm(pS[h // 2][:, (h % 2) * S:(h % 2 + 1) * S], cT[u][:, h, 0:P], qT[:, h, :], start=False, stop=False, skip_group_check=True)
                        last = mm(pS[2][:, h * P:(h + 1) * P], cT[u][:, h, P:S], qT[:, h, P:S], start=False, stop=False, skip_group_check=True)
                    last.then_inc(cT_free, 1)
                    pe.wait_ge(v_ok, at(i, u))
            for k in range(3):
                last = mm(pS[k][:, :], zeros[:, 0:P], zeros[:, :], start=False, stop=True, skip_group_check=True)
            last.then_inc(s_mm, 1)


ORDER = """
F.out0 F.out1 F.gate0 F.gate1 R.stats F.gate2 T.S0 F.gate3 F.stats T.S1 R.norm R.turn F.norm T.S2 F.turn R.gates T.S3
F.affine R.up0 T.S4 R.up1 T.S5 F.x1a0 T.S6 F.x1a1 R.shared T.S7 F.x1b0 T.P0 T.S8 F.x1b1 T.M0 F.res1 T.S9 R.down0 R.down1 R.acc
T.S10 F.norm2 T.S11 R.sigmoid T.Q0a F.turn2 T.Q0b R.chosen F.gates T.S12 F.up0 F.best T.S13 F.up1 R.pos F.weight T.S14 F.up2 T.S15 F.up3 T.P1
T.Q1a T.V0a T.Q1b T.V0b T.M1 R.places F.expert0 T.Q2a T.V1a F.expert1 T.Q2b T.V1b F.down0 R.send0 R.send1 R.send2 R.send3 T.Q3a T.V2a F.down1 T.Q3b T.V2b
F.res2 T.Q4a T.V3a T.Q4b T.V3b T.A0 F.norm3 T.Q5a T.V4a T.Q5b T.V4b F.q1 F.q2 T.Q6a T.V5a T.Q6b T.V5b T.Q7a T.V6a T.Q7b T.V6b
T.V7a T.V7b T.A1
""".split()


HALF = {"a": (0, 1), "b": (2, 3)}


def ring_slots():
    slots = []
    for name in ORDER:
        stage = name[2:]
        if name[:3] == "T.S":
            slots += [(name, ("mx_ok", 2 * int(stage[1:]) + m + 1, KC * HS)) for m in range(2)]
        elif name[:3] == "T.M":
            slots.append((name, ("mrow_ok", int(stage[1:]) + 1, NG)))
        elif name[:3] == "T.Q":
            slots += [(name, ("exp_ok", G * int(stage[1]) + q + 1, KC * HS)) for q in HALF[stage[2]]]
        elif name == "R.gates":
            slots.append((name, ("eg_ok", 1, 1)))
        elif name == "R.pos":
            slots.append((name, ("pos_ok", 1, 1)))
    assert len(slots) % 2 == 0
    return slots


SLOTS = ring_slots()


def first_slot(name):
    return [s[0] for s in SLOTS].index(name)


def after(eng, s, i, c, k, per=1, unit=1):
    if isinstance(i, int):
        if (2 * i + c) * per + k > 0:
            eng.wait_ge(s, ((2 * i + c) * per + k) * unit)
    else:
        assert c * per + k > 0
        eng.wait_ge(s, i * (2 * per * unit) + (c * per + k) * unit)


def steps(eng, stages, peeled=0):
    def step(i, **streams):
        for name in ORDER:
            if name[0] in streams and name in stages:
                stages[name](i, streams[name[0]], streams)

    assert set(stages) <= set(ORDER)
    step(0, F=0)
    step(0, T=0, F=1)
    with eng.Fori(0, NB // 2 - 1 - peeled) as i:
        for u in range(2):
            step(i, R=u, T=u + 1, F=u + 2)
    for i in range(NB // 2 - 1 - peeled, NB // 2 - 1):
        for u in range(2):
            step(i, R=u, T=u + 1, F=u + 2)
    step(NB // 2 - 1, R=0, T=1)
    step(NB // 2 - 1, R=1)


def main_loop(nc, io, v):
    outer = v["outer"]
    with ExitStack() as ctx:
        sem = lambda n: outer.enter_context(nc.semaphore(n))
        sb = lambda n, s, d=F32: ctx.enter_context(nc.sbuf_tensor(n, s, d))
        ps = lambda n, s, d=F32: ctx.enter_context(nc.psum_tensor(n, s, d))
        ident, ident16, ones32, ones16, before16 = (v[n] for n in "ident ident16 ones32 ones16 before16".split())
        mhalf, iota_e, tok_f, tg_x, tg_f, AT = (v[n] for n in "mhalf iota_e tok_f tg_x tg_f AT".split())
        wg, wo, wupT, wdnT, wexp, wg0, wg1, wsu, wsd = (v[n] for n in "wg wo wupT wdnT wexp wg0 wg1 wsu wsd".split())
        gamma, beta, slots_all, comb_all = (v[n] for n in "gamma beta slots_all comb_all".split())
        xnT_d, v_d, kparts_d, qparts_d, xn4_d, acc_d, ids_d = (
            v[n] for n in "xnT_d v_d kparts_d qparts_d xn4_d acc_d ids_d".split())
        two = lambda name, shape, dt=F32: [sb(f"{name}{u}", shape, dt) for u in range(2)]

        xin = sb("b_x", [P, T, D])
        xnT = sb("b_xnT", [P, KC, S])
        val = sb("b_val", [P, T, D])
        cT = sb("b_cT", [P, KC, S])
        ka = two("b_ka", [P, HS, D], BF16)
        kb = sb("b_kb", [P, HS, D], BF16)
        qa = two("b_qa", [P, HS, D], BF16)
        qb = sb("b_qb", [P, HS, D], BF16)
        KB = 3 * HD + 3
        norm = sb("f_norm", [P, T, D])
        normT = sb("f_normT", [P, KC, S])
        hT = sb("f_hT", [P, KC, S])
        zT = sb("f_zT", [P, KC, S])
        tmp = zT[:, :, :].rearrange("p k s -> p (k s)").rearrange("p (t d) -> p t d", t=T)
        xs = two("f_xs", [P, T, D])
        qp = sb("f_qp", [P, 3, T, D], BF16)
        stF, mvF, vepsF, rstdF = sb("f_st", [P, T, 6]), sb("f_mv", [P, T, 2]), sb("f_veps", [P, T]), sb("f_rstd", [P, T])
        m8 = sb("f_m8", [P, T, 8])
        gap = sb("f_gap", [P, T, 1])
        egap = sb("f_egap", [P, T, 1])
        rw = sb("f_rw", [P, 3, T])
        probs = [sb(f"t_probs{k}", [P, G, D]) for k in range(2)]
        rsum = sb("t_rsum", [P, D])
        att = sb("t_att", [P, D])
        nmx = sb("t_nmx", [P, KC, G])
        nmr = sb("t_nmr", [P, 2, KC, G])
        nmp = sb("t_nmp", [P, KC, 3, G], BF16)
        mrow = sb("t_mrow", [3 * G, D], BF16)
        acc = sb("r_acc", [P, T, D])
        normR = sb("r_norm", [P, T, D])
        normRT = sb("r_normT", [P, KC, S])
        stR, mvR, vepsR, rstdR = sb("r_st", [P, T, 6]), sb("r_mv", [P, T, 2]), sb("r_veps", [P, T]), sb("r_rstd", [P, T])
        eg = sb("r_eg", [P, T, E1])
        score = sb("r_score", [P, T, E1])
        top = sb("r_top", [P, T, 8])
        topi = sb("r_topi", [P, T, 8], U32)
        topf = sb("r_topf", [P, T, TOPK])
        onehot = sb("r_onehot", [P, T, TOPK, E1], BF16)
        chosen = sb("r_chosen", [P, T, E1])
        chosen16 = sb("r_chosen16", [P, T, E1], BF16)
        cum = sb("r_cum", [P, E1])
        cum16 = sb("r_cum16", [P, T, E1], BF16)
        post = sb("r_post", [P, T, E1])
        ohp = sb("r_ohp", [P, T, TOPK, E1])
        pos = sb("r_pos", [P, T, TOPK])
        small = sb("r_small", [P, 6, T, TOPK])
        wsum = sb("r_wsum", [P, 2, T])
        addr = sb("r_addr", [P, T, TOPK], U32)
        tok = sb("r_tok", [P, T], U32)
        es = sb("r_es", [P, S])
        es2 = sb("r_es2", [P, S])
        shT = sb("r_shT", [P, S])

        pA = ps("f_pA", [P, 1024])
        pB = ps("f_pB", [P, 1024])
        ring = [ps(f"ring{k}", [P, 512]) for k in range(2)]
        pV = ps("t_pV", [P, 512])
        pZ = ps("t_pZ", [P, 512])
        a3 = lambda t: t[:, :].rearrange("p (k s) -> p k s", k=KC)
        t3 = lambda t: t[:, :].rearrange("p (t d) -> p t d", t=T)

        W = {}
        for name in ("gate_mm", "o_mm", "nT_mm", "x1_mm", "x2T_mm", "lg_mm", "up_mm", "ex_mm", "dn_mm",
                     "s_mm", "mT_mm", "st_mm", "pv_step", "x4T_mm", "gt_mm", "su_mm", "pos_mm", "sd_mm",
                     "f_chain", "t_chain", "r_chain", "f_var", "f_rstd_ok", "r_var", "r_rstd_ok",
                     "n_ok", "zT_ok", "x1_ok", "x2n_ok", "gap_ok", "x2_ok", "x3n_ok", "q_chain",
                     "mx_ok", "nmp_ok", "att_ok", "x3_ok", "x4n_ok", "m_ok", "pos_ok", "route_ok", "shT_ok", "acc_ok",
                     "yT_ok", "x2T_ok", "uT_ok", "egap_ok", "mrow_ok", "exp_ok", "x4T_ok", "eg_ok", "es_ok",
                     "kept_ok", "ones_ok", "cum_ok", "addr_free", "passed", "pool_passed",
                     "x_in", "xnT_in", "val_in", "cT_in", "ka_in0", "ka_in1", "kb_in", "qa_in", "qb_in",
                     "qst", "mld", "x4st", "accst", "scat"):
            W[name] = sem("b_" + name)
        block = ctx.enter_context(nc.Block())

        @block.sync
        def _(sp):
            def by_batch(i, c):
                return i * 2 + c

            def load_front(i, c, streams):
                b = by_batch(i, c)
                sp.dma_start(xnT[:, :, :], xnT_d[bass.ds(b, 1), :, :].rearrange("o p (k s) -> (o p) k s", k=KC)).then_inc(W["xnT_in"], 16)
                sp.dma_start(val[:, :, :], v_d[bass.ds(b, 1), :, :].rearrange("o p (t d) -> (o p) t d", t=T)).then_inc(W["val_in"], 16)
                sp.dma_start(xin[:, :, :], io["x"][bass.ds(b, 1), :, :].rearrange("o (t p) d -> p (o t) d", p=P)).then_inc(W["x_in"], 16)

            def stack(dst, src, parts, s):
                for blk, part in enumerate(parts):
                    sp.dma_start(dst[HD * blk:HD * (blk + 1), :, :], src(part).rearrange("(h r) d -> r h d", r=HD)).then_inc(s, 16)

            keys = lambda i, c: (lambda part: kparts_d[part, bass.ds(by_batch(i, c) * S, S), :])
            queries = lambda c: (lambda part: qparts_d[c % 2, part, :, :])

            def load_ka(i, c):
                stack(ka[c % 2], keys(i, c), (0, 1, 0, 1), W[f"ka_in{c % 2}"])

            def load_back(i, c):
                stack(kb, keys(i, c), (0, 2, 2), W["kb_in"])
                sp.dma_start(cT[:, :, :], io["ctxT"][bass.ds(by_batch(i, c), 1), :, :].rearrange("o p (k s) -> (o p) k s", k=KC)).then_inc(W["cT_in"], 16)

            def f_next(i, c, streams):
                after(sp, W["x1_ok"], i, c, 1)
                if not (isinstance(i, int) and 2 * i + c == NB - 1):
                    load_front(i, c + 1, streams)

            def f_queries(i, c, streams):
                after(sp, W["q_chain"], i, c, 4, 4)
                for k in range(3):
                    sp.dma_start(qparts_d[c % 2, k, :, :].rearrange("(t p) d -> p t d", p=P), qp[:, k, :, :]).then_inc(W["qst"], 16)
                after(sp, W["qst"], i, c, 3, 3, 16)
                stack(qa[c % 2], queries(c), (0, 0, 1, 1), W["qa_in"])
                if "T" not in streams:
                    stack(qb, queries(c), (2, 0, 1), W["qb_in"])

            def t_rows(g):
                def stage(i, c, streams):
                    after(sp, W["mrow_ok"], i, c, g + 1, NG)
                    for k in range(3):
                        sp.dma_start(qb[3 * HD + k:3 * HD + k + 1, G * g:G * (g + 1), :], mrow[G * k:G * (k + 1), :]).then_inc(W["mld"], 16)
                return stage

            def t_next(i, c, streams):
                after(sp, W["pv_step"], i, c, NG * KC, NG * KC)
                if "F" in streams:
                    stack(qb, queries(c + 1), (2, 0, 1), W["qb_in"])
                    load_back(i, c + 1)
                    if isinstance(i, int) and 2 * i + c + 2 >= NB:
                        return
                    load_ka(i, c + 2)

            def r_rows(i, c, streams):
                after(sp, W["x4n_ok"], i, c, 1)
                sp.dma_start(xn4_d[bass.ds(by_batch(i, c) * S, S), :].rearrange("(t p) d -> p t d", p=P), normR[:, :, :]).then_inc(W["x4st"], 16)

            def r_acc(i, c, streams):
                after(sp, W["acc_ok"], i, c, 1)
                sp.dma_start(acc_d[bass.ds(by_batch(i, c) * T, T), :, :].rearrange("t p d -> p t d"), acc[:, :, :]).then_inc(W["accst"], 16)

            load_front(0, 0, None)
            sp.sem_inc(W["x4st"], 16)
            sp.wait_ge(W["ones_ok"], 1)
            load_back(0, 0)
            load_ka(0, 0)
            load_ka(0, 1)
            steps(sp, {"R.norm": r_rows, "T.M0": t_rows(0), "R.acc": r_acc, "F.res1": f_next, "T.M1": t_rows(1),
                       "F.q2": f_queries, "T.V7b": t_next}, peeled=1)
            sp.wait_ge(W["x4st"], 16 * NB + 16)
            sp.wait_ge(W["accst"], 16 * NB)
            sp.wait_ge(W["qst"], 48 * NB)

        @block.gpsimd
        def _(pool):
            g_ = nc.gpsimd
            last = g_.memset(kb[3 * HD:3 * HD + 3, :, :], 1.0)
            last.then_inc(W["ones_ok"], 1)
            pool.wait_ge(W["ones_ok"], 1)
            g_.memset(cum[:, :], 0.0).then_inc(W["cum_ok"], 1)
            pool.sem_inc(W["addr_free"], 1)

            def f_rsqrt(k):
                def stage(i, c, streams):
                    after(pool, W["f_var"], i, c, k, 3)
                    g_.tensor_tensor(rstdF[:, :], vepsF[:, :], mhalf[:, :], ALU.pow).then_inc(W["f_rstd_ok"], 1)
                return stage

            def r_rsqrt(i, c, streams):
                after(pool, W["r_var"], i, c, 1)
                g_.tensor_tensor(rstdR[:, :], vepsR[:, :], mhalf[:, :], ALU.pow).then_inc(W["r_rstd_ok"], 1)

            def q_rest(i, c, streams):
                after(pool, W["q_chain"], i, c, 1, 4)
                g_.tensor_tensor(tmp, norm[:, :, :], qp[:, 0, :, :], ALU.subtract).then_inc(W["q_chain"], 1)

            def q_last(i, c, streams):
                after(pool, W["q_chain"], i, c, 3, 4)
                g_.tensor_tensor(qp[:, 2, :, :], tmp, qp[:, 1, :, :], ALU.subtract).then_inc(W["q_chain"], 1)

            def add(g):
                def stage(i, c, streams):
                    after(pool, W["att_ok"], i, c, g + 1, NG)
                    after(pool, W["accst"], i, c, 0, 1, 16)
                    g_.tensor_tensor(acc[:, g, :], xs[c % 2][:, g, :], att[:, :], ALU.add).then_inc(W["x3_ok"], 1)
                return stage

            def send(n):
                def stage(i, c, streams):
                    if n == 0:
                        after(pool, W["route_ok"], i, c, 1)
                        pool.sem_inc(W["pool_passed"], 1)
                    per = T * TOPK // 4
                    for j in range(n * per, (n + 1) * per):
                        t, k = j // TOPK, j % TOPK
                        g_.indirect_dma_start(out=ids_d, out_offset=bass.IndirectOffsetOnAxis(ap=addr[:, t, k:k + 1], axis=0),
                                              in_=tok[:, t:t + 1], in_offset=None, bounds_check=P * P - 1,
                                              oob_is_err=False).then_inc(W["scat"], 16)
                    if n == 3:
                        after(pool, W["scat"], i, c, T * TOPK, T * TOPK, 16)
                        pool.sem_inc(W["addr_free"], 1)
                return stage

            steps(pool, {"R.stats": r_rsqrt, "F.stats": f_rsqrt(1), "F.res1": f_rsqrt(2), "F.res2": f_rsqrt(3), "F.q1": q_rest,
                         "F.q2": q_last, "T.A0": add(0), "T.A1": add(1),
                         "R.send0": send(0), "R.send1": send(1), "R.send2": send(2), "R.send3": send(3)})

        @block.scalar
        def _(act):
            A = nc.scalar.activation
            act.preload_act_table(ACT.Exp)

            def affine(i, c, streams):
                after(act, W["nT_mm"], i, c, 1)
                for k in range(KC):
                    last = A(hT[:, k, :], a3(pB)[:, k, :], ACT.Identity, bias=beta[:, k:k + 1], scale=gamma[:, k:k + 1])
                last.then_inc(W["yT_ok"], 1)

            def turn2(i, c, streams):
                after(act, W["x2T_mm"], i, c, 1)
                A(normT[:, :, :], a3(pB), ACT.Copy).then_inc(W["x2T_ok"], 1)

            def weight(i, c, streams):
                after(act, W["gap_ok"], i, c, 1)
                A(egap[:, :, :], gap[:, :, :], ACT.Exp).then_inc(W["egap_ok"], 1)
                after(act, W["up_mm"], i, c, 1)
                A(hT[:, :, :], a3(pA), ACT.Relu).then_inc(W["uT_ok"], 1)

            def q1(i, c, streams):
                after(act, W["x3n_ok"], i, c, 1)
                A(qp[:, 0, :, :], norm[:, :, :], ACT.Copy).then_inc(W["q_chain"], 1)

            def q2(i, c, streams):
                after(act, W["q_chain"], i, c, 2, 4)
                A(qp[:, 1, :, :], tmp, ACT.Copy).then_inc(W["q_chain"], 1)

            def rows_of(g):
                def stage(i, c, streams):
                    slot = first_slot(f"T.M{g}") % 2
                    after(act, W["mT_mm"], i, c, g + 1, NG)
                    after(act, W["mld"], i, c, g * 3, NG * 3, 16)
                    A(mrow[:, :], ring[slot][:, :].bitcast(BF16)[0:3 * G, 0:D], ACT.Copy).then_inc(W["mrow_ok"], 1)
                return stage

            def exps(s, half):
                def stage(i, c, streams):
                    if half == "a":
                        after(act, W["pv_step"], i, c, s - 1, NG * KC)
                    for j, q in enumerate(HALF[half]):
                        after(act, W["st_mm"], i, c, G * s + q + 1, KC * HS)
                        A(probs[s % 2][:, q, :], ring[(first_slot(f"T.Q{s}{half}") + j) % 2][:, :], ACT.Exp, scale=SCALE1).then_inc(W["exp_ok"], 1)
                return stage

            def keep(g):
                def stage(i, c, streams):
                    after(act, W["pv_step"], i, c, KC * (g + 1), NG * KC)
                    after(act, W["x3_ok"], i, c, g, NG)
                    A(rsum[:, :], pZ[:, :], ACT.Copy)
                    A(att[:, :], pV[:, :], ACT.Copy).then_inc(W["kept_ok"], 1)
                return stage

            def turn4(i, c, streams):
                after(act, W["x4T_mm"], i, c, 1)
                A(normRT[:, 0:2, :], pV[:, :].rearrange("p (k s) -> p k s", k=2), ACT.Copy)
                A(normRT[:, 2:4, :], pZ[:, :].rearrange("p (k s) -> p k s", k=2), ACT.Copy).then_inc(W["x4T_ok"], 1)

            def gates(i, c, streams):
                after(act, W["gt_mm"], i, c, 1)
                A(eg[:, :, :], ring[first_slot("R.gates") % 2][:, 0:T * E1].rearrange("p (t e) -> p t e", t=T), ACT.Exp, scale=-1.0).then_inc(W["eg_ok"], 1)

            def shared(i, c, streams):
                after(act, W["su_mm"], i, c, 1)
                A(es[:, :], pZ[:, S:2 * S], ACT.Exp, scale=-1.0).then_inc(W["es_ok"], 1)

            stages = {"F.affine": affine, "F.turn2": turn2, "F.weight": weight, "F.q1": q1, "F.q2": q2,
                      "T.M0": rows_of(0), "T.M1": rows_of(1), "R.turn": turn4, "R.gates": gates,
                      "R.up1": shared, "T.A0": keep(0), "T.A1": keep(1)}
            for s in range(NG * KC):
                for half in "ab":
                    stages[f"T.Q{s}{half}"] = exps(s, half)
            steps(act, stages)

        @block.vector
        def _(dve):
            V = nc.vector
            done = {"F": 0, "T": 0, "R": 0}
            PER = {"F": 15, "T": 10, "R": 28}

            def link(stream, ins, i, c, alone=False):
                s = W[stream.lower() + "_chain"]
                done[stream] += 1
                ins.then_inc(s, 1)
                after(dve, s, i, c, done[stream], PER[stream])
                if alone:
                    dve.sem_inc(W["passed"], 1)

            def opens(stream):
                done[stream] = 0

            def closes(stream):
                assert done[stream] == PER[stream], (stream, done[stream])

            def stats(stream, i, c, src, eps, st, mv, veps, ok):
                for t in range(T):
                    last = V.bn_stats(st[:, t, :], src(t))
                link(stream, last, i, c, alone=True)
                for t in range(T):
                    last = V.bn_aggr(mv[:, t, :], st[:, t, :])
                link(stream, last, i, c)
                V.tensor_scalar(veps[:, :], mv[:, :, 1], eps, None, ALU.add).then_inc(W[ok], 1)

            def f_stats(i, c, streams):
                opens("F")
                after(dve, W["o_mm"], i, c, 1)
                stats("F", i, c, lambda t: pB[:, t * D:(t + 1) * D], GN_EPS, stF, mvF, vepsF, "f_var")

            def f_norm(k, src, ok):
                def stage(i, c, streams):
                    after(dve, W["f_rstd_ok"], i, c, k, 3)
                    after(dve, W["q_chain"], i, c, 0, 4)
                    for t in range(T):
                        last = V.tensor_scalar(norm[:, t, :], src(c, t), mvF[:, t, 0:1], rstdF[:, t:t + 1], ALU.subtract, ALU.mult)
                    last.then_inc(W[ok], 1)
                return stage

            def f_affine(i, c, streams):
                after(dve, W["yT_ok"], i, c, 1)
                after(dve, W["gate_mm"], i, c, 1)
                V.scalar_tensor_tensor(out=zT[:, :, :], in0=a3(pA), scalar=0.0, in1=hT[:, :, :],
                                       op0=ALU.max, op1=ALU.mult).then_inc(W["zT_ok"], 1)

            def f_res1(i, c, streams):
                after(dve, W["x1_mm"], i, c, 1)
                after(dve, W["x_in"], i, c, 1, 1, 16)
                x = xs[c % 2]
                link("F", V.scalar_tensor_tensor(out=x[:, :, :], in0=t3(pA), scalar=tg_x[:, 0:1], in1=xin[:, :, :],
                                                 op0=ALU.mult, op1=ALU.add), i, c)
                dve.sem_inc(W["x1_ok"], 1)
                stats("F", i, c, lambda t: x[:, t, :], LN_EPS, stF, mvF, vepsF, "f_var")

            def f_best(i, c, streams):
                after(dve, W["lg_mm"], i, c, 1)
                dve.sem_inc(W["passed"], 1)
                for t in range(T):
                    last = V.max(m8[:, t, :], pB[:, t * E0:(t + 1) * E0])
                link("F", last, i, c)
                V.tensor_tensor(gap[:, :, :], m8[:, :, 1:2], m8[:, :, 0:1], ALU.subtract).then_inc(W["gap_ok"], 1)

            def f_weight(i, c, streams):
                after(dve, W["egap_ok"], i, c, 1)
                e_ = egap[:, :, 0]
                link("F", V.tensor_scalar(rw[:, 0, :], e_, 1.0, None, ALU.add), i, c)
                link("F", V.reciprocal(rw[:, 1, :], rw[:, 0, :]), i, c)
                link("F", V.tensor_tensor(rw[:, 2, :], rw[:, 1, :], e_, ALU.mult), i, c)
                link("F", V.tensor_tensor(rw[:, 0, :], rw[:, 1, :], rw[:, 2, :], ALU.add), i, c)
                link("F", V.tensor_scalar(rw[:, 2, :], rw[:, 0, :], tg_f[:, 0:1], None, ALU.mult), i, c)

            def f_res2(i, c, streams):
                x = xs[c % 2]
                after(dve, W["ex_mm"], i, c, 1)
                for t in range(T):
                    last = V.scalar_tensor_tensor(out=x[:, t, :], in0=pB[:, t * D:(t + 1) * D], scalar=rw[:, 2, t:t + 1],
                                                  in1=x[:, t, :], op0=ALU.mult, op1=ALU.add)
                link("F", last, i, c)
                after(dve, W["dn_mm"], i, c, 1)
                link("F", V.scalar_tensor_tensor(out=x[:, :, :], in0=t3(pA), scalar=tg_f[:, 0:1], in1=x[:, :, :],
                                                 op0=ALU.mult, op1=ALU.add), i, c)
                dve.sem_inc(W["x2_ok"], 1)
                stats("F", i, c, lambda t: x[:, t, :], LN_EPS, stF, mvF, vepsF, "f_var")
                closes("F")

            def maxima(n):
                def stage(i, c, streams):
                    for r in range(2):
                        h, m = (2 * n + r) // KC, (2 * n + r) % KC
                        after(dve, W["s_mm"], i, c, 2 * n + r + 1, KC * HS)
                        if h == G and m == 0:
                            after(dve, W["t_chain"], i, c, 4, PER["T"])
                            after(dve, W["nmp_ok"], i, c, 1, NG)
                        V.tensor_reduce(nmx[:, m, h % G:h % G + 1], ring[(first_slot(f"T.S{n}") + r) % 2][:, :],
                                        axis=AX.X, op=ALU.max, negate=True).then_inc(W["mx_ok"], 1)
                return stage

            def parts(g):
                def stage(i, c, streams):
                    if g == 0:
                        opens("T")
                    after(dve, W["mx_ok"], i, c, KC * G * (g + 1), KC * HS)
                    after(dve, W["mT_mm"], i, c, g, NG)
                    link("T", V.tensor_copy(nmp[:, :, 0, :], nmx[:, :, :]), i, c)
                    link("T", V.tensor_tensor(nmr[:, 0, :, :], nmx[:, :, :], nmp[:, :, 0, :], ALU.subtract), i, c)
                    link("T", V.tensor_copy(nmp[:, :, 1, :], nmr[:, 0, :, :]), i, c)
                    link("T", V.tensor_tensor(nmr[:, 1, :, :], nmr[:, 0, :, :], nmp[:, :, 1, :], ALU.subtract), i, c)
                    V.tensor_copy(nmp[:, :, 2, :], nmr[:, 1, :, :]).then_inc(W["nmp_ok"], 1)
                return stage

            def attended(g):
                def stage(i, c, streams):
                    after(dve, W["kept_ok"], i, c, g + 1, NG)
                    link("T", V.reciprocal(rsum[:, :], rsum[:, :]), i, c)
                    V.scalar_tensor_tensor(out=att[:, :], in0=att[:, :], scalar=tg_x[:, 1:2], in1=rsum[:, :],
                                           op0=ALU.mult, op1=ALU.mult).then_inc(W["att_ok"], 1)
                    if g:
                        closes("T")
                return stage

            def r_stats(i, c, streams):
                opens("R")
                after(dve, W["x3_ok"], i, c, NG, NG)
                stats("R", i, c, lambda t: acc[:, t, :], LN_EPS, stR, mvR, vepsR, "r_var")

            def r_norm(i, c, streams):
                after(dve, W["r_rstd_ok"], i, c, 1)
                after(dve, W["x4st"], i, c, 1, 1, 16)
                for t in range(T):
                    last = V.tensor_scalar(normR[:, t, :], acc[:, t, :], mvR[:, t, 0:1], rstdR[:, t:t + 1], ALU.subtract, ALU.mult)
                last.then_inc(W["x4n_ok"], 1)

            def r_shared(i, c, streams):
                after(dve, W["es_ok"], i, c, 1)
                link("R", V.tensor_scalar(es[:, :], es[:, :], 1.0, None, ALU.add), i, c)
                link("R", V.reciprocal(es2[:, :], es[:, :]), i, c)
                link("R", V.tensor_tensor(es[:, :], pZ[:, S:2 * S], es2[:, :], ALU.mult), i, c)
                V.tensor_tensor(shT[:, :], pZ[:, 0:S], es[:, :], ALU.mult).then_inc(W["shT_ok"], 1)

            def r_acc(i, c, streams):
                after(dve, W["sd_mm"], i, c, 1)
                for t, p in enumerate((pV, pZ)):
                    last = V.scalar_tensor_tensor(out=acc[:, t, :], in0=p[:, :], scalar=tg_f[:, 1:2], in1=acc[:, t, :],
                                                  op0=ALU.mult, op1=ALU.add)
                last.then_inc(W["acc_ok"], 1)

            def r_sigmoid(i, c, streams):
                after(dve, W["eg_ok"], i, c, 1)
                link("R", V.tensor_scalar(eg[:, :, :], eg[:, :, :], 1.0, None, ALU.add), i, c)
                link("R", V.reciprocal(score[:, :, :], eg[:, :, :]), i, c, alone=True)
                for t in range(T):
                    last = V.max(top[:, t, :], score[:, t, :])
                link("R", last, i, c, alone=True)
                for t in range(T):
                    last = V.max_index(topi[:, t, :], top[:, t, :], score[:, t, :])
                link("R", last, i, c)
                link("R", V.tensor_copy(topf[:, :, :], topi[:, :, 0:TOPK]), i, c)

            def r_chosen(i, c, streams):
                for t in range(T):
                    last = V.tensor_tensor(onehot[:, t, :, :], iota_e[:, :].unsqueeze(1).broadcast_to([P, TOPK, E1]),
                                           topf[:, t, :].unsqueeze(2).broadcast_to([P, TOPK, E1]), ALU.is_equal)
                link("R", last, i, c)
                link("R", V.tensor_reduce(chosen[:, :, :], onehot[:, :, :, :].rearrange("p t k e -> p t e k"), axis=AX.X, op=ALU.add), i, c)
                V.tensor_copy(chosen16[:, :, :], chosen[:, :, :])
                if isinstance(i, int) or c == 0:
                    dve.wait_ge(W["cum_ok"], 1)
                for t in range(T):
                    V.tensor_copy(cum16[:, t, :], cum[:, :])
                    link("R", V.tensor_tensor(cum[:, :], cum[:, :], chosen[:, t, :], ALU.add), i, c)
                dve.sem_inc(W["m_ok"], 1)
                link("R", V.tensor_reduce(wsum[:, 0, :], top[:, :, 0:TOPK], axis=AX.X, op=ALU.add), i, c)
                link("R", V.reciprocal(wsum[:, 1, :], wsum[:, 0, :]), i, c)

            def r_pos(i, c, streams):
                after(dve, W["pos_mm"], i, c, 1)
                link("R", V.tensor_copy(post[:, :, :], ring[first_slot("R.pos") % 2][:, 0:T * E1].rearrange("p (t e) -> p t e", t=T)), i, c)
                dve.sem_inc(W["pos_ok"], 1)

            def r_places(i, c, streams):
                for t in range(T):
                    last = V.tensor_tensor(ohp[:, t, :, :], onehot[:, t, :, :],
                                           post[:, t, :].unsqueeze(1).broadcast_to([P, TOPK, E1]), ALU.mult)
                link("R", last, i, c)
                link("R", V.tensor_reduce(pos[:, :, :], ohp[:, :, :, :], axis=AX.X, op=ALU.add), i, c)
                fits, high, a_, b_, c_, d_ = (small[:, k, :, :] for k in range(6))
                V.tensor_scalar(fits, pos[:, :, :], float(CAP), None, ALU.is_lt)
                V.tensor_scalar(high, pos[:, :, :], float(P), None, ALU.is_ge)
                V.tensor_scalar(a_, topf[:, :, :], 2.0, None, ALU.mult)
                link("R", V.tensor_scalar(b_, pos[:, :, :], float(CAP - 1), None, ALU.min), i, c)
                V.scalar_tensor_tensor(out=slots_all[:, bass.ds(i * (2 * T) + c * T, T), :], in0=topf[:, :, :], scalar=float(CAP),
                                       in1=b_, op0=ALU.mult, op1=ALU.add)
                link("R", V.scalar_tensor_tensor(out=c_, in0=pos[:, :, :], scalar=float(P), in1=a_, op0=ALU.mult, op1=ALU.add), i, c)
                link("R", V.scalar_tensor_tensor(out=d_, in0=high, scalar=-float(P * P - 1), in1=c_, op0=ALU.mult, op1=ALU.add), i, c)
                link("R", V.tensor_scalar(a_, fits, -SKIP, SKIP, ALU.mult, ALU.add), i, c)
                link("R", V.tensor_tensor(b_, fits, top[:, :, 0:TOPK], ALU.mult), i, c)
                for t in range(T):
                    V.tensor_scalar(comb_all[:, bass.ds(i * (2 * T) + (c * T + t), 1), :].rearrange("p o k -> p (o k)"),
                                    b_[:, t, :], wsum[:, 1, t:t + 1], tg_f[:, 1:2], ALU.mult, ALU.mult)
                after(dve, W["addr_free"], i, c, 1)
                V.tensor_tensor(addr[:, :, :], d_, a_, ALU.add)
                for t in range(T):
                    link("R", V.tensor_copy(tok[:, t:t + 1], tok_f[:, :]), i, c)
                    link("R", V.tensor_scalar(tok_f[:, :], tok_f[:, :], float(P), None, ALU.add), i, c)
                dve.sem_inc(W["route_ok"], 1)
                closes("R")

            stages = {"F.stats": f_stats, "F.affine": f_affine, "F.res1": f_res1, "F.best": f_best, "F.weight": f_weight,
                      "F.res2": f_res2,
                      "F.norm": f_norm(1, lambda c, t: pB[:, t * D:(t + 1) * D], "n_ok"),
                      "F.norm2": f_norm(2, lambda c, t: xs[c % 2][:, t, :], "x2n_ok"),
                      "F.norm3": f_norm(3, lambda c, t: xs[c % 2][:, t, :], "x3n_ok"),
                      "T.P0": parts(0), "T.P1": parts(1), "T.A0": attended(0), "T.A1": attended(1),
                      "R.stats": r_stats, "R.norm": r_norm, "R.shared": r_shared, "R.acc": r_acc, "R.sigmoid": r_sigmoid,
                      "R.chosen": r_chosen, "R.pos": r_pos, "R.places": r_places}
            for n in range(KC * HS // 2):
                stages[f"T.S{n}"] = maxima(n)
            steps(dve, stages)

        @block.tensor
        def _(pe):
            mm, tr = nc.tensor.matmul, nc.tensor.transpose

            def transposes(dst, src):
                for k in range(KC):
                    for t in range(T):
                        last = tr(dst(k)[:, t * P:(t + 1) * P], src[:, t, k * P:(k + 1) * P], ident[:, :])
                return last

            def by_rows(dst, lhs, w, tiles=range(T), ks=range(KC), k_all=KC):
                for t in tiles:
                    for k in ks:
                        last = mm(dst(t), lhs(k)[:, t * P:(t + 1) * P], w(k), start=(k == 0), stop=(k == k_all - 1))
                return last

            def by_features(dst, w, rhs, o):
                for k in range(KC):
                    last = mm(dst[:, o * S:(o + 1) * S], w[:, k, o * P:(o + 1) * P], rhs[:, k, :], start=(k == 0), stop=(k == KC - 1))
                return last

            tiles = lambda p, n=D: (lambda t: p[:, t * n:(t + 1) * n])
            chunks = lambda p: (lambda k: p[:, k * S:(k + 1) * S])

            def slot(r, i, streams):
                q = r - 2
                while q >= 0 and SLOTS[q][0][0] not in streams:
                    q -= 2
                if q >= 0:
                    name, (s, k, per) = SLOTS[q]
                    after(pe, W[s], i, streams[name[0]], k, per)
                return ring[r % 2]

            def f_gate(o):
                def stage(i, c, streams):
                    if o == 0:
                        after(pe, W["x2_ok"], i, c, 0)
                        after(pe, W["xnT_in"], i, c, 1, 1, 16)
                    last = by_features(pA, wg, xnT, o)
                    if o == KC - 1:
                        last.then_inc(W["gate_mm"], 1)
                return stage

            def f_out(s):
                def stage(i, c, streams):
                    if s == 0:
                        after(pe, W["x2_ok"], i, c, 0)
                        after(pe, W["val_in"], i, c, 1, 1, 16)
                    for h in range(H0):
                        for t in range(T):
                            last = mm(pB[:, s * D + h * P:s * D + (h + 1) * P], AT[:, t, h, s * P:(s + 1) * P],
                                      val[:, t, h * P:(h + 1) * P], start=(t == 0), stop=(t == T - 1))
                    if s == T - 1:
                        last.then_inc(W["o_mm"], 1)
                return stage

            def f_turn(i, c, streams):
                after(pe, W["n_ok"], i, c, 1)
                transposes(chunks(pB), norm).then_inc(W["nT_mm"], 1)

            def f_x1(t, half):
                def stage(i, c, streams):
                    if t == 0 and half == 0:
                        after(pe, W["zT_ok"], i, c, 1)
                    last = by_rows(tiles(pA), lambda k: zT[:, k, :], lambda k: wo[:, k, :], [t], range(2 * half, 2 * half + 2))
                    if t == T - 1 and half == 1:
                        last.then_inc(W["x1_mm"], 1)
                return stage

            def f_turn2(i, c, streams):
                after(pe, W["x2n_ok"], i, c, 1)
                transposes(chunks(pB), norm).then_inc(W["x2T_mm"], 1)

            def f_gates(i, c, streams):
                after(pe, W["x2T_ok"], i, c, 1)
                by_rows(tiles(pB, E0), lambda k: normT[:, k, :], lambda k: wg0[:, k, :]).then_inc(W["lg_mm"], 1)

            def f_up(o):
                def stage(i, c, streams):
                    last = by_features(pA, wupT, normT, o)
                    if o == KC - 1:
                        last.then_inc(W["up_mm"], 1)
                return stage

            def f_expert(t):
                def stage(i, c, streams):
                    if t == 0:
                        after(pe, W["gap_ok"], i, c, 1)
                    last = by_rows(tiles(pB), lambda k: normT[:, k, :], lambda k: wexp[:, k, :], [t])
                    if t == T - 1:
                        last.then_inc(W["ex_mm"], 1)
                return stage

            def f_down(t):
                def stage(i, c, streams):
                    if t == 0:
                        after(pe, W["uT_ok"], i, c, 1)
                    last = by_rows(tiles(pA), lambda k: hT[:, k, :], lambda k: wdnT[:, k, :], [t])
                    if t == T - 1:
                        last.then_inc(W["dn_mm"], 1)
                return stage

            def scores(n):
                def stage(i, c, streams):
                    if n == 0:
                        pe.wait_ge(W[f"ka_in{c % 2}"], (i + c // 2) * 64 + 64)
                        after(pe, W["qa_in"], i, c, 4, 4, 16)
                    for r in range(2):
                        h, m = (2 * n + r) // KC, (2 * n + r) % KC
                        dst = slot(first_slot(f"T.S{n}") + r, i, streams)
                        mm(dst[:, :], qa[c % 2][:, h, m * P:(m + 1) * P], ka[c % 2][:, h, :], start=True, stop=True).then_inc(W["s_mm"], 1)
                return stage

            def rows_of(g):
                def stage(i, c, streams):
                    after(pe, W["nmp_ok"], i, c, g + 1, NG)
                    dst = slot(first_slot(f"T.M{g}"), i, streams)[:, :].bitcast(BF16)
                    for m in range(KC):
                        last = tr(dst[0:3 * G, m * P:(m + 1) * P], nmp[:, m, :, :].rearrange("p k h -> p (k h)"), ident16[:, :])
                    last.then_inc(W["mT_mm"], 1)
                return stage

            def shifted(s, half):
                def stage(i, c, streams):
                    g, n = s // KC, s % KC
                    if s == 0 and half == "a":
                        after(pe, W["kb_in"], i, c, 3, 3, 16)
                        after(pe, W["qb_in"], i, c, 3, 3, 16)
                    if n == 0 and half == "a":
                        after(pe, W["mld"], i, c, 3 * (g + 1), 3 * NG, 16)
                    for j, q in enumerate(HALF[half]):
                        h = g * G + q
                        dst = slot(first_slot(f"T.Q{s}{half}") + j, i, streams)
                        mm(dst[:, :], ka[c % 2][:, h, n * P:(n + 1) * P], qa[c % 2][:, h, :], start=True, stop=False)
                        mm(dst[:, :], kb[0:KB, h, n * P:(n + 1) * P], qb[0:KB, h, :], start=False, stop=True).then_inc(W["st_mm"], 1)
                return stage

            def weighted(s, half):
                def stage(i, c, streams):
                    g, n = s // KC, s % KC
                    if half == "a":
                        after(pe, W["exp_ok"], i, c, G * (s + 1), KC * HS)
                        if s == 0:
                            after(pe, W["cT_in"], i, c, 1, 1, 16)
                            after(pe, W["acc_ok"], i, c, 0)
                        elif n == 0:
                            after(pe, W["kept_ok"], i, c, 1, NG)
                    for q in range(G):
                        if half == "a":
                            r = (g * G + q) * HD
                            last = mm(pV[q * HD:(q + 1) * HD, :], cT[:, n, r:r + HD], probs[s % 2][:, q, :], start=(n == 0), stop=(n == KC - 1))
                        else:
                            last = mm(pZ[q * HD:(q + 1) * HD, :], ones32[:, :], probs[s % 2][:, q, :], start=(n == 0), stop=(n == KC - 1))
                    if half == "b":
                        last.then_inc(W["pv_step"], 1)
                return stage

            def r_turn(i, c, streams):
                after(pe, W["x4n_ok"], i, c, 1)
                transposes(lambda k: (pV, pZ)[k // 2][:, (k % 2) * S:(k % 2 + 1) * S], normR).then_inc(W["x4T_mm"], 1)

            def r_gates(i, c, streams):
                after(pe, W["x4T_ok"], i, c, 1)
                dst = slot(first_slot("R.gates"), i, streams)
                by_rows(tiles(dst, E1), lambda k: normRT[:, k, :], lambda k: wg1[:, k, :]).then_inc(W["gt_mm"], 1)

            def r_up(o):
                def stage(i, c, streams):
                    last = by_features(pZ, wsu, normRT, o)
                    if o == 1:
                        last.then_inc(W["su_mm"], 1)
                return stage

            def r_pos(i, c, streams):
                after(pe, W["m_ok"], i, c, 1)
                dst = slot(first_slot("R.pos"), i, streams)
                for t in range(T):
                    mm(dst[:, t * E1:(t + 1) * E1], before16[:, :], chosen16[:, t, :], start=True, stop=False)
                    last = mm(dst[:, t * E1:(t + 1) * E1], ones16[:, :], cum16[:, t, :], start=False, stop=True)
                last.then_inc(W["pos_mm"], 1)

            def r_down(t):
                def stage(i, c, streams):
                    if t == 0:
                        after(pe, W["shT_ok"], i, c, 1)
                    last = by_rows(lambda t: (pV, pZ)[t][:, :], lambda k: shT[:, :], lambda k: wsd[:, :], [t], [0], 1)
                    if t == T - 1:
                        last.then_inc(W["sd_mm"], 1)
                return stage

            stages = {"F.turn": f_turn, "F.turn2": f_turn2, "F.gates": f_gates, "T.M0": rows_of(0), "T.M1": rows_of(1),
                      "R.turn": r_turn, "R.gates": r_gates, "R.pos": r_pos}
            for t in range(T):
                stages[f"F.out{t}"] = f_out(t)
                stages[f"F.expert{t}"] = f_expert(t)
                stages[f"F.down{t}"] = f_down(t)
                stages[f"R.down{t}"] = r_down(t)
                stages[f"R.up{t}"] = r_up(t)
                for half in range(2):
                    stages[f"F.x1{'ab'[t]}{half}"] = f_x1(t, half)
            for o in range(KC):
                stages[f"F.gate{o}"] = f_gate(o)
                stages[f"F.up{o}"] = f_up(o)
            for n in range(KC * HS // 2):
                stages[f"T.S{n}"] = scores(n)
            for s in range(NG * KC):
                for half in "ab":
                    stages[f"T.Q{s}{half}"] = shifted(s, half)
                    stages[f"T.V{s}{half}"] = weighted(s, half)
            steps(pe, stages)




def experts(nc, io, out, v):
    outer = v["outer"]
    with ExitStack() as ctx:
        sem = lambda n: outer.enter_context(nc.semaphore(n))
        sb = lambda n, s, d=F32: ctx.enter_context(nc.sbuf_tensor(n, s, d))
        ps = lambda n, s, d=F32: ctx.enter_context(nc.psum_tensor(n, s, d))
        ident, slots_all, comb_all = v["ident"], v["slots_all"], v["comb_all"]
        ids_d, xn4_d, eout_d, acc_d = v["ids_d"], v["xn4_d"], v["eout_d"], v["acc_d"]
        TP = 2 * HT
        ids = sb("e_ids", [P, P], U32)
        two = lambda name, shape, dt=F32: [sb(f"e_{name}{u}", shape, dt) for u in range(2)]
        idx = two("idx", [P, TP], U32)
        xg = two("xg", [P, TP, D])
        xT = two("xT", [P, 2, KC, CAP])
        wu = two("wu", [P, 2, KC, 2 * HE])
        wd = two("wd", [2 * HE, D])
        gate = two("gate", [2 * HE, CAP])
        hT = two("hT", [2 * HE, CAP])
        eo = two("eo", [P, TP, D])
        cidx = two("cidx", [P, TOPK], U32)
        rows_ = two("rows", [P, TOPK, D])
        tot = two("tot", [P, D])
        pT = [ps(f"e_pT{e}", [P, KC * CAP]) for e in range(2)]
        pU = ps("e_pU", [P, 2 * CAP])
        pD = [ps(f"e_pD{k}", [P, D]) for k in range(2)]

        ids_in = sem("e_ids_in")
        gath, wu_in, wd_in, est, cg, acc_in, ost = ([sem(f"e_{n}{u}") for u in range(2)] for n in "gath wu_in wd_in est cg acc_in ost".split())
        pool_passed = sem("e_pool_passed")
        idx_ok, cidx_ok, T_mm, up_mm, dn_mm = (sem("e_" + n) for n in "idx_ok cidx_ok T_mm up_mm dn_mm".split())
        xA_ok, xB_ok, gate_ok, h_ok, oe_ok, oo_ok, tchain, tot_ok = (sem("e_" + n) for n in "xA_ok xB_ok gate_ok h_ok oe_ok oo_ok tchain tot_ok".split())
        block = ctx.enter_context(nc.Block())

        def pipelined(eng, transpose, up, down):
            transpose(0, 0)
            transpose(0, 1)
            up(0, 0)
            with eng.Fori(0, PAIRS // 2 - 1) as i:
                for c in range(2):
                    transpose(i, c + 2)
                    down(i, c)
                    up(i, c + 1)
            last = PAIRS // 2 - 1
            down(last, 0)
            up(last, 1)
            down(last, 1)

        def pair_of(i, c):
            return i * 2 + c

        def wait_count(eng, s, i, c, per=1, less=0):
            if isinstance(i, int) and (2 * i + c + 1) * per - less <= 0:
                return
            eng.wait_ge(s, i * (2 * per) + ((c + 1) * per - less))

        @block.sync
        def _(sp):
            def load(i, c):
                u = c % 2
                sp.dma_start(wu[u][:, :, :, :], io["wu"][bass.ds(pair_of(i, c), 1), :, :].rearrange("o p (e k n) -> (o p) e k n", e=2, k=KC)).then_inc(wu_in[u], 16)
                sp.dma_start(wd[u][:, :], io["wd"][bass.ds(pair_of(i, c), 1), :, :].rearrange("o p n -> (o p) n")).then_inc(wd_in[u], 16)

            def store(i, c):
                u = c % 2
                wait_count(sp, oe_ok, i, c, 2)
                wait_count(sp, oo_ok, i, c, 2)
                sp.dma_start(eout_d[bass.ds(pair_of(i, c) * (2 * CAP), 2 * CAP), :].rearrange("(t p) d -> p t d", p=P), eo[u][:, :, :]).then_inc(est[u], 16)

            sp.dma_start(ids[:, :], v["ids_d"].rearrange("(p n) o -> p (n o)", p=P)).then_inc(ids_in, 16)
            for c in range(2):
                load(0, c)
            with sp.Fori(0, PAIRS // 2 - 1) as i:
                for c in range(2):
                    store(i, c)
                    load(i, c + 2)
            for c in range(2):
                store(PAIRS // 2 - 1, c)
            def load_acc(i, u):
                sp.dma_start(tot[u][:, :], acc_d[bass.ds(i * 2 + u, 1), :, :].rearrange("o p d -> (o p) d")).then_inc(acc_in[u], 16)

            def store_out(i, u):
                sp.wait_ge(tot_ok, i * 2 + (u + 1))
                sp.dma_start(out.rearrange("b (t p) d -> (b t) p d", p=P)[bass.ds(i * 2 + u, 1), :, :].rearrange("o p d -> (o p) d"),
                             tot[u][:, :]).then_inc(ost[u], 16)

            for u in range(2):
                load_acc(0, u)
            with sp.Fori(0, NT // 2 - 1) as i:
                for u in range(2):
                    store_out(i, u)
                    sp.wait_ge(ost[u], i * 16 + 16)
                    load_acc(i + 1, u)
            for u in range(2):
                store_out(NT // 2 - 1, u)
            for u in range(2):
                sp.wait_ge(ost[u], 16 * (NT // 2))
                sp.wait_ge(est[u], 16 * (PAIRS // 2))

        @block.gpsimd
        def _(pool):
            g_ = nc.gpsimd

            def gather(i, c):
                u = c % 2
                wait_count(pool, T_mm, i, c - 2)
                g_.tensor_copy(idx[u][:, :], ids[:, bass.ds(pair_of(i, c) * TP, TP)]).then_inc(idx_ok, 1)
                wait_count(pool, idx_ok, i, c)
                pool.sem_inc(pool_passed, 1)
                for t in range(TP):
                    g_.indirect_dma_start(out=xg[u][:, t, :], out_offset=None, in_=xn4_d,
                                          in_offset=bass.IndirectOffsetOnAxis(ap=idx[u][:, t:t + 1], axis=0)).then_inc(gath[u], 16)

            pool.wait_ge(ids_in, 16)
            gather(0, 0)
            gather(0, 1)
            with pool.Fori(0, PAIRS // 2 - 1) as i:
                for c in range(2):
                    gather(i, c + 2)
            for u in range(2):
                pool.wait_ge(est[u], 16 * (PAIRS // 2))

            def collect(i, u):
                wait_tile = i * 2 + u
                g_.tensor_copy(cidx[u][:, :], slots_all[:, bass.ds(wait_tile, 1), :].rearrange("p o k -> p (o k)")).then_inc(cidx_ok, 1)
                hold(pool, cidx_ok, i * 2 + (u + 1), pool_passed)
                for k in range(TOPK):
                    g_.indirect_dma_start(out=rows_[u][:, k, :], out_offset=None, in_=eout_d,
                                          in_offset=bass.IndirectOffsetOnAxis(ap=cidx[u][:, k:k + 1], axis=0)).then_inc(cg[u], 16)

            for u in range(2):
                collect(0, u)
            with pool.Fori(0, NT // 2 - 1) as i:
                for u in range(2):
                    pool.wait_ge(tot_ok, i * 2 + (u + 1))
                    collect(i + 1, u)

        @block.scalar
        def _(act):
            A = nc.scalar.activation
            act.preload_act_table(ACT.Silu)

            def transpose(i, c):
                wait_count(act, T_mm, i, c)
                wait_count(act, up_mm, i, c - 2)
                A(xT[c % 2][:, 0, :, :], pT[0][:, :].rearrange("p (k s) -> p k s", k=KC), ACT.Copy).then_inc(xA_ok, 1)

            def up(i, c):
                wait_count(act, up_mm, i, c)
                A(gate[c % 2][:, :], pU[:, 0:CAP], ACT.Silu).then_inc(gate_ok, 1)

            def down(i, c):
                if not (isinstance(i, int) and i == 0 and c < 2):
                    act.wait_ge(est[c % 2], store_count(i, c))
                for k in (0, 2):
                    wait_count(act, dn_mm, i, c, TP, TP - k - 1)
                    A(eo[c % 2][:, k, :], pD[0][:, :], ACT.Copy).then_inc(oe_ok, 1)

            pipelined(act, transpose, up, down)

        @block.vector
        def _(dve):
            V = nc.vector

            def transpose(i, c):
                wait_count(dve, T_mm, i, c)
                wait_count(dve, up_mm, i, c - 2)
                V.tensor_copy(xT[c % 2][:, 1, :, :], pT[1][:, :].rearrange("p (k s) -> p k s", k=KC)).then_inc(xB_ok, 1)

            def up(i, c):
                wait_count(dve, gate_ok, i, c)
                wait_count(dve, dn_mm, i, c - 2, TP)
                V.tensor_tensor(hT[c % 2][:, :], pU[:, CAP:2 * CAP], gate[c % 2][:, :], ALU.mult).then_inc(h_ok, 1)

            def down(i, c):
                if not (isinstance(i, int) and i == 0 and c < 2):
                    dve.wait_ge(est[c % 2], store_count(i, c))
                for k in (1, 3):
                    wait_count(dve, dn_mm, i, c, TP, TP - k - 1)
                    V.tensor_copy(eo[c % 2][:, k, :], pD[1][:, :]).then_inc(oo_ok, 1)

            pipelined(dve, transpose, up, down)
            with dve.Fori(0, NT // 2) as i:
                for u in range(2):
                    dve.wait_ge(acc_in[u], i * 16 + 16)
                    dve.wait_ge(cg[u], i * (16 * TOPK) + 16 * TOPK)
                    for k in range(TOPK):
                        w = comb_all[:, bass.ds(i * 2 + u, 1), k]
                        ins = V.scalar_tensor_tensor(out=tot[u][:, :], in0=rows_[u][:, k, :], scalar=w, in1=tot[u][:, :],
                                                     op0=ALU.mult, op1=ALU.add)
                        if k < TOPK - 1:
                            ins.then_inc(tchain, 1)
                            dve.wait_ge(tchain, i * (2 * (TOPK - 1)) + (u * (TOPK - 1) + k + 1))
                        else:
                            ins.then_inc(tot_ok, 1)

        @block.tensor
        def _(pe):
            mm, tr = nc.tensor.matmul, nc.tensor.transpose

            def transpose(i, c):
                u = c % 2
                pe.wait_ge(gath[u], (i + c // 2) * (16 * TP) + 16 * TP)
                wait_count(pe, xA_ok, i, c - 1)
                wait_count(pe, xB_ok, i, c - 1)
                for e in range(2):
                    for t in range(HT):
                        for k in range(KC):
                            last = tr(pT[e][:, k * CAP + t * P:k * CAP + (t + 1) * P], xg[u][:, HT * e + t, k * P:(k + 1) * P], ident[:, :])
                last.then_inc(T_mm, 1)

            def up(i, c):
                u = c % 2
                pe.wait_ge(wu_in[u], (i + c // 2) * 16 + 16)
                wait_count(pe, xA_ok, i, c)
                wait_count(pe, xB_ok, i, c)
                wait_count(pe, h_ok, i, c - 1)
                for j in range(2):
                    for k in range(KC):
                        for e in range(2):
                            last = mm(pU[HE * e:HE * (e + 1), j * CAP:(j + 1) * CAP], wu[u][:, e, k, j * HE:(j + 1) * HE],
                                      xT[u][:, e, k, :], start=(k == 0), stop=(k == KC - 1))
                last.then_inc(up_mm, 1)

            def down(i, c):
                u = c % 2
                pe.wait_ge(wd_in[u], (i + c // 2) * 16 + 16)
                wait_count(pe, h_ok, i, c)
                for n in range(TP):
                    e, t = n // HT, n % HT
                    wait_count(pe, (oe_ok, oo_ok)[n % 2], i, c, 2, 2 - n // 2)
                    mm(pD[n % 2][:, :], hT[u][HE * e:HE * (e + 1), t * P:(t + 1) * P], wd[u][HE * e:HE * (e + 1), :],
                       start=True, stop=True).then_inc(dn_mm, 1)

            pipelined(pe, transpose, up, down)


def store_count(i, c):
    return i * 16 + (c // 2) * 16


_SHAPE = (NB, S, D)


def rows(w):
    k = w.shape[0] // P
    return np.ascontiguousarray(w.reshape(k, P, w.shape[1]).transpose(1, 0, 2))


def kernel(x, ctx_2048, g_xattn, g_ffn, L0_xattn_Wh, L0_xattn_wg_w, L0_xattn_wo_w, L0_xattn_gn_gamma,
           L0_xattn_gn_beta, L0_ffn_W_up, L0_ffn_W_down, L0_ffn_W_gate, L0_ffn_W_expert, L1_ffn_w_gate,
           L1_ffn_w_shared_up, L1_ffn_w_shared_down, L1_ffn_w_up, L1_ffn_w_down):
    import concourse.bacc as bacc
    from concourse.bass_utils import run_bass_kernel_spmd as run

    a = lambda t: np.asarray(t)
    c = np.ascontiguousarray
    wh = a(L0_xattn_Wh)
    arrays = {
        "x": c(a(x)),
        "ctx": c(a(ctx_2048)),
        "ctxT": c(a(ctx_2048).reshape(NB, S, KC, P).transpose(0, 3, 2, 1).reshape(NB, P, KC * S)),
        "gates": c(np.concatenate([np.tile(a(g_xattn)[None, :], (P, 1)), np.tile(a(g_ffn)[None, :], (P, 1))], axis=1)),
        "mask": decay_mask(),
        "wh": c(wh.transpose(1, 0, 2)),
        "whT": c(wh.transpose(2, 0, 1)),
        "wg": rows(a(L0_xattn_wg_w)),
        "wo": rows(a(L0_xattn_wo_w)),
        "wupT": rows(a(L0_ffn_W_up).T),
        "wdnT": rows(a(L0_ffn_W_down).T),
        "wexp": rows(a(L0_ffn_W_expert)),
        "wg0": rows(a(L0_ffn_W_gate).T),
        "wg1": rows(a(L1_ffn_w_gate)),
        "wsu": rows(a(L1_ffn_w_shared_up)),
        "wsd": c(a(L1_ffn_w_shared_down)),
        "gamma": c(a(L0_xattn_gn_gamma).reshape(KC, P).T),
        "beta": c(a(L0_xattn_gn_beta).reshape(KC, P).T),
        "wu": c(a(L1_ffn_w_up).reshape(PAIRS, 2, KC, P, 2 * HE).transpose(0, 3, 1, 2, 4).reshape(PAIRS, P, 2 * KC * 2 * HE)),
        "wd": c(a(L1_ffn_w_down).reshape(PAIRS, 2 * HE, D)),
    }
    nc = bacc.Bacc("TRN2", target_bir_lowering=False, num_devices=1)
    io = {n: nc.dram_tensor("in_" + n, t.shape, F32, kind="ExternalInput").ap() for n, t in arrays.items()}
    out = nc.dram_tensor("out", _SHAPE, F32, kind="ExternalOutput").ap()
    build(nc, io, out)
    r = run(nc, [{"in_" + n: t for n, t in arrays.items()}], core_ids=[0])
    return r.results[0]["out"]
```

```python
from contextlib import ExitStack

import numpy as np

import concourse.bass as bass
from concourse import mybir

F32 = mybir.dt.float32
BF16 = mybir.dt.bfloat16
U32 = mybir.dt.uint32
ALU = mybir.AluOpType
ACT = mybir.ActivationFunctionType
AX = mybir.AxisListType

P = 128
NB, S, D = 8, 256, 512
T = S // P
NT = NB * T
KC = D // P
H0 = 4
HS = 8
HD = S // HS
G = 4
NG = HS // G
E0 = 8
E1, HE, TOPK, CAP = 64, 64, 6, 256
HT = CAP // P
SH = 128
GN_EPS, LN_EPS = 1e-3, 1e-5
SCALE1 = float(1.0 / np.sqrt(np.float32(HD)))
SKIP = 1.0e6
PAIRS = E1 // 2


def decay_mask():
    gam = (1.0 - 2.0 ** (-5.0 - np.arange(H0, dtype=np.float32))).astype(np.float32)
    idx = np.arange(S, dtype=np.float32)
    expo = idx[None, :] - idx[:, None]
    d = np.where(expo[None] <= 0, gam[:, None, None] ** np.minimum(expo, 0.0)[None], 0.0).astype(np.float32)
    dn = d / np.sqrt(d.sum(-1))[:, None, :]
    m = (dn / np.sqrt(np.float32(P))).transpose(2, 0, 1)
    return np.ascontiguousarray(m.reshape(T, P, H0, S).transpose(1, 0, 2, 3)).astype(np.float32)


def build(nc, io, out):
    dram = lambda name, shape, dt=F32: nc.dram_tensor(name, shape, dt, kind="Internal").ap()
    xnT_d = dram("xnT_d", (NB, P, KC * S))
    v_d = dram("v_d", (NB, P, T * D))
    kparts_d = dram("kparts_d", (3, NB * S, D), BF16)
    qparts_d = dram("qparts_d", (2, 3, S, D), BF16)
    xn4_d = dram("xn4_d", (NB * S, D))
    acc_d = dram("acc_d", (NT, P, D))
    ids_d = dram("ids_d", (P * P, 1), U32)
    eout_d = dram("eout_d", (E1 * CAP, D))

    with ExitStack() as outer:
        def sem(name):
            return outer.enter_context(nc.semaphore(name))

        def sb(name, shape, dt=F32, ctx=outer):
            return ctx.enter_context(nc.sbuf_tensor(name, shape, dt))

        ident = sb("ident", [P, P])
        ident16 = sb("ident16", [P, P], BF16)
        ones32 = sb("ones32", [P, HD])
        ones16 = sb("ones16", [P, P], BF16)
        before16 = sb("before16", [P, P], BF16)
        mhalf = sb("mhalf", [P, T])
        iota_e = sb("iota_e", [P, E1])
        tok_f = sb("tok_f", [P, 1])
        tg_x = sb("tg_x", [P, 2])
        tg_f = sb("tg_f", [P, 2])
        slots_all = sb("slots_all", [P, NT, TOPK], U32)
        comb_all = sb("comb_all", [P, NT, TOPK])

        with ExitStack() as mid:
            wg = sb("wg", [P, KC, D], ctx=mid)
            wo = sb("wo", [P, KC, D], ctx=mid)
            wupT = sb("wupT", [P, KC, D], ctx=mid)
            wdnT = sb("wdnT", [P, KC, D], ctx=mid)
            wexp = sb("wexp", [P, KC, D], ctx=mid)
            wg0 = sb("wg0", [P, KC, E0], ctx=mid)
            wg1 = sb("wg1", [P, KC, E1], ctx=mid)
            wsu = sb("wsu", [P, KC, 2 * SH], ctx=mid)
            wsd = sb("wsd", [P, D], ctx=mid)
            gamma = sb("gamma", [P, KC], ctx=mid)
            beta = sb("beta", [P, KC], ctx=mid)
            AT = sb("AT", [P, T, H0, S], ctx=mid)
            setup_and_scores(nc, io, outer, mid, locals())
            main_loop(nc, io, locals())
        experts(nc, io, out, locals())


def at(i, u, k=1, per=1):
    return i * (2 * per) + (u * per + k)


def hold(eng, s, n, passed):
    eng.wait_ge(s, n)
    eng.sem_inc(passed, 1)


def setup_and_scores(nc, io, outer, mid, v):
    ident, ident16, ones32, ones16, before16 = (v[n] for n in "ident ident16 ones32 ones16 before16".split())
    mhalf, iota_e, tok_f, tg_x, tg_f, AT = (v[n] for n in "mhalf iota_e tok_f tg_x tg_f AT".split())
    xnT_d, v_d, kparts_d, ids_d = (v[n] for n in "xnT_d v_d kparts_d ids_d".split())
    with ExitStack() as ctx:
        sem = lambda n: outer.enter_context(nc.semaphore(n))
        sb = lambda n, s, d=F32: ctx.enter_context(nc.sbuf_tensor(n, s, d))
        ps = lambda n, s, d=F32: ctx.enter_context(nc.psum_tensor(n, s, d))
        wh = sb("wh", [P, H0, P])
        whT = sb("whT", [P, H0, P])
        gram = sb("gram", [P, H0, P])
        mask = sb("mask", [P, T, H0, S])
        gates = sb("gates", [P, 4])
        zeros = sb("zeros", [P, D], BF16)
        zids = sb("zids", [P, P], U32)
        xin = [sb(f"a_x{u}", [P, T, D]) for u in range(2)]
        cT = [sb(f"a_cT{u}", [P, KC, S]) for u in range(2)]
        xn = [sb(f"a_xn{u}", [P, T, D]) for u in range(2)]
        xnT = [sb(f"a_xnT{u}", [P, KC, S]) for u in range(2)]
        qT = sb("a_qT", [P, H0, S])
        val = [sb(f"a_val{u}", [P, T, D]) for u in range(2)]
        st = sb("a_st", [P, T, 6])
        mv = sb("a_mv", [P, T, 2])
        veps = sb("a_veps", [P, T])
        rstd = sb("a_rstd", [P, T])
        pX = ps("a_pX", [P, KC * S])
        pY = ps("a_pY", [P, KC * S])
        pS = [ps(f"a_pS{k}", [P, 512]) for k in range(3)]

        weights_in, gates_in, wh_in, mask_in = sem("weights_in"), sem("gates_in"), sem("wh_in"), sem("mask_in")
        ids_zeroed, pool_c, zero_set, tg_done = sem("ids_zeroed"), sem("pool_c"), sem("zero_set"), sem("tg_done")
        gram_mm, gram_ok = sem("gram_mm"), sem("gram_ok")
        x_in = [sem(f"ax_in{u}") for u in range(2)]
        cT_in = [sem(f"acT_in{u}") for u in range(2)]
        x_free, cT_free = sem("ax_free"), sem("acT_free")
        chain, var_ok, rstd_ok, xn_ok = sem("a_chain"), sem("a_var"), sem("a_rstd_s"), sem("a_xn_s")
        xT_mm, xT_ok, q_mm, q_ok, v_mm, v_ok, s_mm = (sem("a_" + n) for n in "xT_mm xT_ok q_mm q_ok v_mm v_ok s_mm".split())
        stored = [sem(f"a_stored{u}") for u in range(2)]
        sc_chain, at_done, passed = sem("a_sc_chain"), sem("a_at_done"), sem("a_passed")
        block = ctx.enter_context(nc.Block())

        @block.sync
        def _(sp):
            def weights(*names):
                for name in names:
                    t = v[name]
                    ap = t[:, :, :] if len(t.shape) == 3 else t[:, :]
                    sp.dma_start(ap, io[name]).then_inc(weights_in, 16)

            def load_x(b, u):
                sp.dma_start(xin[u][:, :, :], io["x"][bass.ds(b, 1), :, :].rearrange("o (t p) d -> p (o t) d", p=P)).then_inc(x_in[u], 16)

            def load_ctx(b, u):
                sp.dma_start(cT[u][:, :, :], io["ctxT"][bass.ds(b, 1), :, :].rearrange("o p (k s) -> (o p) k s", k=KC)).then_inc(cT_in[u], 16)

            def store(i, b, u):
                sp.wait_ge(v_ok, at(i, u, 2))
                sp.dma_start(v_d[bass.ds(b, 1), :, :].rearrange("o p (t d) -> (o p) t d", t=T), val[u][:, :, :]).then_inc(stored[u], 16)
                sp.wait_ge(xT_ok, at(i, u))
                sp.dma_start(xnT_d[bass.ds(b, 1), :, :].rearrange("o p (k s) -> (o p) k s", k=KC), xnT[u][:, :, :]).then_inc(stored[u], 16)

            sp.dma_start(wh[:, :, :], io["wh"]).then_inc(wh_in, 16)
            sp.dma_start(whT[:, :, :], io["whT"]).then_inc(wh_in, 16)
            for u in range(2):
                load_x(u, u)
                load_ctx(u, u)
            sp.dma_start(gates[:, :], io["gates"]).then_inc(gates_in, 16)
            sp.dma_start(mask[:, :, :, :], io["mask"]).then_inc(mask_in, 16)
            weights("wg", "gamma", "beta", "wo", "wg0", "wupT")
            sp.wait_ge(pool_c, 1)
            sp.dma_start(ids_d.rearrange("(p n) o -> p (n o)", p=P), zids[:, :]).then_inc(ids_zeroed, 16)
            with sp.Fori(0, NB // 2 - 1) as i:
                for u in range(2):
                    sp.wait_ge(x_free, at(i, u))
                    load_x(i * 2 + (2 + u), u)
                    store(i, i * 2 + u, u)
                    sp.wait_ge(cT_free, at(i, u))
                    load_ctx(i * 2 + (2 + u), u)
            weights("wdnT", "wexp", "wg1", "wsu", "wsd")
            last = NB // 2 - 1
            for u in range(2):
                store(last, 2 * last + u, u)
            for u in range(2):
                sp.wait_ge(stored[u], 2 * 16 * (NB // 2))
            sp.wait_ge(weights_in, 16 * 11)
            sp.wait_ge(ids_zeroed, 16)

        @block.gpsimd
        def _(pool):
            g = nc.gpsimd
            g.memset(zids[:, :], 0).then_inc(pool_c, 1)
            g.memset(ident[:, :], 0.0).then_inc(pool_c, 1)
            g.memset(ident16[:, :], 0.0).then_inc(pool_c, 1)
            g.memset(before16[:, :], 1.0).then_inc(pool_c, 1)
            g.memset(ones32[:, :], 1.0)
            g.memset(ones16[:, :], 1.0)
            g.memset(mhalf[:, :], -0.5).then_inc(pool_c, 1)
            g.iota(iota_e[:, :], pattern=[[1, E1]], base=0, channel_multiplier=0, allow_small_or_imprecise_dtypes=True)
            g.iota(tok_f[:, :], pattern=[[0, 1]], base=0, channel_multiplier=1, allow_small_or_imprecise_dtypes=True)
            pool.wait_ge(pool_c, 5)
            for m in (ident, ident16):
                g.affine_select(out=m[:, :], in_=m[:, :], compare_op=ALU.not_equal, fill=1.0, base=0,
                                pattern=[[-1, P]], channel_multiplier=1).then_inc(pool_c, 1)
            g.affine_select(out=before16[:, :], in_=before16[:, :], compare_op=ALU.is_gt, fill=0.0, base=0,
                            pattern=[[1, P]], channel_multiplier=-1).then_inc(pool_c, 1)
            with pool.Fori(0, NB // 2) as i:
                for u in range(2):
                    pool.wait_ge(var_ok, at(i, u))
                    g.tensor_tensor(rstd[:, :], veps[:, :], mhalf[:, :], ALU.pow).then_inc(rstd_ok, 1)

        @block.scalar
        def _(act):
            act.preload_act_table(ACT.Exp)
            act.wait_ge(gates_in, 16)
            nc.scalar.activation(tg_x[:, :], gates[:, 0:2], ACT.Tanh).then_inc(tg_done, 1)
            nc.scalar.activation(tg_f[:, :], gates[:, 2:4], ACT.Tanh).then_inc(tg_done, 1)
            act.wait_ge(gram_mm, 1)
            nc.scalar.activation(gram[:, :, :], pX[:, 0:H0 * P].rearrange("p (h e) -> p h e", h=H0), ACT.Copy).then_inc(gram_ok, 1)
            A = nc.scalar.activation

            def turned(i, u, c):
                if not (isinstance(i, int) and 2 * i + c < 2):
                    act.wait_ge(stored[u], (i + c // 2) * 32)
                act.wait_ge(xT_mm, at(i, c, 3))
                A(xnT[u][:, :, :], pX[:, :].rearrange("p (k s) -> p k s", k=KC), ACT.Copy).then_inc(xT_ok, 1)

            def valued(i, u):
                act.wait_ge(v_mm, at(i, u))
                A(val[u][:, :, :], pY[:, :].rearrange("p (t d) -> p t d", t=T), ACT.Copy).then_inc(v_ok, 1)

            def queried(i, u):
                act.wait_ge(q_mm, at(i, u))
                A(qT[:, :, :], pX[:, :].rearrange("p (k s) -> p k s", k=KC), ACT.Copy).then_inc(q_ok, 1)

            turned(0, 0, 0)
            with act.Fori(0, NB // 2 - 1) as i:
                for u in range(2):
                    queried(i, u)
                    valued(i, u)
                    turned(i, 1 - u, u + 1)
            queried(NB // 2 - 1, 0)
            valued(NB // 2 - 1, 0)
            turned(NB // 2 - 1, 1, 1)
            queried(NB // 2 - 1, 1)
            valued(NB // 2 - 1, 1)

        @block.vector
        def _(dve):
            n = [0]

            def link(ins, sem_, base):
                n[0] += 1
                ins.then_inc(sem_, 1)
                hold(dve, sem_, base + n[0], passed)

            nc.vector.memset(zeros[:, :], 0.0).then_inc(zero_set, 1)
            PER = 3
            with dve.Fori(0, NB // 2) as i:
                for u in range(2):
                    n[0] = u * PER
                    base = i * (2 * PER)
                    dve.wait_ge(x_in[u], i * 16 + 16)
                    for t in range(T):
                        last = nc.vector.bn_stats(st[:, t, :], xin[u][:, t, :])
                    link(last, chain, base)
                    for t in range(T):
                        last = nc.vector.bn_aggr(mv[:, t, :], st[:, t, :])
                    link(last, chain, base)
                    nc.vector.tensor_scalar(veps[:, :], mv[:, :, 1], LN_EPS, None, ALU.add).then_inc(var_ok, 1)
                    dve.wait_ge(xT_mm, at(i, u))
                    dve.wait_ge(rstd_ok, at(i, u))
                    for t in range(T):
                        last = nc.vector.tensor_scalar(xn[u][:, t, :], xin[u][:, t, :], mv[:, t, 0:1], rstd[:, t:t + 1], ALU.subtract, ALU.mult)
                    link(last, chain, base)
                    assert n[0] == (u + 1) * PER
                    dve.sem_inc(xn_ok, 1)
                    dve.sem_inc(x_free, 1)
            dve.wait_ge(mask_in, 16)
            dve.wait_ge(s_mm, 1)
            k = 0
            for j in range(2):
                nc.vector.tensor_tensor(AT[:, 0, 2 * j:2 * j + 2, :], pS[j][:, :].rearrange("p (h s) -> p h s", h=2),
                                        mask[:, 0, 2 * j:2 * j + 2, :], ALU.mult).then_inc(sc_chain, 1)
            nc.vector.memset(AT[:, 1, :, 0:P], 1.0)
            nc.vector.tensor_tensor(AT[:, 1, :, P:S], pS[2][:, :].rearrange("p (h s) -> p h s", h=H0),
                                    mask[:, 1, :, P:S], ALU.mult).then_inc(sc_chain, 1)
            dve.wait_ge(sc_chain, 3)
            flat = lambda t: t[:, :, :, :].rearrange("p t h s -> p (t h s)")
            nc.vector.scalar_tensor_tensor(out=flat(mask), in0=flat(AT), scalar=-1.0, in1=flat(AT), op0=ALU.mult, op1=ALU.max).then_inc(at_done, 1)
            dve.wait_ge(at_done, 1)
            nc.vector.tensor_scalar(flat(AT), flat(mask), 1.0, None, ALU.max).then_inc(at_done, 1)
            dve.wait_ge(at_done, 2)

        @block.tensor
        def _(pe):
            mm = nc.tensor.matmul
            pe.sem_inc(v_ok, 1)
            pe.sem_inc(xT_mm, 2)
            pe.wait_ge(wh_in, 32)
            for h in range(H0):
                last = mm(pX[:, h * P:(h + 1) * P], whT[:, h, :], whT[:, h, :], start=True, stop=True)
            last.then_inc(gram_mm, 1)
            pe.wait_ge(zero_set, 1)
            for k in range(3):
                mm(pS[k][:, :], zeros[:, 0:P], zeros[:, :], start=True, stop=False, skip_group_check=True)
            pe.wait_ge(pool_c, 8)
            pe.wait_ge(gram_ok, 1)

            def turn(i, u, c):
                pe.wait_ge(xn_ok, at(i, c))
                for t in range(T):
                    for k in range(KC):
                        last = nc.tensor.transpose(pX[:, k * S + t * P:k * S + (t + 1) * P], xn[u][:, t, k * P:(k + 1) * P], ident[:, :])
                last.then_inc(xT_mm, 1)

            def values(i, u):
                pe.wait_ge(cT_in[u], i * 16 + 16)
                pe.wait_ge(v_ok, at(i, u))
                for t in range(T):
                    for h in range(H0):
                        last = mm(pY[:, t * D + h * P:t * D + (h + 1) * P], cT[u][:, h, t * P:(t + 1) * P], wh[:, h, :], start=True, stop=True)
                last.then_inc(v_mm, 1)

            def queries(i, u):
                pe.wait_ge(xT_ok, at(i, u))
                for h in range(H0):
                    last = mm(pX[:, h * S:(h + 1) * S], gram[:, h, :], xnT[u][:, h, :], start=True, stop=True)
                last.then_inc(q_mm, 1)

            def scores(i, u):
                for h in range(H0):
                    mm(pS[h // 2][:, (h % 2) * S:(h % 2 + 1) * S], cT[u][:, h, 0:P], qT[:, h, :], start=False, stop=False, skip_group_check=True)
                    last = mm(pS[2][:, h * P:(h + 1) * P], cT[u][:, h, P:S], qT[:, h, P:S], start=False, stop=False, skip_group_check=True)
                last.then_inc(cT_free, 1)

            turn(0, 0, 0)
            with pe.Fori(0, NB // 2 - 1) as i:
                for u in range(2):
                    queries(i, u)
                    values(i, u)
                    pe.wait_ge(q_ok, at(i, u))
                    turn(i, 1 - u, u + 1)
                    scores(i, u)
            last_pair = NB // 2 - 1
            queries(last_pair, 0)
            values(last_pair, 0)
            pe.wait_ge(q_ok, at(last_pair, 0))
            turn(last_pair, 1, 1)
            scores(last_pair, 0)
            queries(last_pair, 1)
            values(last_pair, 1)
            pe.wait_ge(q_ok, at(last_pair, 1))
            scores(last_pair, 1)
            for k in range(3):
                last = mm(pS[k][:, :], zeros[:, 0:P], zeros[:, :], start=False, stop=True, skip_group_check=True)
            last.then_inc(s_mm, 1)


ORDERS = {"all": """
F.out0 F.out1 F.stats F.gate0 R.stats F.gate1 F.norm F.gate2 T.S0 R.norm F.turn F.gate3 T.S1 F.affine R.turn T.S2 R.gates
T.S3 F.x1a0 T.S4 F.x1a1 T.S5 F.x1b0 T.S6 T.S7 F.x1b1 T.P0 F.res1 T.M0 R.up0 R.up1 T.Q0a F.norm2 T.Q0b F.turn2 T.Q1a T.S8
F.gates T.S9 R.shared F.up0 T.Q1b F.up1 T.S10 F.best R.sigmoid R.down0 R.down1 F.weight T.S11 R.acc F.up2 F.up3 R.chosen
F.expert0 R.pos T.V0a T.V0b T.Q2a T.V1a R.places T.Q2b T.V1b F.expert1 T.S12 R.send0 T.S13 F.downa0 T.S14 F.downa1 T.S15 T.P1 F.keys
T.Q3a T.V2a T.M1 T.Q3b T.V2b F.downb0 R.send1 T.V3a T.V3b T.A0 F.downb1 F.res2 R.send2 T.Q4a T.Q4b R.send3
T.Q5a T.V4a T.Q5b T.V4b F.norm3 T.add0 T.Q6a T.V5a T.Q6b T.V5b T.Q7a T.V6a T.Q7b T.V6b
T.V7a T.V7b T.A1 T.add1
""".split(), "attention and routing": """
R.stats T.S0 R.norm T.S1 R.turn T.S2 T.S3 R.gates T.S4 T.S5 R.up0 T.S6 R.up1 T.S7 T.P0 T.M0 R.shared T.S8 T.S9 R.down0 R.down1 R.acc
T.Q0a T.Q0b T.S10 T.S11 T.Q1a T.Q1b T.V0a T.V0b T.S12 T.S13 T.Q2a T.V1a T.S14 T.Q2b T.V1b T.S15 T.P1 R.sigmoid T.Q3a T.V2a T.M1
T.Q3b T.V2b R.chosen T.V3a T.V3b T.A0 R.pos T.Q4a T.Q4b R.places T.Q5a T.V4a T.Q5b T.V4b R.send0 T.add0 R.send1 T.Q6a T.V5a
T.Q6b T.V5b R.send2 T.Q7a T.V6a T.Q7b T.V6b R.send3 T.V7a T.V7b T.A1 T.add1
""".split(), "routing": """
R.stats R.norm R.turn R.gates R.sigmoid R.up0 R.up1 R.chosen R.pos R.places R.send0 R.send1 R.send2 R.send3 R.shared R.down0
R.down1 R.acc
""".split()}


HALF = {"a": (0, 1), "b": (2, 3)}


def ring_slots(order):
    slots = []
    for name in order:
        stage = name[2:]
        if name[:3] == "T.S":
            slots += [(name, ("mx_ok", 2 * int(stage[1:]) + m + 1, KC * HS)) for m in range(2)]
        elif name[:3] == "T.M":
            slots.append((name, ("mrow_ok", int(stage[1:]) + 1, NG)))
        elif name[:3] == "T.Q":
            slots += [(name, ("exp_ok", G * int(stage[1]) + q + 1, KC * HS)) for q in HALF[stage[2]]]
        elif name == "R.gates":
            slots.append((name, ("eg_ok", 1, 1)))
        elif name == "R.pos":
            slots.append((name, ("pos_ok", 1, 1)))
    assert len(slots) % 2 == 0
    return slots


SLOTS = {name: ring_slots(order) for name, order in ORDERS.items()}


def first_slot(name, streams):
    return [s[0] for s in SLOTS[streams["order"]]].index(name)


def after(eng, s, i, c, k, per=1, unit=1):
    if isinstance(i, int):
        if (2 * i + c) * per + k > 0:
            eng.wait_ge(s, ((2 * i + c) * per + k) * unit)
    else:
        assert c * per + k > 0
        eng.wait_ge(s, i * (2 * per * unit) + (c * per + k) * unit)


def steps(eng, stages, peeled=0):
    def step(order, i, **streams):
        for name in ORDERS[order]:
            if name[0] in streams and name in stages:
                stages[name](i, streams[name[0]], {**streams, "order": order})

    assert set(stages) <= set(ORDERS["all"])
    step("all", 0, F=0)
    step("all", 0, T=0, F=1)
    with eng.Fori(0, NB // 2 - 1 - peeled) as i:
        for u in range(2):
            step("all", i, R=u, T=u + 1, F=u + 2)
    for i in range(NB // 2 - 1 - peeled, NB // 2 - 1):
        for u in range(2):
            step("all", i, R=u, T=u + 1, F=u + 2)
    step("attention and routing", NB // 2 - 1, R=0, T=1)
    step("routing", NB // 2 - 1, R=1)


def main_loop(nc, io, v):
    outer = v["outer"]
    with ExitStack() as ctx:
        sem = lambda n: outer.enter_context(nc.semaphore(n))
        sb = lambda n, s, d=F32: ctx.enter_context(nc.sbuf_tensor(n, s, d))
        ps = lambda n, s, d=F32: ctx.enter_context(nc.psum_tensor(n, s, d))
        ident, ident16, ones32, ones16, before16 = (v[n] for n in "ident ident16 ones32 ones16 before16".split())
        mhalf, iota_e, tok_f, tg_x, tg_f, AT = (v[n] for n in "mhalf iota_e tok_f tg_x tg_f AT".split())
        wg, wo, wupT, wdnT, wexp, wg0, wg1, wsu, wsd = (v[n] for n in "wg wo wupT wdnT wexp wg0 wg1 wsu wsd".split())
        gamma, beta, slots_all, comb_all = (v[n] for n in "gamma beta slots_all comb_all".split())
        xnT_d, v_d, kparts_d, qparts_d, xn4_d, acc_d, ids_d = (
            v[n] for n in "xnT_d v_d kparts_d qparts_d xn4_d acc_d ids_d".split())
        two = lambda name, shape, dt=F32: [sb(f"{name}{u}", shape, dt) for u in range(2)]

        xin = sb("b_x", [P, T, D])
        kin = sb("b_k", [P, T, D])
        xnT = sb("b_xnT", [P, KC, S])
        val = sb("b_val", [P, T, D])
        cT = sb("b_cT", [P, KC, S])
        ka = two("b_ka", [P, HS, D], BF16)
        kb = sb("b_kb", [P, HS, D], BF16)
        qa = two("b_qa", [P, HS, D], BF16)
        qb = sb("b_qb", [P, HS, D], BF16)
        KB = 3 * HD + 3
        norm = sb("f_norm", [P, T, D])
        normT = sb("f_normT", [P, KC, S])
        hT = sb("f_hT", [P, KC, S])
        zT = sb("f_zT", [P, KC, S])
        tmp = zT[:, :, :].rearrange("p k s -> p (k s)").rearrange("p (t d) -> p t d", t=T)
        xs = two("f_xs", [P, T, D])
        qp = sb("f_qp", [P, 3, T, D], BF16)
        stF, mvF, vepsF, rstdF = sb("f_st", [P, T, 6]), sb("f_mv", [P, T, 2]), sb("f_veps", [P, T]), sb("f_rstd", [P, T])
        m8 = sb("f_m8", [P, T, 8])
        gap = sb("f_gap", [P, T, 1])
        egap = sb("f_egap", [P, T, 1])
        rw = sb("f_rw", [P, 3, T])
        probs = [sb(f"t_probs{k}", [P, G, D]) for k in range(2)]
        rsum = sb("t_rsum", [P, D])
        rcol = sb("t_rcol", [P, D // HD])
        att = sb("t_att", [P, D])
        nmx = sb("t_nmx", [P, KC, G])
        nmr = sb("t_nmr", [P, 2, KC, G])
        nmp = sb("t_nmp", [P, KC, 3, G], BF16)
        mrow = sb("t_mrow", [3 * G, D], BF16)
        acc = sb("r_acc", [P, T, D])
        normR = sb("r_norm", [P, T, D])
        normRT = sb("r_normT", [P, KC, S])
        stR, mvR, vepsR, rstdR = sb("r_st", [P, T, 6]), sb("r_mv", [P, T, 2]), sb("r_veps", [P, T]), sb("r_rstd", [P, T])
        eg = sb("r_eg", [P, T, E1])
        score = sb("r_score", [P, T, E1])
        top = sb("r_top", [P, T, 8])
        topi = sb("r_topi", [P, T, 8], U32)
        topf = sb("r_topf", [P, T, TOPK])
        onehot = sb("r_onehot", [P, T, TOPK, E1], BF16)
        chosen = sb("r_chosen", [P, T, E1])
        chosen16 = sb("r_chosen16", [P, T, E1], BF16)
        cum = sb("r_cum", [P, E1])
        cum16 = sb("r_cum16", [P, T, E1], BF16)
        post = sb("r_post", [P, T, E1])
        ohp = sb("r_ohp", [P, T, TOPK, E1])
        pos = sb("r_pos", [P, T, TOPK])
        small = sb("r_small", [P, 6, T, TOPK])
        wsum = sb("r_wsum", [P, 2, T])
        addr = sb("r_addr", [P, T, TOPK], U32)
        tok = sb("r_tok", [P, T], U32)
        es = sb("r_es", [P, S])
        es2 = sb("r_es2", [P, S])
        shT = sb("r_shT", [P, S])

        pA = ps("f_pA", [P, 1024])
        pB = ps("f_pB", [P, 1024])
        ring = [ps(f"ring{k}", [P, 512]) for k in range(2)]
        pV = ps("t_pV", [P, 512])
        pZ = ps("t_pZ", [P, 512])
        a3 = lambda t: t[:, :].rearrange("p (k s) -> p k s", k=KC)
        t3 = lambda t: t[:, :].rearrange("p (t d) -> p t d", t=T)

        W = {}
        for name in ("gate_mm", "o_mm", "nT_mm", "x1_mm", "x2T_mm", "lg_mm", "up_mm", "ex_mm", "dn_mm",
                     "s_mm", "mT_mm", "st_mm", "pv_step", "x4T_mm", "gt_mm", "su_mm", "pos_mm", "sd_mm",
                     "f_chain", "t_chain", "r_chain", "f_var", "f_rstd_ok", "r_var", "r_rstd_ok",
                     "n_ok", "zT_ok", "x1_ok", "x2n_ok", "gap_ok", "x2_ok", "q_ok", "k_ok", "kst", "kin_in",
                     "mx_ok", "nmp_ok", "att_ok", "x3_ok", "x4n_ok", "m_ok", "pos_ok", "route_ok", "shT_ok", "acc_ok",
                     "yT_ok", "x2T_ok", "uT_ok", "egap_ok", "mrow_ok", "exp_ok", "x4T_ok", "eg_ok", "es_ok",
                     "kept_ok", "sums_ok", "ones_ok", "cum_ok", "addr_free", "passed", "pool_passed",
                     "x_in", "xnT_in", "val_in", "cT_in", "ka_in0", "ka_in1", "kb_in", "qa_in", "qb_in",
                     "qst", "mld", "x4st", "accst", "scat"):
            W[name] = sem("b_" + name)
        block = ctx.enter_context(nc.Block())

        @block.sync
        def _(sp):
            def by_batch(i, c):
                return i * 2 + c

            def load_front(i, c, streams):
                b = by_batch(i, c)
                sp.dma_start(xnT[:, :, :], xnT_d[bass.ds(b, 1), :, :].rearrange("o p (k s) -> (o p) k s", k=KC)).then_inc(W["xnT_in"], 16)
                sp.dma_start(val[:, :, :], v_d[bass.ds(b, 1), :, :].rearrange("o p (t d) -> (o p) t d", t=T)).then_inc(W["val_in"], 16)
                sp.dma_start(xin[:, :, :], io["x"][bass.ds(b, 1), :, :].rearrange("o (t p) d -> p (o t) d", p=P)).then_inc(W["x_in"], 16)

            def stack(dst, src, parts, s):
                for blk, part in enumerate(parts):
                    sp.dma_start(dst[HD * blk:HD * (blk + 1), :, :], src(part).rearrange("(h r) d -> r h d", r=HD)).then_inc(s, 16)

            keys = lambda i, c: (lambda part: kparts_d[part, bass.ds(by_batch(i, c) * S, S), :])
            queries = lambda c: (lambda part: qparts_d[c % 2, part, :, :])

            def load_ka(i, c):
                stack(ka[c % 2], keys(i, c), (0, 1, 0, 1), W[f"ka_in{c % 2}"])

            def load_kin(i, c):
                sp.dma_start(kin[:, :, :], io["ctx"][bass.ds(by_batch(i, c), 1), :, :].rearrange("o (t p) d -> p (o t) d", p=P)).then_inc(W["kin_in"], 16)

            def f_keys(i, c, streams):
                after(sp, W["k_ok"], i, c, 1)
                for k in range(3):
                    sp.dma_start(kparts_d[k, bass.ds(by_batch(i, c) * S, S), :].rearrange("(t p) d -> p t d", p=P), qp[:, k, :, :]).then_inc(W["kst"], 16)
                if not (isinstance(i, int) and 2 * i + c == NB - 1):
                    load_kin(i, c + 1)
                after(sp, W["kst"], i, c, 3, 3, 16)
                load_ka(i, c)

            def load_back(i, c):
                stack(kb, keys(i, c), (0, 2, 2), W["kb_in"])
                sp.dma_start(cT[:, :, :], io["ctxT"][bass.ds(by_batch(i, c), 1), :, :].rearrange("o p (k s) -> (o p) k s", k=KC)).then_inc(W["cT_in"], 16)

            def f_next(i, c, streams):
                after(sp, W["x1_ok"], i, c, 1)
                if not (isinstance(i, int) and 2 * i + c == NB - 1):
                    load_front(i, c + 1, streams)

            def f_queries(i, c, streams):
                after(sp, W["q_ok"], i, c, 1)
                for k in range(3):
                    sp.dma_start(qparts_d[c % 2, k, :, :].rearrange("(t p) d -> p t d", p=P), qp[:, k, :, :]).then_inc(W["qst"], 16)
                after(sp, W["qst"], i, c, 3, 3, 16)
                stack(qa[c % 2], queries(c), (0, 0, 1, 1), W["qa_in"])
                if "T" not in streams:
                    load_back(i, c)
                    stack(qb, queries(c), (2, 0, 1), W["qb_in"])

            def t_next(i, c, streams):
                after(sp, W["pv_step"], i, c, NG * KC, NG * KC)
                if "F" in streams:
                    stack(qb, queries(c + 1), (2, 0, 1), W["qb_in"])
                    load_back(i, c + 1)

            def r_rows(i, c, streams):
                after(sp, W["x4n_ok"], i, c, 1)
                sp.dma_start(xn4_d[bass.ds(by_batch(i, c) * S, S), :].rearrange("(t p) d -> p t d", p=P), normR[:, :, :]).then_inc(W["x4st"], 16)

            def r_acc(i, c, streams):
                after(sp, W["acc_ok"], i, c, 1)
                sp.dma_start(acc_d[bass.ds(by_batch(i, c) * T, T), :, :].rearrange("t p d -> p t d"), acc[:, :, :]).then_inc(W["accst"], 16)

            load_front(0, 0, None)
            sp.sem_inc(W["x4st"], 16)
            sp.wait_ge(W["ones_ok"], 1)
            load_kin(0, 0)
            steps(sp, {"R.norm": r_rows, "R.acc": r_acc, "F.up2": f_next, 
                       "F.keys": f_keys, "F.norm3": f_queries, "T.V7b": t_next}, peeled=1)
            sp.wait_ge(W["x4st"], 16 * NB + 16)
            sp.wait_ge(W["accst"], 16 * NB)
            sp.wait_ge(W["qst"], 48 * NB)
            sp.wait_ge(W["kst"], 48 * NB)

        @block.gpsimd
        def _(pool):
            g_ = nc.gpsimd
            last = g_.memset(kb[3 * HD:3 * HD + 3, :, :], 1.0)
            last.then_inc(W["ones_ok"], 1)
            pool.wait_ge(W["ones_ok"], 1)
            g_.memset(cum[:, :], 0.0).then_inc(W["cum_ok"], 1)
            pool.sem_inc(W["addr_free"], 1)

            def f_rsqrt(k):
                def stage(i, c, streams):
                    after(pool, W["f_var"], i, c, k, 3)
                    g_.tensor_tensor(rstdF[:, :], vepsF[:, :], mhalf[:, :], ALU.pow).then_inc(W["f_rstd_ok"], 1)
                return stage

            def r_rsqrt(i, c, streams):
                after(pool, W["r_var"], i, c, 1)
                g_.tensor_tensor(rstdR[:, :], vepsR[:, :], mhalf[:, :], ALU.pow).then_inc(W["r_rstd_ok"], 1)

            def add(g):
                def stage(i, c, streams):
                    after(pool, W["att_ok"], i, c, g + 1, NG)
                    after(pool, W["accst"], i, c, 0, 1, 16)
                    g_.tensor_tensor(acc[:, g, :], xs[c % 2][:, g, :], att[:, :], ALU.add).then_inc(W["x3_ok"], 1)
                return stage

            def send(n):
                def stage(i, c, streams):
                    if n == 0:
                        after(pool, W["route_ok"], i, c, 1)
                        pool.sem_inc(W["pool_passed"], 1)
                    per = T * TOPK // 4
                    for j in range(n * per, (n + 1) * per):
                        t, k = j // TOPK, j % TOPK
                        g_.indirect_dma_start(out=ids_d, out_offset=bass.IndirectOffsetOnAxis(ap=addr[:, t, k:k + 1], axis=0),
                                              in_=tok[:, t:t + 1], in_offset=None, bounds_check=P * P - 1,
                                              oob_is_err=False).then_inc(W["scat"], 16)
                    if n == 3:
                        after(pool, W["scat"], i, c, T * TOPK, T * TOPK, 16)
                        pool.sem_inc(W["addr_free"], 1)
                return stage

            steps(pool, {"R.stats": r_rsqrt, "F.stats": f_rsqrt(1), "F.res1": f_rsqrt(2), "F.res2": f_rsqrt(3), 
                         "T.add0": add(0), "T.add1": add(1),
                         "R.send0": send(0), "R.send1": send(1), "R.send2": send(2), "R.send3": send(3)})

        @block.scalar
        def _(act):
            A = nc.scalar.activation
            act.preload_act_table(ACT.Exp)

            def affine(i, c, streams):
                after(act, W["nT_mm"], i, c, 1)
                for k in range(KC):
                    last = A(hT[:, k, :], a3(pB)[:, k, :], ACT.Identity, bias=beta[:, k:k + 1], scale=gamma[:, k:k + 1])
                last.then_inc(W["yT_ok"], 1)

            def turn2(i, c, streams):
                after(act, W["x2T_mm"], i, c, 1)
                A(normT[:, :, :], a3(pB), ACT.Copy).then_inc(W["x2T_ok"], 1)

            def weight(i, c, streams):
                after(act, W["gap_ok"], i, c, 1)
                A(egap[:, :, :], gap[:, :, :], ACT.Exp).then_inc(W["egap_ok"], 1)
                after(act, W["up_mm"], i, c, 1)
                A(hT[:, :, :], a3(pA), ACT.Relu).then_inc(W["uT_ok"], 1)

            def rows_of(g):
                def stage(i, c, streams):
                    slot = first_slot(f"T.M{g}", streams) % 2
                    after(act, W["mT_mm"], i, c, g + 1, NG)
                    after(act, W["mld"], i, c, g, NG, 16)
                    A(mrow[:, :], ring[slot][:, :].bitcast(BF16)[0:3 * G, 0:D], ACT.Copy).then_inc(W["mrow_ok"], 1)
                    after(act, W["mrow_ok"], i, c, g + 1, NG)
                    act.dma_start(qb[3 * HD:3 * HD + 3, G * g:G * (g + 1), :], mrow[:, :]).then_inc(W["mld"], 16)
                return stage

            def exps(s, half):
                def stage(i, c, streams):
                    if half == "a":
                        after(act, W["pv_step"], i, c, s - 1, NG * KC)
                    for j, q in enumerate(HALF[half]):
                        after(act, W["st_mm"], i, c, G * s + q + 1, KC * HS)
                        A(probs[s % 2][:, q, :], ring[(first_slot(f"T.Q{s}{half}", streams) + j) % 2][:, :], ACT.Exp, scale=SCALE1).then_inc(W["exp_ok"], 1)
                return stage

            def keep(g):
                def stage(i, c, streams):
                    after(act, W["pv_step"], i, c, KC * (g + 1), NG * KC)
                    after(act, W["x3_ok"], i, c, g, NG)
                    A(att[:, :], pV[:, :], ACT.Copy).then_inc(W["kept_ok"], 1)
                return stage

            def turn4(i, c, streams):
                after(act, W["x4T_mm"], i, c, 1)
                A(normRT[:, 0:2, :], pV[:, :].rearrange("p (k s) -> p k s", k=2), ACT.Copy)
                A(normRT[:, 2:4, :], pZ[:, :].rearrange("p (k s) -> p k s", k=2), ACT.Copy).then_inc(W["x4T_ok"], 1)

            def gates(i, c, streams):
                after(act, W["gt_mm"], i, c, 1)
                A(eg[:, :, :], ring[first_slot("R.gates", streams) % 2][:, 0:T * E1].rearrange("p (t e) -> p t e", t=T), ACT.Exp, scale=-1.0).then_inc(W["eg_ok"], 1)

            def shared(i, c, streams):
                after(act, W["su_mm"], i, c, 1)
                A(es[:, :], pZ[:, S:2 * S], ACT.Exp, scale=-1.0).then_inc(W["es_ok"], 1)

            stages = {"F.affine": affine, "F.turn2": turn2, "F.weight": weight, 
                      "T.M0": rows_of(0), "T.M1": rows_of(1), "R.turn": turn4, "R.gates": gates,
                      "R.up1": shared, "T.A0": keep(0), "T.A1": keep(1)}
            for s in range(NG * KC):
                for half in "ab":
                    stages[f"T.Q{s}{half}"] = exps(s, half)
            steps(act, stages)

        @block.vector
        def _(dve):
            V = nc.vector
            done = {"F": 0, "T": 0, "R": 0}
            PER = {"F": 24, "T": 12, "R": 28}

            def link(stream, ins, i, c, alone=False):
                s = W[stream.lower() + "_chain"]
                done[stream] += 1
                ins.then_inc(s, 1)
                after(dve, s, i, c, done[stream], PER[stream])
                if alone:
                    dve.sem_inc(W["passed"], 1)

            def opens(stream):
                assert done[stream] in (0, PER[stream]), (stream, done[stream])
                done[stream] = 0

            def stats(stream, i, c, src, eps, st, mv, veps, ok):
                for t in range(T):
                    last = V.bn_stats(st[:, t, :], src(t))
                link(stream, last, i, c, alone=True)
                for t in range(T):
                    last = V.bn_aggr(mv[:, t, :], st[:, t, :])
                link(stream, last, i, c)
                V.tensor_scalar(veps[:, :], mv[:, :, 1], eps, None, ALU.add).then_inc(W[ok], 1)

            def f_stats(i, c, streams):
                opens("F")
                after(dve, W["o_mm"], i, c, 1)
                stats("F", i, c, lambda t: pB[:, t * D:(t + 1) * D], GN_EPS, stF, mvF, vepsF, "f_var")

            def f_norm(k, src, ok):
                def stage(i, c, streams):
                    after(dve, W["f_rstd_ok"], i, c, k, 3)
                    for t in range(T):
                        last = V.tensor_scalar(norm[:, t, :], src(c, t), mvF[:, t, 0:1], rstdF[:, t:t + 1], ALU.subtract, ALU.mult)
                    last.then_inc(W[ok], 1)
                return stage

            def split(src, i, c):
                link("F", V.tensor_copy(qp[:, 0, :, :], src[:, :, :]), i, c)
                link("F", V.tensor_tensor(tmp, src[:, :, :], qp[:, 0, :, :], ALU.subtract), i, c)
                link("F", V.tensor_copy(qp[:, 1, :, :], tmp), i, c)
                link("F", V.tensor_tensor(qp[:, 2, :, :], tmp, qp[:, 1, :, :], ALU.subtract), i, c)

            def f_norm3(i, c, streams):
                after(dve, W["f_rstd_ok"], i, c, 3, 3)
                for t in range(T):
                    last = V.tensor_scalar(norm[:, t, :], xs[c % 2][:, t, :], mvF[:, t, 0:1], rstdF[:, t:t + 1], ALU.subtract, ALU.mult)
                link("F", last, i, c)
                after(dve, W["kst"], i, c, 3, 3, 16)
                split(norm, i, c)
                dve.sem_inc(W["q_ok"], 1)

            def f_keys(i, c, streams):
                after(dve, W["kin_in"], i, c, 1, 1, 16)
                after(dve, W["qst"], i, c, 0, 3, 16)
                split(kin, i, c)
                dve.sem_inc(W["k_ok"], 1)

            def f_affine(i, c, streams):
                after(dve, W["yT_ok"], i, c, 1)
                after(dve, W["gate_mm"], i, c, 1)
                V.scalar_tensor_tensor(out=zT[:, :, :], in0=a3(pA), scalar=0.0, in1=hT[:, :, :],
                                       op0=ALU.max, op1=ALU.mult).then_inc(W["zT_ok"], 1)

            def f_res1(i, c, streams):
                after(dve, W["x1_mm"], i, c, 1)
                after(dve, W["x_in"], i, c, 1, 1, 16)
                x = xs[c % 2]
                link("F", V.scalar_tensor_tensor(out=x[:, :, :], in0=t3(pA), scalar=tg_x[:, 0:1], in1=xin[:, :, :],
                                                 op0=ALU.mult, op1=ALU.add), i, c)
                dve.sem_inc(W["x1_ok"], 1)
                stats("F", i, c, lambda t: x[:, t, :], LN_EPS, stF, mvF, vepsF, "f_var")

            def f_best(i, c, streams):
                after(dve, W["lg_mm"], i, c, 1)
                dve.sem_inc(W["passed"], 1)
                for t in range(T):
                    last = V.max(m8[:, t, :], pB[:, t * E0:(t + 1) * E0])
                link("F", last, i, c)
                V.tensor_tensor(gap[:, :, :], m8[:, :, 1:2], m8[:, :, 0:1], ALU.subtract).then_inc(W["gap_ok"], 1)

            def f_weight(i, c, streams):
                after(dve, W["egap_ok"], i, c, 1)
                e_ = egap[:, :, 0]
                link("F", V.tensor_scalar(rw[:, 0, :], e_, 1.0, None, ALU.add), i, c)
                link("F", V.reciprocal(rw[:, 1, :], rw[:, 0, :]), i, c)
                link("F", V.tensor_tensor(rw[:, 2, :], rw[:, 1, :], e_, ALU.mult), i, c)
                link("F", V.tensor_tensor(rw[:, 0, :], rw[:, 1, :], rw[:, 2, :], ALU.add), i, c)
                link("F", V.tensor_scalar(rw[:, 2, :], rw[:, 0, :], tg_f[:, 0:1], None, ALU.mult), i, c)

            def f_res2(i, c, streams):
                x = xs[c % 2]
                after(dve, W["ex_mm"], i, c, 1)
                for t in range(T):
                    last = V.scalar_tensor_tensor(out=x[:, t, :], in0=pB[:, t * D:(t + 1) * D], scalar=rw[:, 2, t:t + 1],
                                                  in1=x[:, t, :], op0=ALU.mult, op1=ALU.add)
                link("F", last, i, c)
                after(dve, W["dn_mm"], i, c, 1)
                link("F", V.scalar_tensor_tensor(out=x[:, :, :], in0=t3(pA), scalar=tg_f[:, 0:1], in1=x[:, :, :],
                                                 op0=ALU.mult, op1=ALU.add), i, c)
                dve.sem_inc(W["x2_ok"], 1)
                stats("F", i, c, lambda t: x[:, t, :], LN_EPS, stF, mvF, vepsF, "f_var")

            def maxima(n):
                def stage(i, c, streams):
                    for r in range(2):
                        h, m = (2 * n + r) // KC, (2 * n + r) % KC
                        after(dve, W["s_mm"], i, c, 2 * n + r + 1, KC * HS)
                        if h == G and m == 0:
                            after(dve, W["t_chain"], i, c, 4, PER["T"])
                            after(dve, W["nmp_ok"], i, c, 1, NG)
                        V.tensor_reduce(nmx[:, m, h % G:h % G + 1], ring[(first_slot(f"T.S{n}", streams) + r) % 2][:, :],
                                        axis=AX.X, op=ALU.max, negate=True).then_inc(W["mx_ok"], 1)
                return stage

            def parts(g):
                def stage(i, c, streams):
                    if g == 0:
                        opens("T")
                    after(dve, W["mx_ok"], i, c, KC * G * (g + 1), KC * HS)
                    after(dve, W["mT_mm"], i, c, g, NG)
                    link("T", V.tensor_copy(nmp[:, :, 0, :], nmx[:, :, :]), i, c)
                    link("T", V.tensor_tensor(nmr[:, 0, :, :], nmx[:, :, :], nmp[:, :, 0, :], ALU.subtract), i, c)
                    link("T", V.tensor_copy(nmp[:, :, 1, :], nmr[:, 0, :, :]), i, c)
                    link("T", V.tensor_tensor(nmr[:, 1, :, :], nmr[:, 0, :, :], nmp[:, :, 1, :], ALU.subtract), i, c)
                    V.tensor_copy(nmp[:, :, 2, :], nmr[:, 1, :, :]).then_inc(W["nmp_ok"], 1)
                return stage

            def attended(g):
                def stage(i, c, streams):
                    after(dve, W["pv_step"], i, c, KC * (g + 1), NG * KC)
                    blocks = rsum[:, :].rearrange("p (b r) -> p b r", r=HD)
                    after(dve, W["att_ok"], i, c, g, NG)
                    V.transpose(rsum[:, :], pZ[:, :]).then_inc(W["sums_ok"], 1)
                    after(dve, W["sums_ok"], i, c, g + 1, NG)
                    link("T", V.reciprocal(rcol[:, :], blocks[:, :, 0]), i, c)
                    link("T", V.transpose(rsum[:, :], rcol[:, :].unsqueeze(2).broadcast_to([P, D // HD, HD])), i, c)
                    after(dve, W["kept_ok"], i, c, g + 1, NG)
                    V.scalar_tensor_tensor(out=att[:, :], in0=att[:, :], scalar=tg_x[:, 1:2], in1=rsum[:, :],
                                           op0=ALU.mult, op1=ALU.mult).then_inc(W["att_ok"], 1)
                return stage

            def r_stats(i, c, streams):
                opens("R")
                after(dve, W["x3_ok"], i, c, NG, NG)
                stats("R", i, c, lambda t: acc[:, t, :], LN_EPS, stR, mvR, vepsR, "r_var")

            def r_norm(i, c, streams):
                after(dve, W["r_rstd_ok"], i, c, 1)
                after(dve, W["x4st"], i, c, 1, 1, 16)
                for t in range(T):
                    last = V.tensor_scalar(normR[:, t, :], acc[:, t, :], mvR[:, t, 0:1], rstdR[:, t:t + 1], ALU.subtract, ALU.mult)
                last.then_inc(W["x4n_ok"], 1)

            def r_shared(i, c, streams):
                after(dve, W["es_ok"], i, c, 1)
                link("R", V.tensor_scalar(es[:, :], es[:, :], 1.0, None, ALU.add), i, c)
                link("R", V.reciprocal(es2[:, :], es[:, :]), i, c)
                link("R", V.tensor_tensor(es[:, :], pZ[:, S:2 * S], es2[:, :], ALU.mult), i, c)
                V.tensor_tensor(shT[:, :], pZ[:, 0:S], es[:, :], ALU.mult).then_inc(W["shT_ok"], 1)

            def r_acc(i, c, streams):
                after(dve, W["sd_mm"], i, c, 1)
                for t, p in enumerate((pV, pZ)):
                    last = V.scalar_tensor_tensor(out=acc[:, t, :], in0=p[:, :], scalar=tg_f[:, 1:2], in1=acc[:, t, :],
                                                  op0=ALU.mult, op1=ALU.add)
                last.then_inc(W["acc_ok"], 1)

            def r_sigmoid(i, c, streams):
                after(dve, W["eg_ok"], i, c, 1)
                link("R", V.tensor_scalar(eg[:, :, :], eg[:, :, :], 1.0, None, ALU.add), i, c)
                link("R", V.reciprocal(score[:, :, :], eg[:, :, :]), i, c, alone=True)
                for t in range(T):
                    last = V.max(top[:, t, :], score[:, t, :])
                link("R", last, i, c, alone=True)
                for t in range(T):
                    last = V.max_index(topi[:, t, :], top[:, t, :], score[:, t, :])
                link("R", last, i, c)
                link("R", V.tensor_copy(topf[:, :, :], topi[:, :, 0:TOPK]), i, c)

            def r_chosen(i, c, streams):
                for t in range(T):
                    last = V.tensor_tensor(onehot[:, t, :, :], iota_e[:, :].unsqueeze(1).broadcast_to([P, TOPK, E1]),
                                           topf[:, t, :].unsqueeze(2).broadcast_to([P, TOPK, E1]), ALU.is_equal)
                link("R", last, i, c)
                link("R", V.tensor_reduce(chosen[:, :, :], onehot[:, :, :, :].rearrange("p t k e -> p t e k"), axis=AX.X, op=ALU.add), i, c)
                V.tensor_copy(chosen16[:, :, :], chosen[:, :, :])
                if isinstance(i, int) or c == 0:
                    dve.wait_ge(W["cum_ok"], 1)
                for t in range(T):
                    V.tensor_copy(cum16[:, t, :], cum[:, :])
                    link("R", V.tensor_tensor(cum[:, :], cum[:, :], chosen[:, t, :], ALU.add), i, c)
                dve.sem_inc(W["m_ok"], 1)
                link("R", V.tensor_reduce(wsum[:, 0, :], top[:, :, 0:TOPK], axis=AX.X, op=ALU.add), i, c)
                link("R", V.reciprocal(wsum[:, 1, :], wsum[:, 0, :]), i, c)

            def r_pos(i, c, streams):
                after(dve, W["pos_mm"], i, c, 1)
                link("R", V.tensor_copy(post[:, :, :], ring[first_slot("R.pos", streams) % 2][:, 0:T * E1].rearrange("p (t e) -> p t e", t=T)), i, c)
                dve.sem_inc(W["pos_ok"], 1)

            def r_places(i, c, streams):
                for t in range(T):
                    last = V.tensor_tensor(ohp[:, t, :, :], onehot[:, t, :, :],
                                           post[:, t, :].unsqueeze(1).broadcast_to([P, TOPK, E1]), ALU.mult)
                link("R", last, i, c)
                link("R", V.tensor_reduce(pos[:, :, :], ohp[:, :, :, :], axis=AX.X, op=ALU.add), i, c)
                fits, high, a_, b_, c_, d_ = (small[:, k, :, :] for k in range(6))
                V.tensor_scalar(fits, pos[:, :, :], float(CAP), None, ALU.is_lt)
                V.tensor_scalar(high, pos[:, :, :], float(P), None, ALU.is_ge)
                V.tensor_scalar(a_, topf[:, :, :], 2.0, None, ALU.mult)
                link("R", V.tensor_scalar(b_, pos[:, :, :], float(CAP - 1), None, ALU.min), i, c)
                V.scalar_tensor_tensor(out=slots_all[:, bass.ds(i * (2 * T) + c * T, T), :], in0=topf[:, :, :], scalar=float(CAP),
                                       in1=b_, op0=ALU.mult, op1=ALU.add)
                link("R", V.scalar_tensor_tensor(out=c_, in0=pos[:, :, :], scalar=float(P), in1=a_, op0=ALU.mult, op1=ALU.add), i, c)
                link("R", V.scalar_tensor_tensor(out=d_, in0=high, scalar=-float(P * P - 1), in1=c_, op0=ALU.mult, op1=ALU.add), i, c)
                link("R", V.tensor_scalar(a_, fits, -SKIP, SKIP, ALU.mult, ALU.add), i, c)
                link("R", V.tensor_tensor(b_, fits, top[:, :, 0:TOPK], ALU.mult), i, c)
                for t in range(T):
                    V.tensor_scalar(comb_all[:, bass.ds(i * (2 * T) + (c * T + t), 1), :].rearrange("p o k -> p (o k)"),
                                    b_[:, t, :], wsum[:, 1, t:t + 1], tg_f[:, 1:2], ALU.mult, ALU.mult)
                after(dve, W["addr_free"], i, c, 1)
                V.tensor_tensor(addr[:, :, :], d_, a_, ALU.add)
                for t in range(T):
                    link("R", V.tensor_copy(tok[:, t:t + 1], tok_f[:, :]), i, c)
                    link("R", V.tensor_scalar(tok_f[:, :], tok_f[:, :], float(P), None, ALU.add), i, c)
                dve.sem_inc(W["route_ok"], 1)

            stages = {"F.stats": f_stats, "F.affine": f_affine, "F.res1": f_res1, "F.best": f_best, "F.weight": f_weight,
                      "F.res2": f_res2,
                      "F.norm": f_norm(1, lambda c, t: pB[:, t * D:(t + 1) * D], "n_ok"),
                      "F.norm2": f_norm(2, lambda c, t: xs[c % 2][:, t, :], "x2n_ok"),
                      "F.norm3": f_norm3, "F.keys": f_keys,
                      "T.P0": parts(0), "T.P1": parts(1), "T.A0": attended(0), "T.A1": attended(1),
                      "R.stats": r_stats, "R.norm": r_norm, "R.shared": r_shared, "R.acc": r_acc, "R.sigmoid": r_sigmoid,
                      "R.chosen": r_chosen, "R.pos": r_pos, "R.places": r_places}
            for n in range(KC * HS // 2):
                stages[f"T.S{n}"] = maxima(n)
            steps(dve, stages)

        @block.tensor
        def _(pe):
            mm, tr = nc.tensor.matmul, nc.tensor.transpose

            def transposes(dst, src):
                for k in range(KC):
                    for t in range(T):
                        last = tr(dst(k)[:, t * P:(t + 1) * P], src[:, t, k * P:(k + 1) * P], ident[:, :])
                return last

            def by_rows(dst, lhs, w, tiles=range(T), ks=range(KC), k_all=KC):
                for t in tiles:
                    for k in ks:
                        last = mm(dst(t), lhs(k)[:, t * P:(t + 1) * P], w(k), start=(k == 0), stop=(k == k_all - 1))
                return last

            def by_features(dst, w, rhs, o):
                for k in range(KC):
                    last = mm(dst[:, o * S:(o + 1) * S], w[:, k, o * P:(o + 1) * P], rhs[:, k, :], start=(k == 0), stop=(k == KC - 1))
                return last

            tiles = lambda p, n=D: (lambda t: p[:, t * n:(t + 1) * n])
            chunks = lambda p: (lambda k: p[:, k * S:(k + 1) * S])

            def slot(r, i, streams):
                q = r - 2
                slots = SLOTS[streams["order"]]
                while q >= 0 and slots[q][0][0] not in streams:
                    q -= 2
                if q >= 0:
                    name, (s, k, per) = slots[q]
                    after(pe, W[s], i, streams[name[0]], k, per)
                return ring[r % 2]

            def f_gate(o):
                def stage(i, c, streams):
                    if o == 0:
                        after(pe, W["x2_ok"], i, c, 0)
                        after(pe, W["xnT_in"], i, c, 1, 1, 16)
                    last = by_features(pA, wg, xnT, o)
                    if o == KC - 1:
                        last.then_inc(W["gate_mm"], 1)
                return stage

            def f_out(s):
                def stage(i, c, streams):
                    if s == 0:
                        after(pe, W["x2_ok"], i, c, 0)
                        after(pe, W["val_in"], i, c, 1, 1, 16)
                    for h in range(H0):
                        for t in range(T):
                            last = mm(pB[:, s * D + h * P:s * D + (h + 1) * P], AT[:, t, h, s * P:(s + 1) * P],
                                      val[:, t, h * P:(h + 1) * P], start=(t == 0), stop=(t == T - 1))
                    if s == T - 1:
                        last.then_inc(W["o_mm"], 1)
                return stage

            def f_turn(i, c, streams):
                after(pe, W["n_ok"], i, c, 1)
                transposes(chunks(pB), norm).then_inc(W["nT_mm"], 1)

            def f_x1(t, half):
                def stage(i, c, streams):
                    if t == 0 and half == 0:
                        after(pe, W["zT_ok"], i, c, 1)
                    last = by_rows(tiles(pA), lambda k: zT[:, k, :], lambda k: wo[:, k, :], [t], range(2 * half, 2 * half + 2))
                    if t == T - 1 and half == 1:
                        last.then_inc(W["x1_mm"], 1)
                return stage

            def f_turn2(i, c, streams):
                after(pe, W["x2n_ok"], i, c, 1)
                transposes(chunks(pB), norm).then_inc(W["x2T_mm"], 1)

            def f_gates(i, c, streams):
                after(pe, W["x2T_ok"], i, c, 1)
                by_rows(tiles(pB, E0), lambda k: normT[:, k, :], lambda k: wg0[:, k, :]).then_inc(W["lg_mm"], 1)

            def f_up(o):
                def stage(i, c, streams):
                    last = by_features(pA, wupT, normT, o)
                    if o == KC - 1:
                        last.then_inc(W["up_mm"], 1)
                return stage

            def f_expert(t):
                def stage(i, c, streams):
                    if t == 0:
                        after(pe, W["gap_ok"], i, c, 1)
                    last = by_rows(tiles(pB), lambda k: normT[:, k, :], lambda k: wexp[:, k, :], [t])
                    if t == T - 1:
                        last.then_inc(W["ex_mm"], 1)
                return stage

            def f_down(t, half):
                def stage(i, c, streams):
                    if t == 0 and half == 0:
                        after(pe, W["uT_ok"], i, c, 1)
                    last = by_rows(tiles(pA), lambda k: hT[:, k, :], lambda k: wdnT[:, k, :], [t], range(2 * half, 2 * half + 2))
                    if t == T - 1 and half == 1:
                        last.then_inc(W["dn_mm"], 1)
                return stage

            def scores(n):
                def stage(i, c, streams):
                    if n == 0:
                        pe.wait_ge(W[f"ka_in{c % 2}"], (i + c // 2) * 64 + 64)
                        after(pe, W["qa_in"], i, c, 4, 4, 16)
                    for r in range(2):
                        h, m = (2 * n + r) // KC, (2 * n + r) % KC
                        dst = slot(first_slot(f"T.S{n}", streams) + r, i, streams)
                        mm(dst[:, :], qa[c % 2][:, h, m * P:(m + 1) * P], ka[c % 2][:, h, :], start=True, stop=True).then_inc(W["s_mm"], 1)
                return stage

            def rows_of(g):
                def stage(i, c, streams):
                    after(pe, W["nmp_ok"], i, c, g + 1, NG)
                    dst = slot(first_slot(f"T.M{g}", streams), i, streams)[:, :].bitcast(BF16)
                    for m in range(KC):
                        last = tr(dst[0:3 * G, m * P:(m + 1) * P], nmp[:, m, :, :].rearrange("p k h -> p (k h)"), ident16[:, :])
                    last.then_inc(W["mT_mm"], 1)
                return stage

            def shifted(s, half):
                def stage(i, c, streams):
                    g, n = s // KC, s % KC
                    if s == 0 and half == "a":
                        after(pe, W["kb_in"], i, c, 3, 3, 16)
                        after(pe, W["qb_in"], i, c, 3, 3, 16)
                    if n == 0 and half == "a":
                        after(pe, W["mld"], i, c, g + 1, NG, 16)
                    for j, q in enumerate(HALF[half]):
                        h = g * G + q
                        dst = slot(first_slot(f"T.Q{s}{half}", streams) + j, i, streams)
                        mm(dst[:, :], ka[c % 2][:, h, n * P:(n + 1) * P], qa[c % 2][:, h, :], start=True, stop=False)
                        mm(dst[:, :], kb[0:KB, h, n * P:(n + 1) * P], qb[0:KB, h, :], start=False, stop=True).then_inc(W["st_mm"], 1)
                return stage

            def weighted(s, half):
                def stage(i, c, streams):
                    g, n = s // KC, s % KC
                    if half == "a":
                        after(pe, W["exp_ok"], i, c, G * (s + 1), KC * HS)
                        if s == 0:
                            after(pe, W["cT_in"], i, c, 1, 1, 16)
                            after(pe, W["acc_ok"], i, c, 0)
                        elif n == 0:
                            after(pe, W["kept_ok"], i, c, 1, NG)
                    elif n == 0 and s:
                        after(pe, W["sums_ok"], i, c, 1, NG)
                    for q in range(G):
                        if half == "a":
                            r = (g * G + q) * HD
                            last = mm(pV[q * HD:(q + 1) * HD, :], cT[:, n, r:r + HD], probs[s % 2][:, q, :], start=(n == 0), stop=(n == KC - 1))
                        else:
                            last = mm(pZ[q * HD:(q + 1) * HD, :], ones32[:, :], probs[s % 2][:, q, :], start=(n == 0), stop=(n == KC - 1))
                    if half == "b":
                        last.then_inc(W["pv_step"], 1)
                return stage

            def r_turn(i, c, streams):
                after(pe, W["x4n_ok"], i, c, 1)
                transposes(lambda k: (pV, pZ)[k // 2][:, (k % 2) * S:(k % 2 + 1) * S], normR).then_inc(W["x4T_mm"], 1)

            def r_gates(i, c, streams):
                after(pe, W["x4T_ok"], i, c, 1)
                dst = slot(first_slot("R.gates", streams), i, streams)
                by_rows(tiles(dst, E1), lambda k: normRT[:, k, :], lambda k: wg1[:, k, :]).then_inc(W["gt_mm"], 1)

            def r_up(o):
                def stage(i, c, streams):
                    last = by_features(pZ, wsu, normRT, o)
                    if o == 1:
                        last.then_inc(W["su_mm"], 1)
                return stage

            def r_pos(i, c, streams):
                after(pe, W["m_ok"], i, c, 1)
                dst = slot(first_slot("R.pos", streams), i, streams)
                for t in range(T):
                    mm(dst[:, t * E1:(t + 1) * E1], before16[:, :], chosen16[:, t, :], start=True, stop=False)
                    last = mm(dst[:, t * E1:(t + 1) * E1], ones16[:, :], cum16[:, t, :], start=False, stop=True)
                last.then_inc(W["pos_mm"], 1)

            def r_down(t):
                def stage(i, c, streams):
                    if t == 0:
                        after(pe, W["shT_ok"], i, c, 1)
                    last = by_rows(lambda t: (pV, pZ)[t][:, :], lambda k: shT[:, :], lambda k: wsd[:, :], [t], [0], 1)
                    if t == T - 1:
                        last.then_inc(W["sd_mm"], 1)
                return stage

            stages = {"F.turn": f_turn, "F.turn2": f_turn2, "F.gates": f_gates, "T.M0": rows_of(0), "T.M1": rows_of(1),
                      "R.turn": r_turn, "R.gates": r_gates, "R.pos": r_pos}
            for t in range(T):
                stages[f"F.out{t}"] = f_out(t)
                stages[f"F.expert{t}"] = f_expert(t)
                stages[f"R.down{t}"] = r_down(t)
                stages[f"R.up{t}"] = r_up(t)
                for half in range(2):
                    stages[f"F.x1{'ab'[t]}{half}"] = f_x1(t, half)
                    stages[f"F.down{'ab'[t]}{half}"] = f_down(t, half)
            for o in range(KC):
                stages[f"F.gate{o}"] = f_gate(o)
                stages[f"F.up{o}"] = f_up(o)
            for n in range(KC * HS // 2):
                stages[f"T.S{n}"] = scores(n)
            for s in range(NG * KC):
                for half in "ab":
                    stages[f"T.Q{s}{half}"] = shifted(s, half)
                    stages[f"T.V{s}{half}"] = weighted(s, half)
            steps(pe, stages)




def experts(nc, io, out, v):
    outer = v["outer"]
    with ExitStack() as ctx:
        sem = lambda n: outer.enter_context(nc.semaphore(n))
        sb = lambda n, s, d=F32: ctx.enter_context(nc.sbuf_tensor(n, s, d))
        ps = lambda n, s, d=F32: ctx.enter_context(nc.psum_tensor(n, s, d))
        ident, slots_all, comb_all = v["ident"], v["slots_all"], v["comb_all"]
        ids_d, xn4_d, eout_d, acc_d = v["ids_d"], v["xn4_d"], v["eout_d"], v["acc_d"]
        TP = 2 * HT
        ids = sb("e_ids", [P, P], U32)
        two = lambda name, shape, dt=F32: [sb(f"e_{name}{u}", shape, dt) for u in range(2)]
        idx = two("idx", [P, TP], U32)
        xg = two("xg", [P, TP, D])
        xT = two("xT", [P, 2, KC, CAP])
        wu = two("wu", [P, 2, KC, 2 * HE])
        wd = two("wd", [2 * HE, D])
        gate = two("gate", [2 * HE, CAP])
        hT = two("hT", [2 * HE, CAP])
        eo = two("eo", [P, TP, D])
        cidx = two("cidx", [P, TOPK], U32)
        rows_ = two("rows", [P, TOPK, D])
        tot = two("tot", [P, D])
        pT = [ps(f"e_pT{e}", [P, KC * CAP]) for e in range(2)]
        pU = ps("e_pU", [P, 2 * CAP])
        pD = [ps(f"e_pD{k}", [P, D]) for k in range(2)]

        ids_in = sem("e_ids_in")
        gath, wu_in, wd_in, est, cg, acc_in, ost = ([sem(f"e_{n}{u}") for u in range(2)] for n in "gath wu_in wd_in est cg acc_in ost".split())
        pool_passed = sem("e_pool_passed")
        idx_ok, cidx_ok, T_mm, up_mm, dn_mm = (sem("e_" + n) for n in "idx_ok cidx_ok T_mm up_mm dn_mm".split())
        xA_ok, xB_ok, gate_ok, h_ok, oe_ok, oo_ok, tchain, tot_ok = (sem("e_" + n) for n in "xA_ok xB_ok gate_ok h_ok oe_ok oo_ok tchain tot_ok".split())
        block = ctx.enter_context(nc.Block())

        def pipelined(eng, transpose, up, down):
            transpose(0, 0)
            transpose(0, 1)
            up(0, 0)
            with eng.Fori(0, PAIRS // 2 - 1) as i:
                for c in range(2):
                    transpose(i, c + 2)
                    down(i, c)
                    up(i, c + 1)
            last = PAIRS // 2 - 1
            down(last, 0)
            up(last, 1)
            down(last, 1)

        def pair_of(i, c):
            return i * 2 + c

        def wait_count(eng, s, i, c, per=1, less=0):
            if isinstance(i, int) and (2 * i + c + 1) * per - less <= 0:
                return
            eng.wait_ge(s, i * (2 * per) + ((c + 1) * per - less))

        @block.sync
        def _(sp):
            def load(i, c):
                u = c % 2
                sp.dma_start(wu[u][:, :, :, :], io["wu"][bass.ds(pair_of(i, c), 1), :, :].rearrange("o p (e k n) -> (o p) e k n", e=2, k=KC)).then_inc(wu_in[u], 16)
                sp.dma_start(wd[u][:, :], io["wd"][bass.ds(pair_of(i, c), 1), :, :].rearrange("o p n -> (o p) n")).then_inc(wd_in[u], 16)

            def store(i, c):
                u = c % 2
                wait_count(sp, oe_ok, i, c, 2)
                wait_count(sp, oo_ok, i, c, 2)
                sp.dma_start(eout_d[bass.ds(pair_of(i, c) * (2 * CAP), 2 * CAP), :].rearrange("(t p) d -> p t d", p=P), eo[u][:, :, :]).then_inc(est[u], 16)

            sp.dma_start(ids[:, :], v["ids_d"].rearrange("(p n) o -> p (n o)", p=P)).then_inc(ids_in, 16)
            for c in range(2):
                load(0, c)
            with sp.Fori(0, PAIRS // 2 - 1) as i:
                for c in range(2):
                    store(i, c)
                    load(i, c + 2)
            for c in range(2):
                store(PAIRS // 2 - 1, c)
            def load_acc(i, u):
                sp.dma_start(tot[u][:, :], acc_d[bass.ds(i * 2 + u, 1), :, :].rearrange("o p d -> (o p) d")).then_inc(acc_in[u], 16)

            def store_out(i, u):
                sp.wait_ge(tot_ok, i * 2 + (u + 1))
                sp.dma_start(out.rearrange("b (t p) d -> (b t) p d", p=P)[bass.ds(i * 2 + u, 1), :, :].rearrange("o p d -> (o p) d"),
                             tot[u][:, :]).then_inc(ost[u], 16)

            for u in range(2):
                load_acc(0, u)
            with sp.Fori(0, NT // 2 - 1) as i:
                for u in range(2):
                    store_out(i, u)
                    sp.wait_ge(ost[u], i * 16 + 16)
                    load_acc(i + 1, u)
            for u in range(2):
                store_out(NT // 2 - 1, u)
            for u in range(2):
                sp.wait_ge(ost[u], 16 * (NT // 2))
                sp.wait_ge(est[u], 16 * (PAIRS // 2))

        @block.gpsimd
        def _(pool):
            g_ = nc.gpsimd

            def gather(i, c):
                u = c % 2
                wait_count(pool, T_mm, i, c - 2)
                g_.tensor_copy(idx[u][:, :], ids[:, bass.ds(pair_of(i, c) * TP, TP)]).then_inc(idx_ok, 1)
                wait_count(pool, idx_ok, i, c)
                pool.sem_inc(pool_passed, 1)
                for t in range(TP):
                    g_.indirect_dma_start(out=xg[u][:, t, :], out_offset=None, in_=xn4_d,
                                          in_offset=bass.IndirectOffsetOnAxis(ap=idx[u][:, t:t + 1], axis=0)).then_inc(gath[u], 16)

            pool.wait_ge(ids_in, 16)
            gather(0, 0)
            gather(0, 1)
            with pool.Fori(0, PAIRS // 2 - 1) as i:
                for c in range(2):
                    gather(i, c + 2)
            for u in range(2):
                pool.wait_ge(est[u], 16 * (PAIRS // 2))

            def collect(i, u):
                wait_tile = i * 2 + u
                g_.tensor_copy(cidx[u][:, :], slots_all[:, bass.ds(wait_tile, 1), :].rearrange("p o k -> p (o k)")).then_inc(cidx_ok, 1)
                hold(pool, cidx_ok, i * 2 + (u + 1), pool_passed)
                for k in range(TOPK):
                    g_.indirect_dma_start(out=rows_[u][:, k, :], out_offset=None, in_=eout_d,
                                          in_offset=bass.IndirectOffsetOnAxis(ap=cidx[u][:, k:k + 1], axis=0)).then_inc(cg[u], 16)

            for u in range(2):
                collect(0, u)
            with pool.Fori(0, NT // 2 - 1) as i:
                for u in range(2):
                    pool.wait_ge(tot_ok, i * 2 + (u + 1))
                    collect(i + 1, u)

        @block.scalar
        def _(act):
            A = nc.scalar.activation
            act.preload_act_table(ACT.Silu)

            def transpose(i, c):
                wait_count(act, T_mm, i, c)
                wait_count(act, up_mm, i, c - 2)
                A(xT[c % 2][:, 0, :, :], pT[0][:, :].rearrange("p (k s) -> p k s", k=KC), ACT.Copy).then_inc(xA_ok, 1)

            def up(i, c):
                wait_count(act, up_mm, i, c)
                A(gate[c % 2][:, :], pU[:, 0:CAP], ACT.Silu).then_inc(gate_ok, 1)

            def down(i, c):
                if not (isinstance(i, int) and i == 0 and c < 2):
                    act.wait_ge(est[c % 2], store_count(i, c))
                for k in (0, 2):
                    wait_count(act, dn_mm, i, c, TP, TP - k - 1)
                    A(eo[c % 2][:, k, :], pD[0][:, :], ACT.Copy).then_inc(oe_ok, 1)

            pipelined(act, transpose, up, down)

        @block.vector
        def _(dve):
            V = nc.vector

            def transpose(i, c):
                wait_count(dve, T_mm, i, c)
                wait_count(dve, up_mm, i, c - 2)
                V.tensor_copy(xT[c % 2][:, 1, :, :], pT[1][:, :].rearrange("p (k s) -> p k s", k=KC)).then_inc(xB_ok, 1)

            def up(i, c):
                wait_count(dve, gate_ok, i, c)
                wait_count(dve, dn_mm, i, c - 2, TP)
                V.tensor_tensor(hT[c % 2][:, :], pU[:, CAP:2 * CAP], gate[c % 2][:, :], ALU.mult).then_inc(h_ok, 1)

            def down(i, c):
                if not (isinstance(i, int) and i == 0 and c < 2):
                    dve.wait_ge(est[c % 2], store_count(i, c))
                for k in (1, 3):
                    wait_count(dve, dn_mm, i, c, TP, TP - k - 1)
                    V.tensor_copy(eo[c % 2][:, k, :], pD[1][:, :]).then_inc(oo_ok, 1)

            pipelined(dve, transpose, up, down)
            with dve.Fori(0, NT // 2) as i:
                for u in range(2):
                    dve.wait_ge(acc_in[u], i * 16 + 16)
                    dve.wait_ge(cg[u], i * (16 * TOPK) + 16 * TOPK)
                    for k in range(TOPK):
                        w = comb_all[:, bass.ds(i * 2 + u, 1), k]
                        ins = V.scalar_tensor_tensor(out=tot[u][:, :], in0=rows_[u][:, k, :], scalar=w, in1=tot[u][:, :],
                                                     op0=ALU.mult, op1=ALU.add)
                        if k < TOPK - 1:
                            ins.then_inc(tchain, 1)
                            dve.wait_ge(tchain, i * (2 * (TOPK - 1)) + (u * (TOPK - 1) + k + 1))
                        else:
                            ins.then_inc(tot_ok, 1)

        @block.tensor
        def _(pe):
            mm, tr = nc.tensor.matmul, nc.tensor.transpose

            def transpose(i, c):
                u = c % 2
                pe.wait_ge(gath[u], (i + c // 2) * (16 * TP) + 16 * TP)
                wait_count(pe, xA_ok, i, c - 1)
                wait_count(pe, xB_ok, i, c - 1)
                for e in range(2):
                    for t in range(HT):
                        for k in range(KC):
                            last = tr(pT[e][:, k * CAP + t * P:k * CAP + (t + 1) * P], xg[u][:, HT * e + t, k * P:(k + 1) * P], ident[:, :])
                last.then_inc(T_mm, 1)

            def up(i, c):
                u = c % 2
                pe.wait_ge(wu_in[u], (i + c // 2) * 16 + 16)
                wait_count(pe, xA_ok, i, c)
                wait_count(pe, xB_ok, i, c)
                wait_count(pe, h_ok, i, c - 1)
                for j in range(2):
                    for k in range(KC):
                        for e in range(2):
                            last = mm(pU[HE * e:HE * (e + 1), j * CAP:(j + 1) * CAP], wu[u][:, e, k, j * HE:(j + 1) * HE],
                                      xT[u][:, e, k, :], start=(k == 0), stop=(k == KC - 1))
                last.then_inc(up_mm, 1)

            def down(i, c):
                u = c % 2
                pe.wait_ge(wd_in[u], (i + c // 2) * 16 + 16)
                wait_count(pe, h_ok, i, c)
                for n in range(TP):
                    e, t = n // HT, n % HT
                    wait_count(pe, (oe_ok, oo_ok)[n % 2], i, c, 2, 2 - n // 2)
                    mm(pD[n % 2][:, :], hT[u][HE * e:HE * (e + 1), t * P:(t + 1) * P], wd[u][HE * e:HE * (e + 1), :],
                       start=True, stop=True).then_inc(dn_mm, 1)

            pipelined(pe, transpose, up, down)


def store_count(i, c):
    return i * 16 + (c // 2) * 16


_SHAPE = (NB, S, D)


def rows(w):
    k = w.shape[0] // P
    return np.ascontiguousarray(w.reshape(k, P, w.shape[1]).transpose(1, 0, 2))


def kernel(x, ctx_2048, g_xattn, g_ffn, L0_xattn_Wh, L0_xattn_wg_w, L0_xattn_wo_w, L0_xattn_gn_gamma,
           L0_xattn_gn_beta, L0_ffn_W_up, L0_ffn_W_down, L0_ffn_W_gate, L0_ffn_W_expert, L1_ffn_w_gate,
           L1_ffn_w_shared_up, L1_ffn_w_shared_down, L1_ffn_w_up, L1_ffn_w_down):
    import concourse.bacc as bacc
    from concourse.bass_utils import run_bass_kernel_spmd as run

    a = lambda t: np.asarray(t)
    c = np.ascontiguousarray
    wh = a(L0_xattn_Wh)
    arrays = {
        "x": c(a(x)),
        "ctx": c(a(ctx_2048)),
        "ctxT": c(a(ctx_2048).reshape(NB, S, KC, P).transpose(0, 3, 2, 1).reshape(NB, P, KC * S)),
        "gates": c(np.concatenate([np.tile(a(g_xattn)[None, :], (P, 1)), np.tile(a(g_ffn)[None, :], (P, 1))], axis=1)),
        "mask": decay_mask(),
        "wh": c(wh.transpose(1, 0, 2)),
        "whT": c(wh.transpose(2, 0, 1)),
        "wg": rows(a(L0_xattn_wg_w)),
        "wo": rows(a(L0_xattn_wo_w)),
        "wupT": rows(a(L0_ffn_W_up).T),
        "wdnT": rows(a(L0_ffn_W_down).T),
        "wexp": rows(a(L0_ffn_W_expert)),
        "wg0": rows(a(L0_ffn_W_gate).T),
        "wg1": rows(a(L1_ffn_w_gate)),
        "wsu": rows(a(L1_ffn_w_shared_up)),
        "wsd": c(a(L1_ffn_w_shared_down)),
        "gamma": c(a(L0_xattn_gn_gamma).reshape(KC, P).T),
        "beta": c(a(L0_xattn_gn_beta).reshape(KC, P).T),
        "wu": c(a(L1_ffn_w_up).reshape(PAIRS, 2, KC, P, 2 * HE).transpose(0, 3, 1, 2, 4).reshape(PAIRS, P, 2 * KC * 2 * HE)),
        "wd": c(a(L1_ffn_w_down).reshape(PAIRS, 2 * HE, D)),
    }
    nc = bacc.Bacc("TRN2", target_bir_lowering=False, num_devices=1)
    io = {n: nc.dram_tensor("in_" + n, t.shape, F32, kind="ExternalInput").ap() for n, t in arrays.items()}
    out = nc.dram_tensor("out", _SHAPE, F32, kind="ExternalOutput").ap()
    build(nc, io, out)
    r = run(nc, [{"in_" + n: t for n, t in arrays.items()}], core_ids=[0])
    return r.results[0]["out"]
```
